# Optimizing a Trainium2 kernel written in Bass

```python
import numpy as np
import jax
import jax.numpy as jnp

def _softmax(x, axis=-1):
    return jax.nn.softmax(x, axis=axis)

def _gelu(x):
    return jax.nn.gelu(x, approximate=True)

def _silu(x):
    return jax.nn.silu(x)

def _sigmoid(x):
    return jax.nn.sigmoid(x)

def _layernorm(x, axis=-1, eps=1e-05):
    m = jnp.mean(x, axis=axis, keepdims=True)
    v = jnp.var(x, axis=axis, keepdims=True)
    return (x - m) / jnp.sqrt(v + eps)

def _scatter_add(tgt, idx, src, axis=0):
    return tgt.at[idx].add(src)

def _segment_sum(src, seg, n):
    return jax.ops.segment_sum(src, seg, n)
kernel_name = 'mk_early_fusion_embed_d1_tok_img1024_r4_0df3c2'

def setup_inputs(seed: int=0):
    np.random.seed(seed)
    _w = jnp.asarray

    def _rec_inputs():
        import jax
        import jax.numpy as jnp
        _rk = jax.random.key(seed)
        x = -0.00016672 + 0.999947 * jax.random.normal(jax.random.fold_in(_rk, 1), (4, 3, 96, 96), jnp.float32)
        x_txt = jax.random.randint(jax.random.fold_in(_rk, 51), (4, 512), 0, 99987, jnp.int32)
        return (x, x_txt)
    x, x_txt = _rec_inputs()

    def _L0_tok_setup():
        import jax, jax.numpy as jnp
        import numpy as np
        DIM = 256
        IMG = 96
        P = 16
        C = 3
        TEMP = 10000.0
        EPS = 1e-05
        PATCH_DIM = C * P * P
        HP = IMG // P

        def layernorm(x, gamma, beta):
            mu = jnp.mean(x, axis=-1, keepdims=True)
            var = jnp.var(x, axis=-1, keepdims=True)
            return (x - mu) * jax.lax.rsqrt(var + EPS) * gamma + beta

        def posemb_sincos_2d(h, w, dim, dtype):
            y, x = jnp.meshgrid(jnp.arange(h), jnp.arange(w), indexing='ij')
            omega = jnp.arange(dim // 4, dtype=jnp.float32) / (dim // 4 - 1)
            omega = 1.0 / TEMP ** omega
            y = y.reshape(-1)[:, None] * omega[None, :]
            x = x.reshape(-1)[:, None] * omega[None, :]
            pe = jnp.concatenate((jnp.sin(x), jnp.cos(x), jnp.sin(y), jnp.cos(y)), axis=1)
            return pe.astype(dtype)
        key = jax.random.key(seed)
        ks = jax.random.split(key, 8)
        B = 64
        img = jax.random.normal(ks[0], (B, C, IMG, IMG), dtype=jnp.float32)
        cls_token = jax.random.normal(ks[1], (1, 1, DIM), dtype=jnp.float32)
        cls_pos_embedding = jax.random.normal(ks[2], (1, 1, DIM), dtype=jnp.float32)
        ln1_g = jnp.ones((PATCH_DIM,), jnp.float32)
        ln1_b = jnp.zeros((PATCH_DIM,), jnp.float32)
        W = jax.random.normal(ks[3], (PATCH_DIM, DIM), dtype=jnp.float32) / np.sqrt(PATCH_DIM)
        bias = jnp.zeros((DIM,), jnp.float32)
        ln2_g = jnp.ones((DIM,), jnp.float32)
        ln2_b = jnp.zeros((DIM,), jnp.float32)
        return {'img': img, 'cls_token': cls_token, 'cls_pos_embedding': cls_pos_embedding, 'ln1_g': ln1_g, 'ln1_b': ln1_b, 'W': W, 'bias': bias, 'ln2_g': ln2_g, 'ln2_b': ln2_b}
    _L0_tok_all = _L0_tok_setup()
    _L0_tok_in = {k: v for k, v in _L0_tok_all.items() if k in ('cls_token', 'cls_pos_embedding', 'ln1_g', 'ln1_b', 'W', 'bias', 'ln2_g', 'ln2_b')}
    del _L0_tok_all

    def _L0_txt_setup():
        import jax, jax.numpy as jnp
        import numpy as np
        CUTOFFS = (0, 5000, 15000, 25000)
        EMBED_DIM = 256
        EMBED_FACTOR = 4
        BATCH, SEQ = (8, 1024)

        def _bucket_dims():
            return [int(EMBED_DIM // EMBED_FACTOR ** i) for i in range(len(CUTOFFS) - 1)]
        key = jax.random.key(seed)
        ks = jax.random.split(key, 8)
        x = jax.random.randint(ks[0], (BATCH, SEQ), 0, CUTOFFS[-1], dtype=jnp.int64)
        dims = _bucket_dims()
        inp = {'x': x}
        for i, d in enumerate(dims):
            size = CUTOFFS[i + 1] - CUTOFFS[i]
            t = jax.random.normal(ks[1 + i], (size, d), dtype=jnp.float32) * 0.02
            t = t.at[0].set(0.0)
            inp[f't{i}'] = t
            inp[f'w{i}'] = jax.random.normal(ks[4 + i], (d, EMBED_DIM), dtype=jnp.float32) * 0.02
        return inp
    _L0_txt_all = _L0_txt_setup()
    _L0_txt_in = {k: v for k, v in _L0_txt_all.items() if k in ('t0', 't1', 't2', 'w0', 'w1', 'w2')}
    del _L0_txt_all

    def _L0_attn_setup():
        import jax, jax.numpy as jnp
        import numpy as np
        import math
        B, L, D, N = (8, 512, 256, 16)

        def _reference_tuple_inner(x, A_log, D_param, W_B, W_C, W_delta, b_delta):
            A = -jnp.exp(A_log)
            B_in = jnp.einsum('bld,nd->bln', x, W_B)
            C_in = jnp.einsum('bld,nd->bln', x, W_C)
            delta = jax.nn.softplus(jnp.einsum('bld,ed->ble', x, W_delta) + b_delta)
            h0 = jnp.zeros((x.shape[0], x.shape[2], A.shape[1]), dtype=x.dtype)

            def step(h, inp):
                x_t, B_t, C_t, d_t = inp
                A_bar = jnp.exp(d_t[:, :, None] * A[None])
                h = A_bar * h + (d_t * x_t)[:, :, None] * B_t[:, None, :]
                y_t = jnp.einsum('bdn,bn->bd', h, C_t) + D_param * x_t
                return (h, y_t)
            xs = (jnp.swapaxes(x, 0, 1), jnp.swapaxes(B_in, 0, 1), jnp.swapaxes(C_in, 0, 1), jnp.swapaxes(delta, 0, 1))
            h_final, ys = jax.lax.scan(step, h0, xs)
            y = jnp.swapaxes(ys, 0, 1)
            return (y, h_final)
        key = jax.random.key(seed)
        ks = jax.random.split(key, 6)
        x = jax.random.normal(ks[0], (B, L, D), dtype=jnp.float32)
        A_log = jnp.broadcast_to(jnp.log(jnp.arange(1, N + 1, dtype=jnp.float32))[None, :], (D, N))
        D_param = jnp.ones((D,), dtype=jnp.float32)
        s = 1.0 / math.sqrt(D)
        W_B = jax.random.uniform(ks[1], (N, D), minval=-s, maxval=s, dtype=jnp.float32)
        W_C = jax.random.uniform(ks[2], (N, D), minval=-s, maxval=s, dtype=jnp.float32)
        W_delta = jax.random.uniform(ks[3], (D, D), minval=-s, maxval=s, dtype=jnp.float32)
        b_delta = jax.random.uniform(ks[4], (D,), minval=math.log(0.001), maxval=math.log(0.1), dtype=jnp.float32)
        return {'x': x, 'A_log': A_log, 'D_param': D_param, 'W_B': W_B, 'W_C': W_C, 'W_delta': W_delta, 'b_delta': b_delta}
    _L0_attn_all = _L0_attn_setup()
    _L0_attn_in = {k: v for k, v in _L0_attn_all.items() if k in ('A_log', 'D_param', 'W_B', 'W_C', 'W_delta', 'b_delta')}
    del _L0_attn_all

    def _L0_ffn_setup():
        import jax, jax.numpy as jnp
        import numpy as np
        B, S, DIM = (2, 512, 256)
        HID = 512
        E, NSH, TOPK = (8, 2, 2)

        def _ffn(x, w1, w2, w3):
            return jax.nn.silu(x @ w1.T) * (x @ w3.T) @ w2.T
        key = jax.random.key(seed)
        ks = jax.random.split(key, 8)
        sc = 0.02
        return {'x': jax.random.normal(ks[0], (B, S, DIM), jnp.float32), 'router_w': jax.random.normal(ks[1], (E, DIM), jnp.float32) * sc, 'expert_bias': jnp.zeros((E,), jnp.float32), 'w1': jax.random.normal(ks[2], (E, HID, DIM), jnp.float32) * sc, 'w3': jax.random.normal(ks[3], (E, HID, DIM), jnp.float32) * sc, 'w2': jax.random.normal(ks[4], (E, DIM, HID), jnp.float32) * sc, 'sw1': jax.random.normal(ks[5], (NSH, HID, DIM), jnp.float32) * sc, 'sw3': jax.random.normal(ks[6], (NSH, HID, DIM), jnp.float32) * sc, 'sw2': jax.random.normal(ks[7], (NSH, DIM, HID), jnp.float32) * sc}
    _L0_ffn_all = _L0_ffn_setup()
    _L0_ffn_in = {k: v for k, v in _L0_ffn_all.items() if k in ('router_w', 'expert_bias', 'w1', 'w3', 'w2', 'sw1', 'sw3', 'sw2')}
    del _L0_ffn_all
    return {'x': x, 'x_txt': x_txt, 'L0_tok_cls_token': _L0_tok_in['cls_token'], 'L0_tok_cls_pos_embedding': _L0_tok_in['cls_pos_embedding'], 'L0_tok_ln1_g': _L0_tok_in['ln1_g'], 'L0_tok_ln1_b': _L0_tok_in['ln1_b'], 'L0_tok_W': _L0_tok_in['W'], 'L0_tok_bias': _L0_tok_in['bias'], 'L0_tok_ln2_g': _L0_tok_in['ln2_g'], 'L0_tok_ln2_b': _L0_tok_in['ln2_b'], 'L0_txt_t0': _L0_txt_in['t0'], 'L0_txt_t1': _L0_txt_in['t1'], 'L0_txt_t2': _L0_txt_in['t2'], 'L0_txt_w0': _L0_txt_in['w0'], 'L0_txt_w1': _L0_txt_in['w1'], 'L0_txt_w2': _L0_txt_in['w2'], 'L0_attn_A_log': _L0_attn_in['A_log'], 'L0_attn_D_param': _L0_attn_in['D_param'], 'L0_attn_W_B': _L0_attn_in['W_B'], 'L0_attn_W_C': _L0_attn_in['W_C'], 'L0_attn_W_delta': _L0_attn_in['W_delta'], 'L0_attn_b_delta': _L0_attn_in['b_delta'], 'L0_ffn_router_w': _L0_ffn_in['router_w'], 'L0_ffn_expert_bias': _L0_ffn_in['expert_bias'], 'L0_ffn_w1': _L0_ffn_in['w1'], 'L0_ffn_w3': _L0_ffn_in['w3'], 'L0_ffn_w2': _L0_ffn_in['w2'], 'L0_ffn_sw1': _L0_ffn_in['sw1'], 'L0_ffn_sw3': _L0_ffn_in['sw3'], 'L0_ffn_sw2': _L0_ffn_in['sw2']}

def reference(x, x_txt, L0_tok_cls_token, L0_tok_cls_pos_embedding, L0_tok_ln1_g, L0_tok_ln1_b, L0_tok_W, L0_tok_bias, L0_tok_ln2_g, L0_tok_ln2_b, L0_txt_t0, L0_txt_t1, L0_txt_t2, L0_txt_w0, L0_txt_w1, L0_txt_w2, L0_attn_A_log, L0_attn_D_param, L0_attn_W_B, L0_attn_W_C, L0_attn_W_delta, L0_attn_b_delta, L0_ffn_router_w, L0_ffn_expert_bias, L0_ffn_w1, L0_ffn_w3, L0_ffn_w2, L0_ffn_sw1, L0_ffn_sw3, L0_ffn_sw2):
    import jax
    import jax.numpy as jnp

    def _L0_tok_ref(img, cls_token, cls_pos_embedding, ln1_g, ln1_b, W, bias, ln2_g, ln2_b):
        import jax, jax.numpy as jnp
        import numpy as np
        DIM = 256
        IMG = 96
        P = 16
        C = 3
        TEMP = 10000.0
        EPS = 1e-05
        PATCH_DIM = C * P * P
        HP = IMG // P

        def layernorm(x, gamma, beta):
            mu = jnp.mean(x, axis=-1, keepdims=True)
            var = jnp.var(x, axis=-1, keepdims=True)
            return (x - mu) * jax.lax.rsqrt(var + EPS) * gamma + beta

        def posemb_sincos_2d(h, w, dim, dtype):
            y, x = jnp.meshgrid(jnp.arange(h), jnp.arange(w), indexing='ij')
            omega = jnp.arange(dim // 4, dtype=jnp.float32) / (dim // 4 - 1)
            omega = 1.0 / TEMP ** omega
            y = y.reshape(-1)[:, None] * omega[None, :]
            x = x.reshape(-1)[:, None] * omega[None, :]
            pe = jnp.concatenate((jnp.sin(x), jnp.cos(x), jnp.sin(y), jnp.cos(y)), axis=1)
            return pe.astype(dtype)
        b = img.shape[0]
        x = img.reshape(b, C, HP, P, HP, P)
        x = jnp.transpose(x, (0, 2, 4, 3, 5, 1))
        x = x.reshape(b, HP, HP, PATCH_DIM)
        x = layernorm(x, ln1_g, ln1_b)
        x = jnp.einsum('bhwp,pd->bhwd', x, W) + bias
        x = layernorm(x, ln2_g, ln2_b)
        pe = posemb_sincos_2d(HP, HP, DIM, x.dtype)
        x = x.reshape(b, HP * HP, DIM) + pe[None]
        cls_tokens = jnp.broadcast_to(cls_token + cls_pos_embedding, (b, 1, DIM))
        return jnp.concatenate((cls_tokens, x), axis=1)

    def _L0_txt_ref(x, t0, t1, t2, w0, w1, w2):
        import jax, jax.numpy as jnp
        import numpy as np
        CUTOFFS = (0, 5000, 15000, 25000)
        EMBED_DIM = 256
        EMBED_FACTOR = 4
        BATCH, SEQ = (8, 1024)

        def _bucket_dims():
            return [int(EMBED_DIM // EMBED_FACTOR ** i) for i in range(len(CUTOFFS) - 1)]
        'x: [B, S] int ids -> [B, S, EMBED_DIM] float32.\n            For each bucket i covering [CUTOFFS[i], CUTOFFS[i+1]): local id lookup,\n            project to EMBED_DIM, scatter into output via mask (vectorized jnp.where).\n            '
        tables = (t0, t1, t2)
        weights = (w0, w1, w2)
        out = jnp.zeros(x.shape + (EMBED_DIM,), dtype=jnp.float32)
        for i in range(3):
            lo, hi = (CUTOFFS[i], CUTOFFS[i + 1])
            mask = (x >= lo) & (x < hi)
            local = jnp.clip(x - lo, 0, hi - lo - 1)
            e = tables[i][local]
            proj = jnp.einsum('bsd,de->bse', e, weights[i])
            out = out + jnp.where(mask[..., None], proj, 0.0)
        return out

    def _L0_attn_ref(x, A_log, D_param, W_B, W_C, W_delta, b_delta):
        import jax, jax.numpy as jnp
        import numpy as np
        import math
        B, L, D, N = (8, 512, 256, 16)

        def _reference_tuple_inner(x, A_log, D_param, W_B, W_C, W_delta, b_delta):
            A = -jnp.exp(A_log)
            B_in = jnp.einsum('bld,nd->bln', x, W_B)
            C_in = jnp.einsum('bld,nd->bln', x, W_C)
            delta = jax.nn.softplus(jnp.einsum('bld,ed->ble', x, W_delta) + b_delta)
            h0 = jnp.zeros((x.shape[0], x.shape[2], A.shape[1]), dtype=x.dtype)

            def step(h, inp):
                x_t, B_t, C_t, d_t = inp
                A_bar = jnp.exp(d_t[:, :, None] * A[None])
                h = A_bar * h + (d_t * x_t)[:, :, None] * B_t[:, None, :]
                y_t = jnp.einsum('bdn,bn->bd', h, C_t) + D_param * x_t
                return (h, y_t)
            xs = (jnp.swapaxes(x, 0, 1), jnp.swapaxes(B_in, 0, 1), jnp.swapaxes(C_in, 0, 1), jnp.swapaxes(delta, 0, 1))
            h_final, ys = jax.lax.scan(step, h0, xs)
            y = jnp.swapaxes(ys, 0, 1)
            return (y, h_final)
        return _reference_tuple_inner(x, A_log, D_param, W_B, W_C, W_delta, b_delta)[0]

    def _L0_ffn_ref(x, router_w, expert_bias, w1, w3, w2, sw1, sw3, sw2):
        import jax, jax.numpy as jnp
        import numpy as np
        B, S, DIM = (2, 512, 256)
        HID = 512
        E, NSH, TOPK = (8, 2, 2)

        def _ffn(x, w1, w2, w3):
            return jax.nn.silu(x @ w1.T) * (x @ w3.T) @ w2.T
        bs, sl, d = x.shape
        xf = x.reshape(-1, d)
        shared = jnp.zeros_like(xf)
        for i in range(sw1.shape[0]):
            shared = shared + _ffn(xf, sw1[i], sw2[i], sw3[i])
        logits = xf @ router_w.T + expert_bias
        rw, sel = jax.lax.top_k(logits, TOPK)
        rw = jax.nn.softmax(rw.astype(jnp.float32), axis=-1).astype(x.dtype)
        onehot = jax.nn.one_hot(sel, E, dtype=x.dtype)
        combine = jnp.einsum('tk,tke->te', rw, onehot)

        def body(acc, ew):
            e1, e3, e2, cw = ew
            acc = acc + cw[:, None] * _ffn(xf, e1, e2, e3)
            return (acc, None)
        out, _ = jax.lax.scan(body, jnp.zeros_like(xf), (w1, w3, w2, combine.T))
        out = out + shared
        return out.reshape(bs, sl, -1)
    h = _L0_tok_ref(x, L0_tok_cls_token, L0_tok_cls_pos_embedding, L0_tok_ln1_g, L0_tok_ln1_b, L0_tok_W, L0_tok_bias, L0_tok_ln2_g, L0_tok_ln2_b)
    h = jnp.concatenate([h, _L0_txt_ref(x_txt, L0_txt_t0, L0_txt_t1, L0_txt_t2, L0_txt_w0, L0_txt_w1, L0_txt_w2)], axis=1)
    h = h + _L0_attn_ref(_layernorm(h, axis=-1), L0_attn_A_log, L0_attn_D_param, L0_attn_W_B, L0_attn_W_C, L0_attn_W_delta, L0_attn_b_delta)
    h = h + _L0_ffn_ref(_layernorm(h, axis=-1), L0_ffn_router_w, L0_ffn_expert_bias, L0_ffn_w1, L0_ffn_w3, L0_ffn_w2, L0_ffn_sw1, L0_ffn_sw3, L0_ffn_sw2)
    return h

_drawn_inputs = setup_inputs


def setup_inputs(seed=0):
    import zlib

    import numpy as np

    out = dict(_drawn_inputs(seed))
    spreads = {'L0_tok_ln1_g': (1.0, 0.2),
     'L0_tok_ln1_b': (0.0, 0.1),
     'L0_tok_bias': (0.0, 0.1),
     'L0_tok_ln2_g': (1.0, 0.2),
     'L0_tok_ln2_b': (0.0, 0.1),
     'L0_attn_D_param': (1.0, 0.2),
     'L0_ffn_expert_bias': (0.0, 0.8)}
    factors = {'L0_ffn_router_w': 4.868,
     'L0_ffn_w1': 4.183,
     'L0_ffn_w3': 4.168,
     'L0_ffn_w2': 4.157,
     'L0_ffn_sw1': 3.319,
     'L0_ffn_sw3': 3.227,
     'L0_ffn_sw2': 3.22}
    for name, (base, spread) in spreads.items():
        noise = np.random.default_rng([zlib.crc32(name.encode()), seed]).standard_normal(out[name].shape)
        drawn = base * np.exp(spread * noise) if base else spread * noise
        out[name] = jnp.asarray(drawn.astype(out[name].dtype))
    for name, factor in factors.items():
        out[name] = (out[name] * factor).astype(out[name].dtype)
    return out
```

```python
import math
from contextlib import ExitStack

import numpy as np

import concourse.bass as bass
from concourse import mybir

FP32 = mybir.dt.float32
BF16 = mybir.dt.bfloat16
I32 = mybir.dt.int32
U32 = mybir.dt.uint32
ALU = mybir.AluOpType
ACT = mybir.ActivationFunctionType
AX = mybir.AxisListType

P = 128
B = 4
IMG, CH, PATCH = 96, 3, 16
HP = IMG // PATCH
NPATCH = HP * HP
PDIM = CH * PATCH * PATCH
PC = PDIM // P
D = 256
DH = D // P
TXT = 512
KT = TXT // P
NIMG = NPATCH + 1
L = NIMG + TXT
TILES = KT + 1
NT = B * TILES
N = 16
R = P // N
GROUPS = D // R
LC = (L + 1) // 2
LP = 2 * LC
HID = 512
E = 8
NSH = 2
TOPK = 2
KD = D // P
KH = HID // P
CUTS = (0, 5000, 15000, 25000)
DIMS = (256, 64, 16)
ECOLS = sum(DIMS)
NOWHERE = 100000.0
EPS = 1e-5
WC = L // 3
NWC = 3
TOKENS = B * L
RT = (TOPK * TOKENS + E * (P - 1)) // P
CT = (TOKENS + P - 1) // P
SLOTS = 8


def tile_rows(k):
    return (NIMG, 0) if k == 0 else (P, NIMG + (k - 1) * P)


def schedule():
    def embed(b):
        return [("gather", b)] + [x for k in range(KT) for x in (("etrans", b, k), ("embed", b, k))] + [("place", b), ("ln1", b)]

    def project(b):
        return ([("xtrans", b, k) for k in range(TILES)] + [("zproj", b, h, c) for h in range(DH) for c in range(2)]
                + [("soft", b)] + [("bcproj", b, w, c) for w in range(2) for c in range(2)] + [("split", b)])

    def mix(b):
        return [("ytrans", b, k) for k in range(TILES)] + [("ln2", b)]

    def second(b):
        return [("x2trans", b, k) for k in range(TILES)] + [("logits", b)]

    def hidden(b):
        return [("hidden", b, j, c) for j in range(NSH * KH) for c in range(NWC)]

    def down(b):
        return [("down", b, k) for k in range(TILES)]

    before = [("gather", 0), ("image", 0), ("imtrans", 0), ("immul", 0), ("image2", 0),
              ("image", 1), ("imtrans", 1), ("immul", 1), ("image2", 1)] + embed(0)[1:] + project(0)
    beside = [[] for _ in range(B * GROUPS + 8)]

    def spread(items, first, last):
        for n, x in enumerate(items):
            beside[first + n * (last - first) // len(items)].append(x)

    for b in range(B):
        o = b * GROUPS
        if b + 1 < B:
            spread(embed(b + 1), o, o + 10)
            spread(project(b + 1), o + 13, o + 26)
        if b:
            spread(mix(b - 1), o + 5, o + 9)
            spread(second(b - 1), o + 11, o + 15)
            spread(hidden(b - 1), o + 15, o + 30)
            spread(down(b - 1), o + 31, o + 32)
    after = mix(B - 1) + second(B - 1) + [("route",)] + hidden(B - 1) + down(B - 1)
    return before, beside, after


USES_BANK = ("imtrans", "immul", "etrans", "embed", "place", "xtrans", "zproj", "bcproj", "ytrans",
             "x2trans", "logits", "hidden", "down")


def embed_scan_moe(nc, a):
    before, beside, after = schedule()
    order = {}
    for x in before + [y for p in beside for y in p] + after:
        if x[0] in USES_BANK:
            order[x] = len(order)
    norms = {}
    for x in before + [y for p in beside for y in p] + after:
        if x[0] in ("image", "immul", "ln1", "ln2"):
            norms[x] = len(norms) + 1

    def bank_of(x):
        return order[x] % 2

    def turn_of(x):
        return order[x] // 2 + 1

    ctx = ExitStack()
    with ctx:
        def sem(name):
            return ctx.enter_context(nc.semaphore(name))

        def sb(name, shape, dt=FP32, where=ctx):
            return where.enter_context(nc.sbuf_tensor(name, shape, dt))

        h_all = sb("h_all", [P, NT, D])
        x2_all = sb("x2_all", [P, NT, D])
        ident = sb("ident", [P, P])
        ones = sb("ones", [P, P])
        before_me = sb("before_me", [P, P])
        router = sb("router", [P, KD, E])
        ebias = sb("ebias", [1, E])
        logit = sb("logit", [P, NT, E])
        valid = sb("valid", [P, NT])
        desc = sb("desc", [P, NT, E])
        tile_marks = sb("tile_marks", [P, E, CT])
        tile_ids = sb("tile_ids", [1, RT, E])
        keep = sb("keep", [P, E, NT])
        pick = [sb(f"pick{k}", [P, NT, E]) for k in range(TOPK)]
        work = sb("work", [P, NT, E])
        both = sb("both", [P, NT, E])
        counts = sb("counts", [P, E, NT])
        upto = sb("upto", [P, E, NT])
        over = sb("over", [P, E, CT])
        etiles = sb("etiles", [P, E])
        eend = sb("eend", [P, E])
        past = sb("past", [1, RT, E])
        tile_expert_f = sb("tile_expert_f", [1, RT])
        tile_expert = sb("tile_expert", [1, RT], I32)
        top = [sb(f"top{k}", [P, NT]) for k in range(TOPK)]
        first_of = sb("first_of", [P, NT])
        slot_f = [sb(f"slot_f{k}", [P, NT]) for k in range(TOPK)]
        slot = [sb(f"slot{k}", [P, NT], I32) for k in range(TOPK)]
        gate = [sb(f"gate{k}", [P, NT]) for k in range(TOPK)]
        stat = sb("stat", [P, 6, 6])
        mv = sb("mv", [P, TILES, 2])
        var_eps = sb("var_eps", [P, TILES])
        rstd = sb("rstd", [P, TILES])
        minus_half = sb("minus_half", [P, TILES])

        shared_mem = ExitStack()
        w1s = sb("w1s", [P, KD, NSH, HID], where=shared_mem)
        w3s = sb("w3s", [P, KD, NSH, HID], where=shared_mem)
        w2s = sb("w2s", [P, KH, NSH, D], where=shared_mem)
        gated = sb("gated", [P, NSH * KH, L], where=shared_mem)
        x2T = sb("x2T", [P, KD, L], where=shared_mem)
        tanh_h = sb("tanh_h", [P, 2, WC], where=shared_mem)
        silu_h = sb("silu_h", [P, 2, WC], where=shared_mem)
        flat = gated[:, :, :].rearrange("p a b -> p (a b)")
        pair = 2 * NPATCH
        patches = flat[0:pair, 0:2 * PDIM].rearrange("p (m c) -> p m c", m=2)
        w_tok = flat[:, 2 * PDIM:2 * PDIM + PC * D].rearrange("p (c d) -> p c d", c=PC)
        pT = flat[:, 2 * PDIM + PC * D:2 * PDIM + PC * D + 2 * PC * pair].rearrange("p (m c t) -> p m c t", m=2, c=PC)

        scan_mem = ExitStack()
        parts = sb("parts", [P, 2, 3, DH, LP], BF16, scan_mem)
        stack = sb("stack", [96, 2, 2 * 4, LP], BF16, scan_mem)
        xT = sb("xT", [P, 2, DH, LP], where=scan_mem)
        zed = sb("zed", [P, DH, LP], where=scan_mem)
        aux = sb("aux", [P, DH, LP], where=scan_mem)
        Bn = sb("Bn", [P, 2, LP], where=scan_mem)
        Cn = sb("Cn", [P, 2, LP], where=scan_mem)
        decay = sb("decay", [P, 2, LP], where=scan_mem)
        ring = sb("ring", [P, SLOTS, LP], where=scan_mem)
        rows = sb("rows", [P, KT * ECOLS], where=scan_mem)
        erow = rows[:, :].rearrange("p (k c) -> p k c", k=KT)
        xn = rows[:, 0:TILES * D].rearrange("p (k c) -> p k c", k=TILES)
        eT = sb("eT", [P, 2, 3, P], where=scan_mem)
        yT = sb("yT", [P, DH, LP], where=scan_mem)
        w_emb = sb("w_emb", [P, 3, D], where=scan_mem)
        w_delta = sb("w_delta", [P, KD, D], where=scan_mem)
        w_bc = sb("w_bc", [P, KD, 2, P], where=scan_mem)
        b_delta = sb("b_delta", [P, DH], where=scan_mem)
        d_par = sb("d_par", [P, DH], where=scan_mem)
        a_neg = sb("a_neg", [P, GROUPS], where=scan_mem)
        sel_f = ring[0:96, 0, 0:4 * P].rearrange("p (i m) -> p i m", i=4)
        sel = sb("sel", [96, 4, P], BF16, scan_mem)
        red = sb("red", [P, 4, 32], where=scan_mem)
        ids = sb("ids", [P, B * KT], I32, scan_mem)
        ids_f = sb("ids_f", [P, B * KT], where=scan_mem)
        inside = sb("inside", [P, 3, B * KT], where=scan_mem)
        local_f = sb("local_f", [P, 3, B * KT], where=scan_mem)
        local = sb("local", [P, 3, B * KT], I32, scan_mem)
        g1 = sb("g1", [P, PC], where=scan_mem)
        b1 = sb("b1", [P, PC], where=scan_mem)
        tok_bias = sb("tok_bias", [1, D], where=scan_mem)
        g2, b2, pos = (x2_all[0:pair, NT - 1 - i, :] for i in range(3))
        shift = sb("shift", [pair, 2, NIMG], where=scan_mem)
        cls = sb("cls", [2, D], where=scan_mem)
        cls_put = sb("cls_put", [2, NIMG], where=scan_mem)
        himg = sb("himg", [pair, 2, D], where=scan_mem)
        istat = sb("istat", [pair, 2, 6], where=scan_mem)
        imv = sb("imv", [pair, 2], where=scan_mem)
        scan_mem.close()
        shared_mem.close()

        route_mem = ExitStack()
        ctx.enter_context(route_mem)
        xg = sb("xg", [P, 2, D], where=route_mem)
        xgT = sb("xgT", [P, 2, KD, P], where=route_mem)
        rsilu = sb("rsilu", [P, 2, HID], where=route_mem)
        rgate = sb("rgate", [P, 2, HID], where=route_mem)
        rgT = sb("rgT", [P, 2, KH, P], where=route_mem)
        ry = sb("ry", [P, 2, D], where=route_mem)
        back = sb("back", [P, 4, TOPK, D], where=route_mem)
        used = (2 * D + 2 * KD * P + 6 * HID + 2 * D + 4 * TOPK * D)
        shared_size = KD * NSH * HID * 2 + KH * NSH * D + NSH * KH * L + KD * L + 4 * WC
        sb("filler", [P, shared_size - used + 64], where=route_mem)
        w1r = sb("w1r", [P, KD, E, HID], where=route_mem)
        w3r = sb("w3r", [P, KD, E, HID], where=route_mem)
        w2r = sb("w2r", [P, KH, E, D], where=route_mem)

        sorted_x = nc.dram_tensor("sorted_x", (RT * P, D), FP32).ap()
        sorted_y = nc.dram_tensor("sorted_y", (RT * P, D), FP32).ap()

        psum = ctx.enter_context(nc.psum_tensor("psum", [P, 8, 512], FP32))
        p_delta = psum[:, 0:2, 0:LC]
        p_dx = psum[:, 2:4, 0:LC]
        p_y = psum[:, 4:6, 0:LC]
        fill = [psum[:, 6, :], psum[:, 7, :]]

        ids_in = sem("ids_in")
        image_in = sem("image_in")
        const_in = sem("const_in")
        shared_in = sem("shared_in")
        routed_in = sem("routed_in")
        rows_in = [sem(f"rows_in{b}") for b in range(B)]
        stack_in = [sem(f"stack_in{h}") for h in range(DH)]
        zero_out = sem("zero_out")
        bank_full = [sem("bank_full0"), sem("bank_full1")]
        bank_free = [sem("bank_free0"), sem("bank_free1")]
        zeroed = sem("zeroed")
        local_ready = sem("local_ready")
        rows_zero = sem("rows_zero")
        eT_ready = sem("eT_ready")
        h_ready = sem("h_ready")
        patch_ready = sem("patch_ready")
        pT_ready = sem("pT_ready")
        himg_ready = sem("himg_ready")
        xn_ready = sem("xn_ready")
        xT_ready = sem("xT_ready")
        z_ready = sem("z_ready")
        bc_ready = sem("bc_ready")
        log_ready = sem("log_ready")
        delta_ready = sem("delta_ready")
        dx_ready = sem("dx_ready")
        part1 = sem("part1")
        rest1 = sem("rest1")
        part2 = sem("part2")
        part3 = sem("part3")
        sel_ready = sem("sel_ready")
        a_ready = sem("a_ready")
        spread_delta = sem("spread_delta")
        spread_dx = sem("spread_dx")
        decay_ready = sem("decay_ready")
        bx_ready = sem("bx_ready")
        state_ready = sem("state_ready")
        hc_ready = sem("hc_ready")
        summed = sem("summed")
        y_ready = sem("y_ready")
        h2_ready = sem("h2_ready")
        x2_ready = sem("x2_ready")
        x2T_ready = sem("x2T_ready")
        logit_ready = sem("logit_ready")
        tanh_ready = sem("tanh_ready")
        gated_ready = sem("gated_ready")
        var_ready = sem("var_ready")
        rstd_ready = sem("rstd_ready")
        dve_done = sem("dve_done")
        act_done = sem("act_done")
        both_ready = sem("both_ready")
        rank_ready = sem("rank_ready")
        gap_ready = sem("gap_ready")
        gap_exp = sem("gap_exp")
        slots_ready = sem("slots_ready")
        scattered = sem("scattered")
        h_final = sem("h_final")
        xg_in = [sem("xg_in0"), sem("xg_in1")]
        xgt_full = sem("xgt_full")
        xgT_ready = sem("xgT_ready")
        up_done = sem("up_done")
        rsilu_ready = sem("rsilu_ready")
        rgate_ready = sem("rgate_ready")
        rgt_full = sem("rgt_full")
        rgT_ready = sem("rgT_ready")
        down_done = sem("down_done")
        ry_ready = sem("ry_ready")
        y_out = [sem("y_out0"), sem("y_out1")]
        back_in = [sem(f"back_in{i}") for i in range(4)]
        out_done = [sem(f"out_done{i}") for i in range(4)]
        result_ready = sem("result_ready")

        block = ctx.enter_context(nc.Block())

        def places(visit_scan, visit):
            for x in before:
                visit(x)
            for G, items in enumerate(beside):
                visit_scan(G)
                for x in items:
                    visit(x)
            for x in after:
                visit(x)

        def group(G):
            b, g = divmod(G, GROUPS)
            h, g = divmod(g, GROUPS // DH)
            i, j = divmod(g, 4)
            return b, h, i, j

        NG = B * GROUPS
        IMAGE_LOADS, CONST_LOADS = 5, 20

        @block.sync
        def _(sp):
            sp.dma_start(ids[:, :], a["ids"]).then_inc(ids_in, 16)
            sp.dma_start(patches, a["patches"].rearrange("(m p) c -> p m c", m=2)).then_inc(image_in, 16)
            sp.dma_start(ident[:, :], a["ident"]).then_inc(image_in, 16)
            sp.dma_start(g1[:, :], a["ln1_g"]).then_inc(image_in, 16)
            sp.dma_start(b1[:, :], a["ln1_b"]).then_inc(image_in, 16)
            sp.dma_start(w_tok, a["W"].rearrange("(c p) d -> p c d", p=P)).then_inc(image_in, 16)
            for dst, src in ((w_emb[:, :, :], a["w_emb"]),
                             (tok_bias[:, :], a["tok_bias"]),
                             (g2, a["ln2_g"].to_broadcast([pair, D])),
                             (b2, a["ln2_b"].to_broadcast([pair, D])),
                             (pos, a["pos"]), (shift[:, :, :], a["shift"]),
                             (cls[:, :], a["cls"]), (cls_put[:, :], a["cls_put"]),
                             (w_delta[:, :, :], a["w_delta"]), (w_bc[:, :, :, :], a["w_bc"]),
                             (b_delta[:, :], a["b_delta"]), (d_par[:, :], a["d_par"]),
                             (a_neg[:, :], a["a_log"]), (sel_f, a["sel"]), (red[:, :, :], a["red"]),
                             (router[:, :, :], a["router"]), (ebias[:, :], a["ebias"]),
                             (before_me[:, :], a["before_me"]), (valid[:, :], a["valid"]),
                             (desc[:, :, :], a["desc"])):
                sp.dma_start(dst, src).then_inc(const_in, 16)
            for dst, src in ((w1s, a["sw1"]), (w3s, a["sw3"]), (w2s, a["sw2"]),
                             (tile_marks, a["tile_marks"]), (tile_ids, a["tile_ids"]), (keep, a["keep"])):
                sp.dma_start(dst[tuple([slice(None)] * len(dst.shape))], src).then_inc(shared_in, 16)
            sp.wait_ge(zeroed, 1)
            for j in range(RT):
                sp.dma_start(sorted_x[j * P:(j + 1) * P, :], h_all[:, 0, :]).then_inc(zero_out, 16)
            for b in range(B):
                for h in range(DH):
                    for v in range(2):
                        sp.wait_ge(part3, 2 * b + v + 1)
                        if b:
                            sp.wait_ge(spread_dx, (b - 1) * GROUPS + (h + 1) * GROUPS // DH)
                        for q in range(3):
                            for j in range(4):
                                sp.dma_start(stack[32 * q:32 * q + 32, v, 4 * h + j, :],
                                             parts[32 * j:32 * j + 32, v, q, h, :]).then_inc(stack_in[h], 16)
            sp.wait_ge(x2_ready, B)
            sp.wait_ge(h2_ready, NT)
            sp.wait_ge(summed, NG // 4)
            for w, src in ((w1r, a["w1"]), (w3r, a["w3"]), (w2r, a["w2"])):
                for e in range(E):
                    sp.dma_start(w[:, :, e, :], src[:, :, e, :]).then_inc(routed_in, 16)
            sp.wait_ge(h_final, NT)
            sp.wait_ge(scattered, 16 * TOPK * NT)
            for j in range(RT):
                if j >= 2:
                    sp.wait_ge(xgt_full, j - 1)
                sp.dma_start(xg[:, j % 2, :], sorted_x[j * P:(j + 1) * P, :]).then_inc(xg_in[j % 2], 16)
            for t in range(NT):
                b, k = divmod(t, TILES)
                n, c0 = tile_rows(k)
                sp.wait_ge(result_ready, t + 1)
                sp.dma_start(a["out"][b, c0:c0 + n, :], h_all[0:n, t, :]).then_inc(out_done[t % 4], 16)
            for i in range(4):
                sp.wait_ge(out_done[i], 16 * (NT // 4))

        @block.gpsimd
        def _(pool):
            nc.gpsimd.memset(minus_half[:, :], -0.5)
            nc.gpsimd.memset(rows[:, :], 0.0).then_inc(rows_zero, 1)
            pool.wait_ge(rows_zero, 1)

            def scan_part(G):
                pass

            def item(x):
                if x in norms:
                    rows_, cols_ = (2 * NPATCH, 1) if x[0] in ("image", "immul") else (P, TILES)
                    pool.wait_ge(var_ready, norms[x])
                    nc.gpsimd.tensor_tensor(rstd[0:rows_, 0:cols_], var_eps[0:rows_, 0:cols_],
                                            minus_half[0:rows_, 0:cols_], ALU.pow).then_inc(rstd_ready, 1)
                elif x[0] == "gather":
                    b = x[1]
                    if b:
                        last = ("xtrans", b - 1, TILES - 1)
                        first = ("xtrans", b - 1, TILES - 2)
                        pool.wait_ge(bank_full[bank_of(first)], turn_of(first))
                        pool.wait_ge(bank_full[bank_of(last)], turn_of(last))
                        nc.gpsimd.memset(rows[:, :], 0.0).then_inc(rows_zero, 1)
                        pool.wait_ge(rows_zero, b + 1)
                    else:
                        pool.wait_ge(local_ready, 1)
                    for k in range(KT):
                        c0 = 0
                        for t in range(3):
                            pool.indirect_dma_start(
                                erow[:, k, c0:c0 + DIMS[t]], None, a[f"t{t}"],
                                bass.IndirectOffsetOnAxis(ap=local[:, t, b * KT + k:b * KT + k + 1], axis=0),
                                bounds_check=CUTS[t + 1] - CUTS[t] - 1, oob_is_err=False).then_inc(rows_in[b], 16)
                            c0 += DIMS[t]
                elif x[0] == "split":
                    b = x[1]
                    for v in range(2):
                        pool.wait_ge(part1, 2 * b + v + 1)
                        if v:
                            pool.wait_ge(part3, 2 * b + 1)
                        nc.gpsimd.tensor_tensor(aux[:, :, :], zed[:, :, :], parts[:, v, 0, :, :], ALU.subtract).then_inc(rest1, 1)
                        pool.wait_ge(rest1, 2 * b + v + 1)
                        pool.wait_ge(part2, 2 * b + v + 1)
                        nc.gpsimd.tensor_tensor(parts[:, v, 2, :, :], aux[:, :, :], parts[:, v, 1, :, :], ALU.subtract).then_inc(part3, 1)

            places(scan_part, item)
            pool.wait_ge(slots_ready, 1)
            pool.wait_ge(zero_out, 16 * RT)
            for t in range(NT):
                n, _ = tile_rows(t % TILES)
                for k in range(TOPK):
                    pool.indirect_dma_start(
                        sorted_x, bass.IndirectOffsetOnAxis(ap=slot[k][0:n, t:t + 1], axis=0),
                        x2_all[0:n, t, :], None).then_inc(scattered, 16)
            pool.wait_ge(y_out[0], 16 * ((RT + 1) // 2))
            pool.wait_ge(y_out[1], 16 * (RT // 2))
            for t in range(NT):
                n, _ = tile_rows(t % TILES)
                if t >= 4:
                    pool.wait_ge(result_ready, t - 3)
                for k in range(TOPK):
                    pool.indirect_dma_start(
                        back[0:n, t % 4, k, :], None, sorted_y,
                        bass.IndirectOffsetOnAxis(ap=slot[k][0:n, t:t + 1], axis=0)).then_inc(back_in[t % 4], 16)

        @block.tensor
        def _(pe):
            def enter(x):
                n = order[x]
                if n >= 2:
                    pe.wait_ge(bank_free[n % 2], n // 2)
                return fill[n % 2]

            def leave(x, ins):
                ins.then_inc(bank_full[bank_of(x)], 1)

            def scan_part(G):
                if G < NG:
                    b, h, i, j = group(G)
                    if G % (GROUPS // DH) == 0:
                        pe.wait_ge(stack_in[h], 16 * 24 * (b + 1))
                    if G == 0:
                        pe.wait_ge(sel_ready, 1)
                    if G:
                        pe.wait_ge(decay_ready, G)
                    for c in range(2):
                        last = nc.tensor.matmul(p_delta[:, c, :], sel[:, i, :], stack[:, 0, 4 * h + j, c * LC:(c + 1) * LC],
                                                start=True, stop=True)
                    last.then_inc(spread_delta, 1)
                    if G:
                        pe.wait_ge(bx_ready, G)
                    for c in range(2):
                        last = nc.tensor.matmul(p_dx[:, c, :], sel[:, i, :], stack[:, 1, 4 * h + j, c * LC:(c + 1) * LC],
                                                start=True, stop=True)
                    last.then_inc(spread_dx, 1)
                if 6 <= G < NG + 4 and G % 4 == 2:
                    q = G // 4 - 1
                    b, h, i, _ = group(4 * q)
                    pe.wait_ge(hc_ready, 4 * q + 4)
                    if i == 0 and q:
                        pe.wait_ge(y_ready, q // 4)
                    for c in range(2):
                        for j in range(4):
                            last = nc.tensor.matmul(p_y[32 * j:32 * j + 32, c, :], red[:, i, :],
                                                    ring[:, (4 * q + j) % SLOTS, c * LC:(c + 1) * LC],
                                                    start=(i == 0), stop=(i == 3), tile_position=(0, 32 * j))
                    last.then_inc(summed, 1)

            def item(x):
                kind = x[0]
                if kind == "imtrans":
                    m = x[1]
                    f = enter(x)
                    pe.wait_ge(patch_ready, m + 1)
                    for c in range(PC):
                        last = nc.tensor.transpose(f[:, c * pair:(c + 1) * pair], patches[:, m, c * P:(c + 1) * P],
                                                   ident[0:pair, 0:pair])
                    leave(x, last)
                elif kind == "immul":
                    m = x[1]
                    f = enter(x)
                    pe.wait_ge(pT_ready, m + 1)
                    pe.wait_ge(const_in, 16 * CONST_LOADS)
                    for c in range(PC):
                        nc.tensor.matmul(f[0:pair, 0:D], pT[:, m, c, :], w_tok[:, c, :], start=(c == 0), stop=False)
                    leave(x, nc.tensor.matmul(f[0:pair, 0:D], ones[0:1, 0:pair], tok_bias[:, :], start=False, stop=True))
                elif kind == "etrans":
                    b, k = x[1:]
                    f = enter(x)
                    if k == 0:
                        pe.wait_ge(rows_in[b], 16 * 3 * KT)
                    nc.tensor.transpose(f[:, 0:P], erow[:, k, 0:P], ident[:, :])
                    nc.tensor.transpose(f[:, P:2 * P], erow[:, k, P:2 * P], ident[:, :])
                    leave(x, nc.tensor.transpose(f[0:ECOLS - D, 2 * P:3 * P], erow[:, k, D:ECOLS], ident[:, :]))
                elif kind == "embed":
                    b, k = x[1:]
                    f = enter(x)
                    pe.wait_ge(eT_ready, b * KT + k + 1)
                    nc.tensor.matmul(f[:, 0:D], eT[:, k % 2, 0, :], w_emb[:, 0, :], start=True, stop=False)
                    nc.tensor.matmul(f[:, 0:D], eT[:, k % 2, 1, :], w_emb[:, 1, :], start=False, stop=False)
                    leave(x, nc.tensor.matmul(f[:, 0:D], eT[0:ECOLS - D, k % 2, 2, :], w_emb[0:ECOLS - D, 2, :],
                                              start=False, stop=True))
                elif kind == "place":
                    b = x[1]
                    f = enter(x)
                    pe.wait_ge(himg_ready, b // 2 + 1)
                    nc.tensor.matmul(f[0:NIMG, 0:D], shift[:, b % 2, :], himg[:, b // 2, :], start=True, stop=False)
                    leave(x, nc.tensor.matmul(f[0:NIMG, 0:D], cls_put[:, :], cls[:, :], start=False, stop=True))
                elif kind == "xtrans":
                    b, k = x[1:]
                    n, _ = tile_rows(k)
                    f = enter(x)
                    pe.wait_ge(xn_ready, b + 1)
                    for h in range(DH):
                        last = nc.tensor.transpose(f[:, h * P:h * P + n], xn[0:n, k, h * P:(h + 1) * P], ident[0:n, 0:n])
                    leave(x, last)
                elif kind == "zproj":
                    b, h, c = x[1:]
                    f = enter(x)
                    pe.wait_ge(xT_ready, TILES * (b + 1))
                    for k in range(KD):
                        last = nc.tensor.matmul(f[:, 0:LC], w_delta[:, k, h * P:(h + 1) * P],
                                                xT[:, b % 2, k, c * LC:(c + 1) * LC], start=(k == 0), stop=(k == KD - 1))
                    leave(x, last)
                elif kind == "bcproj":
                    b, w, c = x[1:]
                    f = enter(x)
                    for k in range(KD):
                        last = nc.tensor.matmul(f[:, 0:LC], w_bc[:, k, w, :],
                                                xT[:, b % 2, k, c * LC:(c + 1) * LC], start=(k == 0), stop=(k == KD - 1))
                    leave(x, last)
                elif kind == "ytrans":
                    b, k = x[1:]
                    n, c0 = tile_rows(k)
                    f = enter(x)
                    pe.wait_ge(y_ready, DH * (b + 1))
                    for h in range(DH):
                        last = nc.tensor.transpose(f[0:n, h * P:(h + 1) * P], yT[:, h, c0:c0 + n], ident[:, :])
                    leave(x, last)
                elif kind == "x2trans":
                    b, k = x[1:]
                    n, _ = tile_rows(k)
                    f = enter(x)
                    pe.wait_ge(x2_ready, b + 1)
                    for h in range(DH):
                        last = nc.tensor.transpose(f[:, h * P:h * P + n], x2_all[0:n, b * TILES + k, h * P:(h + 1) * P],
                                                   ident[0:n, 0:n])
                    leave(x, last)
                elif kind == "logits":
                    b = x[1]
                    f = enter(x)
                    pe.wait_ge(x2T_ready, TILES * (b + 1))
                    for k in range(TILES):
                        n, c0 = tile_rows(k)
                        for h in range(KD):
                            nc.tensor.matmul(f[0:n, k * E:(k + 1) * E], x2T[:, h, c0:c0 + n], router[:, h, :],
                                             start=(h == 0), stop=False)
                        last = nc.tensor.matmul(f[0:n, k * E:(k + 1) * E], ones[0:1, 0:n], ebias[:, :], start=False, stop=True)
                    leave(x, last)
                elif kind == "hidden":
                    b, j, c = x[1:]
                    e, m = divmod(j, KH)
                    f = enter(x)
                    if b == 0 and j == 0 and c == 0:
                        pe.wait_ge(shared_in, 16 * 6)
                    for w, o in ((w1s, 0), (w3s, WC)):
                        for k in range(KD):
                            last = nc.tensor.matmul(f[:, o:o + WC], w[:, k, e, m * P:(m + 1) * P],
                                                    x2T[:, k, c * WC:(c + 1) * WC], start=(k == 0), stop=(k == KD - 1))
                    leave(x, last)
                elif kind == "down":
                    b, k = x[1:]
                    n, c0 = tile_rows(k)
                    f = enter(x)
                    pe.wait_ge(gated_ready, NSH * KH * NWC * (b + 1))
                    for j in range(NSH * KH):
                        e, m = divmod(j, KH)
                        last = nc.tensor.matmul(f[0:n, 0:D], gated[:, j, c0:c0 + n], w2s[:, m, e, :],
                                                start=(j == 0), stop=(j == NSH * KH - 1))
                    leave(x, last)
                elif kind == "route":
                    pe.wait_ge(both_ready, 1)
                    m = both[:, :, :].rearrange("p t e -> p (t e)")
                    nc.tensor.matmul(psum[:, 0, 0:NT * E], before_me[:, :], m, start=True, stop=True)
                    nc.tensor.matmul(psum[:, 1, 0:NT * E], ones[:, :], m, start=True, stop=True).then_inc(rank_ready, 1)

            pe.wait_ge(image_in, 16 * IMAGE_LOADS)
            places(scan_part, item)

            def xtrans(j):
                pe.wait_ge(xg_in[j % 2], 16 * (j // 2 + 1))
                if j:
                    pe.wait_ge(xgT_ready, j)
                for h in range(KD):
                    last = nc.tensor.transpose(psum[:, 0, h * P:(h + 1) * P], xg[:, j % 2, h * P:(h + 1) * P], ident[:, :])
                last.then_inc(xgt_full, 1)

            def up(j):
                pe.wait_ge(xgT_ready, j + 1)
                if j >= 2:
                    pe.wait_ge(rgate_ready, j - 1)
                ex = pe.value_load(tile_expert[0:1, j:j + 1], min_val=0, max_val=E - 1)
                for w, bank in ((w1r, 1 + j % 2), (w3r, 3 + j % 2)):
                    for k in range(KD):
                        last = nc.tensor.matmul(psum[:, bank, :], xgT[:, j % 2, k, :],
                                                w[:, k, bass.ds(ex, 1), :], start=(k == 0), stop=(k == KD - 1))
                    last.then_inc(up_done, 1)

            def gtrans(j):
                pe.wait_ge(rgate_ready, j + 1)
                if j >= 2:
                    pe.wait_ge(rgT_ready, j - 1)
                for m in range(KH):
                    last = nc.tensor.transpose(psum[:, 5 + j % 2, m * P:(m + 1) * P], rgate[:, j % 2, m * P:(m + 1) * P],
                                               ident[:, :])
                last.then_inc(rgt_full, 1)

            def down(j):
                pe.wait_ge(rgT_ready, j + 1)
                if j:
                    pe.wait_ge(ry_ready, j)
                ex = pe.value_load(tile_expert[0:1, j:j + 1], min_val=0, max_val=E - 1)
                for m in range(KH):
                    last = nc.tensor.matmul(psum[:, 7, 0:D], rgT[:, j % 2, m, :], w2r[:, m, bass.ds(ex, 1), :],
                                            start=(m == 0), stop=(m == KH - 1))
                last.then_inc(down_done, 1)

            pe.wait_ge(routed_in, 16 * 3 * E)
            pe.wait_ge(slots_ready, 1)
            xtrans(0)
            for j in range(RT):
                up(j)
                if j + 1 < RT:
                    xtrans(j + 1)
                if j:
                    down(j - 1)
                gtrans(j)
            down(RT - 1)

        @block.scalar
        def _(act):
            steps = [0]

            def link(ins):
                steps[0] += 1
                ins.then_inc(act_done, 1)
                act.wait_ge(act_done, steps[0])

            def full(x):
                act.wait_ge(bank_full[bank_of(x)], turn_of(x))
                return fill[bank_of(x)]

            act.wait_ge(const_in, 16 * CONST_LOADS)
            nc.scalar.activation(sel[:, :, :], sel_f, ACT.Copy).then_inc(sel_ready, 1)
            link(nc.scalar.activation(a_neg[:, :], a_neg[:, :], ACT.Exp))
            link(nc.scalar.mul(a_neg[:, :], a_neg[:, :], -1.0))

            def scan_part(G):
                if G < NG:
                    b, h, i, j = group(G)
                    act.wait_ge(spread_delta, G + 1)
                    if G >= 2:
                        act.wait_ge(state_ready, G - 1)
                    nc.scalar.activation(decay[:, G % 2, :].rearrange("p (c t) -> p c t", c=2), p_delta, ACT.Exp,
                                         scale=a_neg[:, G % GROUPS:G % GROUPS + 1]).then_inc(decay_ready, 1)

            def item(x):
                kind = x[0]
                if kind == "etrans":
                    b, k = x[1:]
                    f = full(x)
                    if k >= 2:
                        y = ("embed", b, k - 2)
                        act.wait_ge(bank_full[bank_of(y)], turn_of(y))
                    nc.scalar.copy(eT[:, k % 2, 0:2, :].rearrange("p c t -> p (c t)"), f[:, 0:2 * P])
                    nc.scalar.copy(eT[0:ECOLS - D, k % 2, 2, :], f[0:ECOLS - D, 2 * P:3 * P]).then_inc(eT_ready, 1)
                    act.wait_ge(eT_ready, b * KT + k + 1)
                    act.sem_inc(bank_free[bank_of(x)], 1)
                elif kind in ("embed", "place"):
                    b = x[1]
                    k = 1 + x[2] if kind == "embed" else 0
                    n, _ = tile_rows(k)
                    f = full(x)
                    act.wait_ge(zeroed, 1)
                    if b == 0 and k == 1:
                        act.wait_ge(zero_out, 16 * RT)
                    link(nc.scalar.copy(h_all[0:n, b * TILES + k, :], f[0:n, 0:D]))
                    act.sem_inc(h_ready, 1)
                    act.sem_inc(bank_free[bank_of(x)], 1)
                elif kind == "xtrans":
                    b, k = x[1:]
                    n, c0 = tile_rows(k)
                    f = full(x)
                    if b >= 2 and k == 0:
                        act.wait_ge(y_ready, DH * (b - 1))
                        act.wait_ge(dx_ready, b - 1)
                    link(nc.scalar.copy(xT[:, b % 2, :, c0:c0 + n],
                                        f[:, 0:2 * P].rearrange("p (h t) -> p h t", h=2)[:, :, 0:n]))
                    act.sem_inc(xT_ready, 1)
                    act.sem_inc(bank_free[bank_of(x)], 1)
                elif kind == "zproj":
                    b, h, c = x[1:]
                    f = full(x)
                    if b and h == 0 and c == 0:
                        act.wait_ge(part3, 2 * b)
                    link(nc.scalar.activation(zed[:, h, c * LC:(c + 1) * LC], f[:, 0:LC], ACT.Identity,
                                              bias=b_delta[:, h:h + 1]))
                    act.sem_inc(bank_free[bank_of(x)], 1)
                elif kind == "soft":
                    link(nc.scalar.activation(aux[:, :, :], zed[:, :, :], ACT.Abs))
                    link(nc.scalar.activation(aux[:, :, :], aux[:, :, :], ACT.Exp, scale=-1.0))
                    nc.scalar.activation(aux[:, :, :], aux[:, :, :], ACT.Ln, bias=1.0).then_inc(log_ready, 1)
                elif kind == "bcproj":
                    b, w, c = x[1:]
                    f = full(x)
                    if b >= 2:
                        act.wait_ge(hc_ready, (b - 1) * GROUPS)
                    link(nc.scalar.copy((Bn, Cn)[w][:, b % 2, c * LC:(c + 1) * LC], f[:, 0:LC]))
                    act.sem_inc(bc_ready, 1)
                    act.sem_inc(bank_free[bank_of(x)], 1)
                elif kind == "split":
                    b = x[1]
                    for v in range(2):
                        act.wait_ge((delta_ready, dx_ready)[v], b + 1)
                        if b:
                            for h in range(DH):
                                act.wait_ge(stack_in[h], 16 * 24 * b)
                        nc.scalar.copy(parts[:, v, 0, :, :], zed[:, :, :]).then_inc(part1, 1)
                        act.wait_ge(rest1, 2 * b + v + 1)
                        nc.scalar.copy(parts[:, v, 1, :, :], aux[:, :, :]).then_inc(part2, 1)
                elif kind == "x2trans":
                    b, k = x[1:]
                    n, c0 = tile_rows(k)
                    f = full(x)
                    if b and k == 0:
                        act.wait_ge(gated_ready, NSH * KH * NWC * b)
                    link(nc.scalar.copy(x2T[:, :, c0:c0 + n],
                                        f[:, 0:2 * P].rearrange("p (h t) -> p h t", h=2)[:, :, 0:n]))
                    act.sem_inc(x2T_ready, 1)
                    act.sem_inc(bank_free[bank_of(x)], 1)
                elif kind == "logits":
                    b = x[1]
                    f = full(x)
                    act.wait_ge(zeroed, 1)
                    nc.scalar.copy(logit[0:NIMG, b * TILES, :], f[0:NIMG, 0:E])
                    link(nc.scalar.copy(logit[:, b * TILES + 1:(b + 1) * TILES, :],
                                        f[:, E:TILES * E].rearrange("p (k e) -> p k e", e=E)))
                    act.sem_inc(logit_ready, 1)
                    act.sem_inc(bank_free[bank_of(x)], 1)
                elif kind == "hidden":
                    b, j, c = x[1:]
                    f = full(x)
                    n = (b * NSH * KH + j) * NWC + c
                    if n >= 2:
                        act.wait_ge(gated_ready, n - 1)
                    nc.scalar.activation(tanh_h[:, n % 2, :], f[:, 0:WC], ACT.Tanh, scale=0.5).then_inc(tanh_ready, 1)
                elif kind == "route":
                    act.wait_ge(gap_ready, 1)
                    nc.scalar.activation(gate[1][:, :], gate[1][:, :], ACT.Exp).then_inc(gap_exp, 1)

            places(scan_part, item)

            for j in range(RT + 1):
                if j < RT:
                    act.wait_ge(xgt_full, j + 1)
                    if j >= 2:
                        act.wait_ge(up_done, 2 * (j - 1))
                    nc.scalar.copy(xgT[:, j % 2, :, :].rearrange("p c t -> p (c t)"), psum[:, 0, 0:D]).then_inc(xgT_ready, 1)
                if j >= 1:
                    if j >= 2:
                        y = j - 2
                        act.wait_ge(down_done, y + 1)
                        if y >= 2:
                            act.wait_ge(y_out[y % 2], 16 * (y // 2))
                        nc.scalar.copy(ry[:, y % 2, :], psum[:, 7, 0:D]).then_inc(ry_ready, 1)
                        act.wait_ge(ry_ready, y + 1)
                        act.dma_start(sorted_y[y * P:(y + 1) * P, :], ry[:, y % 2, :]).then_inc(y_out[y % 2], 16)
                if j < RT:
                    act.wait_ge(up_done, 2 * j + 1)
                    if j >= 2:
                        act.wait_ge(rgate_ready, j - 1)
                    nc.scalar.activation(rsilu[:, j % 2, :], psum[:, 1 + j % 2, :], ACT.Silu).then_inc(rsilu_ready, 1)
            y = RT - 1
            act.wait_ge(down_done, y + 1)
            act.wait_ge(y_out[y % 2], 16 * (y // 2))
            nc.scalar.copy(ry[:, y % 2, :], psum[:, 7, 0:D]).then_inc(ry_ready, 1)
            act.wait_ge(ry_ready, y + 1)
            act.dma_start(sorted_y[y * P:(y + 1) * P, :], ry[:, y % 2, :]).then_inc(y_out[y % 2], 16)

        @block.vector
        def _(dve):
            steps = [0]

            def link(ins):
                steps[0] += 1
                ins.then_inc(dve_done, 1)
                dve.wait_ge(dve_done, steps[0])

            def full(x):
                dve.wait_ge(bank_full[bank_of(x)], turn_of(x))
                return fill[bank_of(x)]

            v = nc.vector
            v.memset(h_all[:, 0, :], 0.0).then_inc(zeroed, 1)
            for b in range(1, B):
                v.memset(h_all[:, b * TILES, :], 0.0)
            v.memset(logit[:, :, :], 0.0)
            v.memset(ones[:, :], 1.0)
            link(v.memset(xT[:, :, :, L:LP], 0.0))
            dve.wait_ge(ids_in, 16)
            link(v.tensor_copy(ids_f[:, :], ids[:, :]))
            for t in range(3):
                lo, hi = CUTS[t], CUTS[t + 1]
                link(v.tensor_scalar(inside[:, t, :], ids_f[:, :], float(lo), None, ALU.is_ge))
                link(v.scalar_tensor_tensor(inside[:, t, :], ids_f[:, :], float(hi), inside[:, t, :], ALU.is_lt, ALU.mult))
                link(v.scalar_tensor_tensor(local_f[:, t, :], ids_f[:, :], float(lo) + NOWHERE, inside[:, t, :],
                                            ALU.subtract, ALU.mult))
                link(v.tensor_scalar(local_f[:, t, :], local_f[:, t, :], NOWHERE, None, ALU.add))
            v.tensor_copy(local[:, :, :], local_f[:, :, :]).then_inc(local_ready, 1)

            def scan_part(G):
                if G < NG:
                    b, h, i, j = group(G)
                    if G % GROUPS == 0:
                        dve.wait_ge(bc_ready, 4 * (b + 1))
                    dve.wait_ge(spread_dx, G + 1)
                    if G >= SLOTS:
                        dve.wait_ge(summed, (G - SLOTS) // 4 + 1)
                    v.tensor_tensor(ring[:, G % SLOTS, :].rearrange("p (c t) -> p c t", c=2), p_dx,
                                    Bn[:, b % 2, :].rearrange("p (c t) -> p c t", c=2), ALU.mult).then_inc(bx_ready, 1)
                if 1 <= G <= NG:
                    s = G - 1
                    dve.wait_ge(decay_ready, s + 1)
                    dve.wait_ge(bx_ready, s + 1)
                    r = ring[:, s % SLOTS, :]
                    v.tensor_tensor_scan(r, decay[:, s % 2, :], r, 0.0, ALU.mult, ALU.add).then_inc(state_ready, 1)
                if 2 <= G <= NG + 1:
                    s = G - 2
                    dve.wait_ge(state_ready, s + 1)
                    r = ring[:, s % SLOTS, :]
                    v.tensor_tensor(r, r, Cn[:, (s // GROUPS) % 2, :], ALU.mult).then_inc(hc_ready, 1)
                if G >= 19 and (G - 19) % 16 == 0:
                    n = (G - 19) // 16
                    b, h = divmod(n, DH)
                    dve.wait_ge(summed, 4 * (n + 1))
                    if b:
                        y = ("ytrans", b - 1, TILES - 1)
                        z = ("ytrans", b - 1, TILES - 2)
                        dve.wait_ge(bank_full[bank_of(y)], turn_of(y))
                        dve.wait_ge(bank_full[bank_of(z)], turn_of(z))
                    v.scalar_tensor_tensor(yT[:, h, :].rearrange("p (c t) -> p c t", c=2),
                                           xT[:, b % 2, h, :].rearrange("p (c t) -> p c t", c=2), d_par[:, h:h + 1], p_y,
                                           ALU.mult, ALU.add).then_inc(y_ready, 1)

            def norm(dst, src, turn):
                for k in range(TILES):
                    last = v.bn_stats(stat[:, k, :], src[:, k, :])
                link(last)
                for k in range(TILES):
                    last = v.bn_aggr(mv[:, k, :], stat[:, k, :])
                link(last)
                v.tensor_scalar(var_eps[:, :], mv[:, :, 1], EPS, None, ALU.add).then_inc(var_ready, 1)
                dve.wait_ge(rstd_ready, turn)
                for k in range(TILES):
                    last = v.tensor_scalar(dst[:, k, :], src[:, k, :], mv[:, k, 0:1], rstd[:, k:k + 1],
                                           ALU.subtract, ALU.mult)
                return last

            def item(x):
                kind = x[0]
                if kind == "image":
                    m = x[1]
                    if m == 0:
                        dve.wait_ge(image_in, 16 * IMAGE_LOADS)
                    half = PDIM // 2
                    v.bn_stats(istat[:, 0, :], patches[:, m, 0:half])
                    link(v.bn_stats(istat[:, 1, :], patches[:, m, half:PDIM]))
                    link(v.bn_aggr(imv[:, :], istat[:, :, :].rearrange("p a b -> p (a b)")))
                    v.tensor_scalar(var_eps[0:pair, 0:1], imv[:, 1:2], EPS, None, ALU.add).then_inc(var_ready, 1)
                    dve.wait_ge(rstd_ready, norms[x])
                    v.tensor_scalar(patches[:, m, :], patches[:, m, :], imv[:, 0:1], rstd[0:pair, 0:1],
                                    ALU.subtract, ALU.mult).then_inc(patch_ready, 1)
                elif kind == "imtrans":
                    m = x[1]
                    f = full(x)
                    src = f[:, 0:PC * pair].rearrange("p (c t) -> p c t", c=PC)
                    link(v.tensor_tensor(pT[:, m, :, :], src, g1[:, :].unsqueeze(2).to_broadcast([P, PC, pair]), ALU.mult))
                    dve.sem_inc(bank_free[bank_of(x)], 1)
                    v.tensor_tensor(pT[:, m, :, :], pT[:, m, :, :], b1[:, :].unsqueeze(2).to_broadcast([P, PC, pair]),
                                    ALU.add).then_inc(pT_ready, 1)
                elif kind == "immul":
                    m = x[1]
                    f = full(x)
                    link(v.bn_stats(istat[:, 0, :], f[0:pair, 0:D]))
                    link(v.bn_aggr(imv[:, :], istat[:, 0, :]))
                    v.tensor_scalar(var_eps[0:pair, 0:1], imv[:, 1:2], EPS, None, ALU.add).then_inc(var_ready, 1)
                    dve.wait_ge(rstd_ready, norms[x])
                    link(v.tensor_scalar(himg[:, m, :], f[0:pair, 0:D], imv[:, 0:1], rstd[0:pair, 0:1], ALU.subtract, ALU.mult))
                    dve.sem_inc(bank_free[bank_of(x)], 1)
                elif kind == "image2":
                    m = x[1]
                    dve.wait_ge(const_in, 16 * CONST_LOADS)
                    link(v.tensor_tensor(himg[:, m, :], himg[:, m, :], g2, ALU.mult))
                    link(v.tensor_tensor(himg[:, m, :], himg[:, m, :], b2, ALU.add))
                    v.tensor_tensor(himg[:, m, :], himg[:, m, :], pos, ALU.add).then_inc(himg_ready, 1)
                elif kind == "ln1":
                    b = x[1]
                    dve.wait_ge(h_ready, TILES * (b + 1))
                    norm(xn, h_all[:, b * TILES:(b + 1) * TILES, :], norms[x]).then_inc(xn_ready, 1)
                elif kind == "soft":
                    b = x[1]
                    dve.wait_ge(log_ready, b + 1)
                    v.scalar_tensor_tensor(zed[:, :, :], zed[:, :, :], 0.0, aux[:, :, :], ALU.max, ALU.add).then_inc(delta_ready, 1)
                elif kind == "split":
                    b = x[1]
                    dve.wait_ge(rest1, 2 * b + 1)
                    dve.wait_ge(delta_ready, b + 1)
                    v.tensor_tensor(zed[:, :, :], zed[:, :, :], xT[:, b % 2, :, :], ALU.mult).then_inc(dx_ready, 1)
                elif kind == "ytrans":
                    b, k = x[1:]
                    n, _ = tile_rows(k)
                    f = full(x)
                    t = b * TILES + k
                    link(v.tensor_tensor(h_all[0:n, t, :], h_all[0:n, t, :], f[0:n, 0:D], ALU.add))
                    dve.sem_inc(h2_ready, 1)
                    dve.sem_inc(bank_free[bank_of(x)], 1)
                elif kind == "ln2":
                    b = x[1]
                    norm(x2_all[:, b * TILES:(b + 1) * TILES, :],
                         h_all[:, b * TILES:(b + 1) * TILES, :], norms[x]).then_inc(x2_ready, 1)
                elif kind == "hidden":
                    b, j, c = x[1:]
                    f = full(x)
                    n = (b * NSH * KH + j) * NWC + c
                    dve.wait_ge(tanh_ready, n + 1)
                    if b and j == 0 and c == 0:
                        y = ("down", b - 1, TILES - 1)
                        z = ("down", b - 1, TILES - 2)
                        dve.wait_ge(bank_full[bank_of(y)], turn_of(y))
                        dve.wait_ge(bank_full[bank_of(z)], turn_of(z))
                    link(v.scalar_tensor_tensor(silu_h[:, n % 2, :], tanh_h[:, n % 2, :], 1.0, f[:, 0:WC], ALU.add, ALU.mult))
                    link(v.scalar_tensor_tensor(gated[:, j, c * WC:(c + 1) * WC], f[:, WC:2 * WC], 0.5, silu_h[:, n % 2, :],
                                                ALU.mult, ALU.mult))
                    dve.sem_inc(gated_ready, 1)
                    dve.sem_inc(bank_free[bank_of(x)], 1)
                elif kind == "down":
                    b, k = x[1:]
                    n, _ = tile_rows(k)
                    f = full(x)
                    t = b * TILES + k
                    link(v.tensor_tensor(h_all[0:n, t, :], h_all[0:n, t, :], f[0:n, 0:D], ALU.add))
                    dve.sem_inc(h_final, 1)
                    dve.sem_inc(bank_free[bank_of(x)], 1)
                elif kind == "route":
                    route()

            def route():
                dve.wait_ge(logit_ready, B)
                dve.wait_ge(shared_in, 16 * 6)
                src = logit
                for k in range(TOPK):
                    link(v.tensor_reduce(top[k][:, :], src[:, :, :], AX.X, ALU.max))
                    link(v.tensor_tensor(pick[k][:, :, :], src[:, :, :], top[k][:, :].unsqueeze(2).to_broadcast([P, NT, E]),
                                         ALU.is_equal))
                    link(v.tensor_tensor(pick[k][:, :, :], pick[k][:, :, :], desc[:, :, :], ALU.mult))
                    link(v.tensor_reduce(first_of[:, :], pick[k][:, :, :], AX.X, ALU.max))
                    link(v.tensor_tensor(pick[k][:, :, :], desc[:, :, :], first_of[:, :].unsqueeze(2).to_broadcast([P, NT, E]),
                                         ALU.is_equal))
                    if k == 0:
                        link(v.scalar_tensor_tensor(work[:, :, :], pick[0][:, :, :], -3e38, logit[:, :, :], ALU.mult, ALU.add))
                        src = work
                v.tensor_tensor(gate[1][:, :], top[1][:, :], top[0][:, :], ALU.subtract).then_inc(gap_ready, 1)
                link(v.tensor_tensor(both[:, :, :], pick[0][:, :, :], pick[1][:, :, :], ALU.add))
                v.tensor_tensor(both[:, :, :], both[:, :, :], valid[:, :].unsqueeze(2).to_broadcast([P, NT, E]),
                                ALU.mult).then_inc(both_ready, 1)
                dve.wait_ge(gap_exp, 1)
                link(v.tensor_scalar(gate[0][:, :], gate[1][:, :], 1.0, None, ALU.add))
                link(v.reciprocal(gate[0][:, :], gate[0][:, :]))
                link(v.tensor_tensor(gate[1][:, :], gate[1][:, :], gate[0][:, :], ALU.mult))
                dve.wait_ge(rank_ready, 1)
                link(v.tensor_copy(counts[:, :, :], psum[:, 1, 0:NT * E].rearrange("p (t e) -> p e t", e=E)))
                link(v.tensor_tensor_scan(upto[:, :, :].rearrange("p e t -> p (e t)"), keep[:, :, :].rearrange("p e t -> p (e t)"),
                                          counts[:, :, :].rearrange("p e t -> p (e t)"), 0.0, ALU.mult, ALU.add))
                link(v.tensor_tensor(counts[:, :, :], upto[:, :, :], counts[:, :, :], ALU.subtract))
                link(v.tensor_tensor(over[:, :, :], upto[:, :, NT - 1:NT].to_broadcast([P, E, CT]), tile_marks[:, :, :], ALU.is_gt))
                link(v.tensor_reduce(etiles[:, :], over[:, :, :], AX.X, ALU.add))
                link(v.tensor_tensor_scan(eend[:, :], ones[:, 0:E], etiles[:, :], 0.0, ALU.mult, ALU.add))
                link(v.tensor_tensor(past[:, :, :], tile_ids[:, :, :], eend[0:1, :].unsqueeze(1).to_broadcast([1, RT, E]), ALU.is_ge))
                link(v.tensor_reduce(tile_expert_f[:, :], past[:, :, :], AX.X, ALU.add))
                link(v.tensor_scalar(tile_expert_f[:, :], tile_expert_f[:, :], float(E - 1), None, ALU.min))
                link(v.tensor_copy(tile_expert[:, :], tile_expert_f[:, :]))
                link(v.tensor_tensor(eend[:, :], eend[:, :], etiles[:, :], ALU.subtract))
                link(v.scalar_tensor_tensor(counts[:, :, :], eend[:, :].unsqueeze(2).to_broadcast([P, E, NT]), float(P),
                                            counts[:, :, :], ALU.mult, ALU.add))
                link(v.tensor_tensor(work[:, :, :], psum[:, 0, 0:NT * E].rearrange("p (t e) -> p t e", e=E),
                                     counts[:, :, :].rearrange("p e t -> p t e"), ALU.add))
                for k in range(TOPK):
                    link(v.tensor_tensor(pick[k][:, :, :], pick[k][:, :, :], work[:, :, :], ALU.mult))
                    link(v.tensor_reduce(slot_f[k][:, :], pick[k][:, :, :], AX.X, ALU.add))
                    last = v.tensor_copy(slot[k][:, :], slot_f[k][:, :])
                    link(last)
                dve.sem_inc(slots_ready, 1)

            places(scan_part, item)

            for j in range(RT + 1):
                if j < RT:
                    dve.wait_ge(rsilu_ready, j + 1)
                    dve.wait_ge(up_done, 2 * j + 2)
                    if j >= 2:
                        dve.wait_ge(rgt_full, j - 1)
                    v.tensor_tensor(rgate[:, j % 2, :], rsilu[:, j % 2, :], psum[:, 3 + j % 2, :], ALU.mult).then_inc(rgate_ready, 1)
                    dve.wait_ge(rgt_full, j + 1)
                    if j >= 2:
                        dve.wait_ge(down_done, j - 1)
                    v.tensor_copy(rgT[:, j % 2, :, :].rearrange("p c t -> p (c t)"), psum[:, 5 + j % 2, :]).then_inc(rgT_ready, 1)

            for t in range(NT):
                n, _ = tile_rows(t % TILES)
                dve.wait_ge(back_in[t % 4], 16 * TOPK * (t // 4 + 1))
                link(v.scalar_tensor_tensor(h_all[0:n, t, :], back[0:n, t % 4, 0, :], gate[0][0:n, t:t + 1], h_all[0:n, t, :],
                                            ALU.mult, ALU.add))
                v.scalar_tensor_tensor(h_all[0:n, t, :], back[0:n, t % 4, 1, :], gate[1][0:n, t:t + 1], h_all[0:n, t, :],
                                       ALU.mult, ALU.add).then_inc(result_ready, 1)


def position_table():
    f = np.float32
    y, x = np.meshgrid(np.arange(HP), np.arange(HP), indexing="ij")
    omega = np.arange(D // 4, dtype=f) / f(D // 4 - 1)
    omega = f(1.0) / np.power(f(10000.0), omega)
    y = y.reshape(-1)[:, None].astype(f) * omega[None, :]
    x = x.reshape(-1)[:, None].astype(f) * omega[None, :]
    return np.concatenate((np.sin(x), np.cos(x), np.sin(y), np.cos(y)), axis=1).astype(f)


def constants():
    f = np.float32
    c = {"ident": np.eye(P, dtype=f)}
    c["before_me"] = np.triu(np.ones((P, P), f), 1)
    c["pos"] = np.concatenate([position_table()] * 2)
    shift = np.zeros((2 * NPATCH, 2, NIMG), f)
    for m in range(2):
        for r in range(NPATCH):
            shift[m * NPATCH + r, m, r + 1] = 1
    c["shift"] = shift
    put = np.zeros((2, NIMG), f)
    put[:, 0] = 1
    c["cls_put"] = put
    sel = np.zeros((96, 4, P), f)
    red = np.zeros((P, 4, 32), f)
    for i in range(4):
        for m in range(P):
            r = m % R
            for q in range(3):
                sel[32 * q + R * i + r, i, m] = 1
            red[m, i, R * i + r] = 1
    c["sel"], c["red"] = sel, red
    valid = np.ones((P, NT), f)
    valid[NIMG:, ::TILES] = 0
    c["valid"] = valid
    c["desc"] = np.ascontiguousarray(np.broadcast_to(np.arange(E, 0, -1, dtype=f), (P, NT, E)))
    c["tile_marks"] = np.ascontiguousarray(np.broadcast_to(P * np.arange(CT, dtype=f), (P, E, CT)))
    c["tile_ids"] = np.ascontiguousarray(np.broadcast_to(np.arange(RT, dtype=f)[None, :, None], (1, RT, E)))
    keep = np.ones((P, E, NT), f)
    keep[:, :, 0] = 0
    c["keep"] = keep
    return c


def layout(x, x_txt, **w):
    t = {k.split("_", 2)[2] if k.startswith("L0_") else k: np.asarray(v) for k, v in w.items()}
    x = np.asarray(x)
    a = {}
    a["patches"] = x.reshape(B, CH, HP, PATCH, HP, PATCH).transpose(0, 2, 4, 3, 5, 1).reshape(B * NPATCH, PDIM)
    a["ids"] = np.asarray(x_txt).reshape(B * KT, P).T
    a["cls"] = np.concatenate([t["cls_token"].reshape(1, D), t["cls_pos_embedding"].reshape(1, D)])
    for n in ("ln1_g", "ln1_b"):
        a[n] = t[n].reshape(PC, P).T
    a["W"] = t["W"]
    a["tok_bias"] = t["bias"].reshape(1, D)
    a["ln2_g"], a["ln2_b"] = t["ln2_g"].reshape(1, D), t["ln2_b"].reshape(1, D)
    for n in ("t0", "t1", "t2"):
        a[n] = t[n]
    rest = np.concatenate([t["w1_txt"], t["w2_txt"], np.zeros((P - DIMS[1] - DIMS[2], D), np.float32)])
    a["w_emb"] = np.stack([t["w0_txt"][:P], t["w0_txt"][P:], rest], axis=1)
    al = t["A_log"].reshape(DH, 4, 4, R, N)
    a["a_log"] = al.transpose(4, 3, 0, 2, 1).reshape(P, GROUPS)
    a["w_delta"] = t["W_delta"].T.reshape(KD, P, D).transpose(1, 0, 2)
    bc = np.stack([t["W_B"], t["W_C"]]).transpose(2, 0, 1).reshape(KD, P, 2, N)
    a["w_bc"] = np.repeat(bc.transpose(1, 0, 2, 3), R, axis=3)
    a["b_delta"] = t["b_delta"].reshape(DH, P).T
    a["d_par"] = t["D_param"].reshape(DH, P).T
    a["router"] = t["router_w"].T.reshape(KD, P, E).transpose(1, 0, 2)
    a["ebias"] = t["expert_bias"].reshape(1, E)
    for n in ("w1", "w3", "sw1", "sw3"):
        v = t[n]
        a[n] = v.transpose(2, 0, 1).reshape(KD, P, v.shape[0], HID).transpose(1, 0, 2, 3)
    for n in ("w2", "sw2"):
        v = t[n]
        a[n] = v.transpose(2, 0, 1).reshape(KH, P, v.shape[0], D).transpose(1, 0, 2, 3)
    return a


def kernel(**inputs):
    import numpy as _np
    import concourse.bacc as _bacc
    from concourse import mybir as _mybir
    from concourse.bass_utils import run_bass_kernel_spmd as _run

    named = {}
    for k, v in inputs.items():
        if k in ("L0_txt_w0", "L0_txt_w1", "L0_txt_w2"):
            k += "_txt"
        named[k] = v
    arrays = {k: _np.ascontiguousarray(v) for k, v in {**layout(**named), **constants()}.items()}
    nc = _bacc.Bacc("TRN2", target_bir_lowering=False, num_devices=1)
    feed, a = {}, {}
    for name, v in arrays.items():
        feed[f"in_{name}"] = v
        a[name] = nc.dram_tensor(f"in_{name}", v.shape, _mybir.dt.from_np(v.dtype), kind="ExternalInput").ap()
    a["out"] = nc.dram_tensor("out", (B, L, D), FP32, kind="ExternalOutput").ap()
    embed_scan_moe(nc, a)
    r = _run(nc, [feed], core_ids=[0])
    return r.results[0]["out"]
```

```python
import math
from contextlib import ExitStack

import numpy as np

import concourse.bass as bass
from concourse import mybir

FP32 = mybir.dt.float32
BF16 = mybir.dt.bfloat16
I32 = mybir.dt.int32
U32 = mybir.dt.uint32
ALU = mybir.AluOpType
ACT = mybir.ActivationFunctionType
AX = mybir.AxisListType

P = 128
B = 4
IMG, CH, PATCH = 96, 3, 16
HP = IMG // PATCH
NPATCH = HP * HP
PDIM = CH * PATCH * PATCH
PC = PDIM // P
D = 256
DH = D // P
TXT = 512
KT = TXT // P
NIMG = NPATCH + 1
L = NIMG + TXT
TILES = KT + 1
NT = B * TILES
N = 16
R = P // N
GROUPS = D // R
LC = (L + 1) // 2
LP = 2 * LC
HID = 512
E = 8
NSH = 2
TOPK = 2
KD = D // P
KH = HID // P
CUTS = (0, 5000, 15000, 25000)
DIMS = (256, 64, 16)
DR = D + 2
SPARE = P
ECOLS = sum(DIMS)
NOWHERE = 100000.0
EPS = 1e-5
WC = L // 3
NWC = 3
DOWN_END = 12
UPS = 2
NG = B * GROUPS
TOKENS = B * L
RT = (TOPK * TOKENS + E * (P - 1)) // P
CT = (TOKENS + P - 1) // P
SLOTS = 8


def tile_rows(k):
    return (NIMG, 0) if k == 0 else (P, NIMG + (k - 1) * P)


def schedule():
    def gather(b):
        return [("gather", b, k) for k in range(KT)]

    def embed(b):
        out = [("etrans", b, 0)]
        for k in range(KT):
            out += [("etrans", b, k + 1)] * (k + 1 < KT) + [("embed", b, k)]
        return out + [("place", b)]

    def xtrans(b):
        return [("xtrans", b, k) for k in range(TILES)]

    def zproj(b):
        return [("zproj", b, h, c) for h in range(DH) for c in range(2)]

    def bcproj(b):
        return [("bcproj", b, w, c) for w in range(2) for c in range(2)]

    def ytrans(b):
        return [("ytrans", b, k) for k in range(TILES)]

    def second(b):
        return [("x2trans", b, k) for k in range(TILES)] + [("scores", b, 0), ("scores", b, 1), ("logits", b)]

    def hidden(b):
        return [("hidden", b, j, c) for j in range(NSH * KH) for c in range(NWC)]

    def down(b):
        return [("down", b, k) for k in range(TILES)]

    def image(m):
        return [(x, m) for x in ("image", "imtrans", "immul", "image2")]

    def half(b, h):
        return [("delta", b, h), ("part1", b, h, 0), ("part2", b, h, 0), ("dx", b, h), ("part1", b, h, 1), ("part2", b, h, 1)]

    z, q = zproj(0), [half(0, h) for h in range(DH)]
    g, im, em = gather(0), image(0), embed(0)
    before = (g[:2] + im[:1] + g[2:] + em[:2] + im[1:2] + em[2:3] + im[2:3] + em[3:-1] + im[3:] + em[-1:]
              + [("stats1", 0), ("norm1", 0)] + xtrans(0)
              + z[:2] + [("abs", 0, 0), ("exp", 0, 0)] + z[2:] + [("abs", 0, 1), ("exp", 0, 1), ("log", 0, 0), ("log", 0, 1)]
              + q[0][:2] + bcproj(0) + q[0][2:] + q[1] + gather(1))
    beside = [[] for _ in range(NG + 8)]

    def spread(items, first, last):
        for n, x in enumerate(items):
            beside[first + n * (last - first) // len(items)].append(x)

    spread(image(1), 24, 31)
    spread(embed(1), 0, 4)
    for b in range(B):
        o = b * GROUPS
        if b > 1:
            spread(down(b - 2), o, o + DOWN_END)
        if b:
            spread(ytrans(b - 1), o + 4, o + 7)
            beside[o + 7].append(("stats2", b - 1))
            beside[o + 8].append(("norm2", b - 1))
            spread(second(b - 1), o + 10, o + 13)
        if b + 1 < B:
            n = b + 1
            beside[o + 4].append(("stats1", n))
            beside[o + 5].append(("norm1", n))
            spread(xtrans(n), o + 6, o + 9)
            spread(zproj(n), o + 9, o + 13)
            spread([("abs", n, 0), ("exp", n, 0), ("abs", n, 1), ("exp", n, 1)], o + 11, o + 15)
            beside[o + 15] += [("log", n, 0), ("log", n, 1)]
            spread(bcproj(n), o + 13, o + 18)
            spread(half(n, 0), o + 16, o + 21)
            spread(half(n, 1), o + 21, o + 26)
        if b:
            spread(hidden(b - 1), o + 13, o + 31)
        if b + 2 < B:
            spread(gather(b + 2), o + 10, o + 15)
            spread(embed(b + 2), o + 20, o + 31)
    d = down(B - 2)
    s = second(B - 1)
    after = (ytrans(B - 1) + [("stats2", B - 1)] + d[:1] + [("norm2", B - 1)] + d[1:3] + s[:TILES] + d[3:4] + s[TILES:-1]
             + d[4:] + s[-1:] + [("route",)] + hidden(B - 1) + down(B - 1))
    return before, beside, after


USES_BANK = ("imtrans", "immul", "etrans", "embed", "place", "xtrans", "zproj", "bcproj", "ytrans",
             "x2trans", "scores", "logits", "hidden", "down")


def embed_scan_moe(nc, a):
    before, beside, after = schedule()
    order = {}
    for x in before + [y for p in beside for y in p] + after:
        if x[0] in USES_BANK:
            order[x] = len(order)
    norms = {}
    for x in before + [y for p in beside for y in p] + after:
        if x[0] in ("image", "immul", "stats1", "stats2"):
            norms[x] = len(norms) + 1

    def bank_of(x):
        return order[x] % 2

    def turn_of(x):
        return order[x] // 2 + 1

    ctx = ExitStack()
    with ctx:
        def sem(name):
            return ctx.enter_context(nc.semaphore(name))

        def sb(name, shape, dt=FP32, where=ctx):
            return where.enter_context(nc.sbuf_tensor(name, shape, dt))

        h_all = sb("h_all", [P, NT, D])
        x2_all = sb("x2_all", [P, NT, DR])
        where = sb("where", [P, NT + 1])
        ident = sb("ident", [P, P])
        ones = sb("ones", [P, P])
        before_me = sb("before_me", [P, P])
        router = sb("router", [P, KD, E])
        ebias = sb("ebias", [E, 1])
        logit = sb("logit", [P, NT, E])
        valid = sb("valid", [P, NT])
        desc = sb("desc", [P, NT, E])
        tile_marks = sb("tile_marks", [P, E, CT])
        tile_ids = sb("tile_ids", [1, RT, E])
        keep = sb("keep", [P, E, NT])
        pick = [sb(f"pick{k}", [P, NT, E]) for k in range(TOPK)]
        work = sb("work", [P, NT, E])
        both = sb("both", [P, NT, E])
        counts = sb("counts", [P, E, NT])
        upto = sb("upto", [P, E, NT])
        over = sb("over", [P, E, CT])
        etiles = sb("etiles", [P, E])
        eend = sb("eend", [P, E])
        past = sb("past", [1, RT, E])
        tile_expert_f = sb("tile_expert_f", [1, RT])
        tile_expert = sb("tile_expert", [1, RT], I32)
        top = [sb(f"top{k}", [P, NT]) for k in range(TOPK)]
        first_of = sb("first_of", [P, NT])
        slot_f = [sb(f"slot_f{k}", [P, NT]) for k in range(TOPK)]
        slot = [sb(f"slot{k}", [P, NT], I32) for k in range(TOPK)]
        gate = [sb(f"gate{k}", [P, NT]) for k in range(TOPK)]
        stat = sb("stat", [P, 6, 6])
        mv = sb("mv", [P, TILES, 2])
        var_eps = sb("var_eps", [P, TILES])
        rstd = sb("rstd", [P, TILES])
        minus_half = sb("minus_half", [P, TILES])

        shared_mem = ExitStack()
        w1s = sb("w1s", [P, KD, NSH, HID], where=shared_mem)
        w3s = sb("w3s", [P, KD, NSH, HID], where=shared_mem)
        w2s = sb("w2s", [P, KH, NSH, D], where=shared_mem)
        gated = sb("gated", [P, NSH * KH, L], where=shared_mem)
        x2T = sb("x2T", [P, KD, L], where=shared_mem)
        up_h = sb("up_h", [P, UPS, 2, WC], where=shared_mem)
        tanh_h = sb("tanh_h", [P, UPS, WC], where=shared_mem)
        silu_h = sb("silu_h", [P, 2, WC], where=shared_mem)
        flat = gated[:, :, :].rearrange("p a b -> p (a b)")
        pair = 2 * NPATCH
        patches = flat[0:pair, 0:2 * PDIM].rearrange("p (m c) -> p m c", m=2)
        w_tok = flat[:, 2 * PDIM:2 * PDIM + PC * D].rearrange("p (c d) -> p c d", c=PC)
        pT = flat[:, 2 * PDIM + PC * D:2 * PDIM + PC * D + 2 * PC * pair].rearrange("p (m c t) -> p m c t", m=2, c=PC)

        scan_mem = ExitStack()
        parts = sb("parts", [P, 2, 3, DH, LP], BF16, scan_mem)
        stack = sb("stack", [96, 2, 2 * 4, LP], BF16, scan_mem)
        xT = sb("xT", [P, 2, DH, LP], where=scan_mem)
        zed = sb("zed", [P, DH, LP], where=scan_mem)
        aux = sb("aux", [P, DH, LP], where=scan_mem)
        Bn = sb("Bn", [P, 2, LP], where=scan_mem)
        Cn = sb("Cn", [P, 2, LP], where=scan_mem)
        decay = sb("decay", [P, 2, LP], where=scan_mem)
        ring = sb("ring", [P, SLOTS, LP], where=scan_mem)
        rows = sb("rows", [P, KT * ECOLS], where=scan_mem)
        erow = rows[:, :].rearrange("p (k c) -> p k c", k=KT)
        xn = rows[:, 0:TILES * D].rearrange("p (k c) -> p k c", k=TILES)
        eT = sb("eT", [P, 2, 3, P], where=scan_mem)
        yT = sb("yT", [P, DH, LP], where=scan_mem)
        scoreT = yT[0:E, 0, :]
        w_emb = sb("w_emb", [P, 3, D], where=scan_mem)
        w_delta = sb("w_delta", [P, KD, D], where=scan_mem)
        w_bc = sb("w_bc", [P, KD, 2, P], where=scan_mem)
        b_delta = sb("b_delta", [P, DH], where=scan_mem)
        d_par = sb("d_par", [P, DH], where=scan_mem)
        a_neg = sb("a_neg", [P, GROUPS], where=scan_mem)
        sel_f = ring[0:96, 0, 0:4 * P].rearrange("p (i m) -> p i m", i=4)
        sel = sb("sel", [96, 4, P], BF16, scan_mem)
        red = sb("red", [P, 4, 32], where=scan_mem)
        ids = sb("ids", [P, B * KT], I32, scan_mem)
        ids_f = sb("ids_f", [P, B * KT], where=scan_mem)
        inside = sb("inside", [P, 3, B * KT], where=scan_mem)
        local_f = sb("local_f", [P, 3, B * KT], where=scan_mem)
        local = sb("local", [P, 3, B * KT], I32, scan_mem)
        g1 = sb("g1", [P, PC], where=scan_mem)
        b1 = sb("b1", [P, PC], where=scan_mem)
        tok_bias = sb("tok_bias", [1, D], where=scan_mem)
        g2, b2, pos = (x2_all[0:pair, NT - 1 - i, 0:D] for i in range(3))
        shift = sb("shift", [pair, 2, NIMG], where=scan_mem)
        cls = sb("cls", [2, D], where=scan_mem)
        cls_put = sb("cls_put", [2, NIMG], where=scan_mem)
        himg = x2_all[0:pair, NT - 5:NT - 3, 0:D]
        istat = sb("istat", [pair, 2, 6], where=scan_mem)
        imv = sb("imv", [pair, 2], where=scan_mem)
        scan_mem.close()
        shared_mem.close()

        route_mem = ExitStack()
        ctx.enter_context(route_mem)
        xg = sb("xg", [P, 2, DR], where=route_mem)
        xgT = sb("xgT", [P, 2, KD, P], where=route_mem)
        rsilu = sb("rsilu", [P, 2, HID], where=route_mem)
        rgate = sb("rgate", [P, 2, HID], where=route_mem)
        rgT = sb("rgT", [P, 2, KH, P], where=route_mem)
        ry = sb("ry", [P, 2, D], where=route_mem)
        aim = sb("aim", [P, RT], I32, route_mem)
        share = sb("share", [P, RT], where=route_mem)
        used = (2 * DR + 2 * KD * P + 6 * HID + 2 * D + 2 * RT)
        shared_size = KD * NSH * HID * 2 + KH * NSH * D + NSH * KH * L + KD * L + (2 + 3 * UPS) * WC
        sb("filler", [P, shared_size - used + 64], where=route_mem)
        w1r = sb("w1r", [P, KD, E, HID], where=route_mem)
        w3r = sb("w3r", [P, KD, E, HID], where=route_mem)
        w2r = sb("w2r", [P, KH, E, D], where=route_mem)

        sorted_x = nc.dram_tensor("sorted_x", (RT * P, DR), FP32).ap()

        psum = ctx.enter_context(nc.psum_tensor("psum", [P, 8, 512], FP32))
        p_delta = psum[:, 0:2, 0:LC]
        p_dx = psum[:, 2:4, 0:LC]
        p_y = psum[:, 4:6, 0:LC]
        fill = [psum[:, 6, :], psum[:, 7, :]]

        ids_in = sem("ids_in")
        image_in = sem("image_in")
        ident_in = sem("ident_in")
        embed_in = sem("embed_in")
        const_in = sem("const_in")
        shared_in = sem("shared_in")
        routed_in = sem("routed_in")
        rows_in = [sem(f"rows_in{k}") for k in range(KT)]
        stack_in = [sem(f"stack_in{h}") for h in range(DH)]
        zero_out = sem("zero_out")
        bank_full = [sem("bank_full0"), sem("bank_full1")]
        bank_free = [sem("bank_free0"), sem("bank_free1")]
        zeroed = sem("zeroed")
        local_ready = sem("local_ready")
        rows_zero = sem("rows_zero")
        marked = sem("marked")
        patch_ready = sem("patch_ready")
        pT_ready = sem("pT_ready")
        himg_ready = sem("himg_ready")
        xn_ready = sem("xn_ready")
        log_ready = sem("log_ready")
        delta_ready = sem("delta_ready")
        dx_ready = sem("dx_ready")
        part1 = sem("part1")
        rest1 = sem("rest1")
        part2 = sem("part2")
        part3 = sem("part3")
        sel_ready = sem("sel_ready")
        a_ready = sem("a_ready")
        spread_delta = sem("spread_delta")
        spread_dx = sem("spread_dx")
        decay_ready = sem("decay_ready")
        bx_ready = sem("bx_ready")
        state_ready = sem("state_ready")
        abs_ready = sem("abs_ready")
        exp_ready = sem("exp_ready")
        silu_ready = sem("silu_ready")
        hc_ready = sem("hc_ready")
        summed = sem("summed")
        y_ready = sem("y_ready")
        x2_ready = sem("x2_ready")
        gated_ready = sem("gated_ready")
        var_ready = sem("var_ready")
        rstd_ready = sem("rstd_ready")
        dve_done = sem("dve_done")
        act_done = sem("act_done")
        both_ready = sem("both_ready")
        rank_ready = sem("rank_ready")
        gap_ready = sem("gap_ready")
        gap_exp = sem("gap_exp")
        slots_ready = sem("slots_ready")
        scattered = sem("scattered")
        xg_in = [sem("xg_in0"), sem("xg_in1")]
        xgt_full = sem("xgt_full")
        xgT_ready = sem("xgT_ready")
        up_done = sem("up_done")
        rsilu_ready = sem("rsilu_ready")
        rgate_ready = sem("rgate_ready")
        rgt_full = sem("rgt_full")
        rgT_ready = sem("rgT_ready")
        down_done = sem("down_done")
        ry_ready = sem("ry_ready")
        y_out = sem("y_out")
        h_out = sem("h_out")
        aim_ready = sem("aim_ready")
        gates_in = sem("gates_in")

        block = ctx.enter_context(nc.Block())

        def taken(eng, x):
            eng.wait_ge(bank_free[bank_of(x)], turn_of(x))

        def all_taken(eng, *last):
            for x in last:
                taken(eng, x)

        def read_by_pe(eng, *last):
            for x in last:
                eng.wait_ge(bank_full[bank_of(x)], turn_of(x))

        def places(visit_scan, visit, visit_end=None):
            for x in before:
                visit(x)
            for G, items in enumerate(beside):
                visit_scan(G)
                for x in items:
                    visit(x)
                if visit_end:
                    visit_end(G)
            for x in after:
                visit(x)

        def part_no(x):
            return (x[1] * DH + x[2]) * 2 + x[3]

        def remainder(eng, unit, x):
            _, b, h, v = x
            n = part_no(x) + 1
            if x[0] == "part1":
                eng.wait_ge(part1, n)
                unit.tensor_tensor(aux[:, h, :], zed[:, h, :], parts[:, v, 0, h, :], ALU.subtract).then_inc(rest1, 1)
            else:
                eng.wait_ge(rest1, n)
                eng.wait_ge(part2, n)
                unit.tensor_tensor(parts[:, v, 2, h, :], aux[:, h, :], parts[:, v, 1, h, :], ALU.subtract).then_inc(part3, 1)

        def group(G):
            b, g = divmod(G, GROUPS)
            h, g = divmod(g, GROUPS // DH)
            i, j = divmod(g, 4)
            return b, h, i, j

        IMAGE_LOADS, CONST_LOADS = 4, 19
        RESTACKS = 3 * 4

        @block.sync
        def _(sp):
            def restack(b):
                for h in range(DH):
                    sp.wait_ge(part3, 2 * (b * DH + h + 1))
                    if b:
                        sp.wait_ge(spread_delta, (b - 1) * GROUPS + (h + 1) * GROUPS // DH)
                    for q in range(3):
                        for j in range(4):
                            sp.dma_start(stack[32 * q:32 * q + 32, :, 4 * h + j, :],
                                         parts[32 * j:32 * j + 32, :, q, h, :]).then_inc(stack_in[h], 16)

            sp.dma_start(ids[:, :], a["ids"]).then_inc(ids_in, 16)
            sp.dma_start(ident[:, :], a["ident"]).then_inc(ident_in, 16)
            sp.dma_start(patches, a["patches"].rearrange("(m p) c -> p m c", m=2)).then_inc(image_in, 16)
            sp.dma_start(w_emb[:, :, :], a["w_emb"]).then_inc(embed_in, 16)
            sp.dma_start(g1[:, :], a["ln1_g"]).then_inc(image_in, 16)
            sp.dma_start(b1[:, :], a["ln1_b"]).then_inc(image_in, 16)
            sp.dma_start(w_tok, a["W"].rearrange("(c p) d -> p c d", p=P)).then_inc(image_in, 16)
            for dst, src in ((tok_bias[:, :], a["tok_bias"]),
                             (g2, a["ln2_g"].to_broadcast([pair, D])),
                             (b2, a["ln2_b"].to_broadcast([pair, D])),
                             (pos, a["pos"]), (shift[:, :, :], a["shift"]),
                             (cls[:, :], a["cls"]), (cls_put[:, :], a["cls_put"]),
                             (w_delta[:, :, :], a["w_delta"]), (w_bc[:, :, :, :], a["w_bc"]),
                             (b_delta[:, :], a["b_delta"]), (d_par[:, :], a["d_par"]),
                             (a_neg[:, :], a["a_log"]), (sel_f, a["sel"]), (red[:, :, :], a["red"]),
                             (router[:, :, :], a["router"]), (ebias[:, :], a["ebias"]),
                             (before_me[:, :], a["before_me"]), (valid[:, :], a["valid"]),
                             (desc[:, :, :], a["desc"])):
                sp.dma_start(dst, src).then_inc(const_in, 16)
            restack(0)
            for dst, src in ((w1s, a["sw1"]), (w3s, a["sw3"]), (w2s, a["sw2"]),
                             (tile_marks, a["tile_marks"]), (tile_ids, a["tile_ids"]), (keep, a["keep"]), (where, a["where"])):
                sp.dma_start(dst[tuple([slice(None)] * len(dst.shape))], src).then_inc(shared_in, 16)
            sp.wait_ge(marked, 1)
            sp.dma_start(sorted_x.rearrange("(j p) d -> p j d", p=P),
                         x2_all[:, 0, :].unsqueeze(1).to_broadcast([P, RT, DR])).then_inc(zero_out, 16)
            sp.dma_start(a["out"][TOKENS:TOKENS + SPARE, :], x2_all[:, 0, 0:D]).then_inc(zero_out, 16)

            def store(b):
                all_taken(sp, ("down", b, TILES - 2), ("down", b, TILES - 1))
                o = b * L
                sp.dma_start(a["out"][o:o + NIMG, :], h_all[0:NIMG, b * TILES, :]).then_inc(h_out, 16)
                sp.dma_start(a["out"][o + NIMG:o + L, :].rearrange("(k p) d -> p k d", p=P),
                             h_all[:, b * TILES + 1:(b + 1) * TILES, :]).then_inc(h_out, 16)

            for b in range(1, B):
                restack(b)
                if b >= 2:
                    store(b - 2)
            sp.wait_ge(x2_ready, B)
            all_taken(sp, ("ytrans", B - 1, TILES - 2), ("ytrans", B - 1, TILES - 1))
            sp.wait_ge(summed, NG // 4)
            for w, src in ((w1r, a["w1"]), (w3r, a["w3"]), (w2r, a["w2"])):
                if w is w2r:
                    taken(sp, ("logits", B - 1))
                for e in range(E):
                    sp.dma_start(w[:, :, e, :], src[:, :, e, :]).then_inc(routed_in, 16)
            store(B - 2)
            store(B - 1)
            sp.wait_ge(scattered, 16 * TOPK * NT)
            for j in range(RT):
                if j >= 2:
                    sp.wait_ge(xgt_full, j - 1)
                    sp.wait_ge(aim_ready, j - 1)
                sp.dma_start(xg[:, j % 2, :], sorted_x[j * P:(j + 1) * P, :]).then_inc(xg_in[j % 2], 16)

        @block.gpsimd
        def _(pool):
            nc.gpsimd.memset(minus_half[:, :], -0.5)
            nc.gpsimd.memset(rows[:, :], 0.0).then_inc(rows_zero, 1)
            pool.wait_ge(rows_zero, 1)

            def scan_part(G):
                if G == 6:
                    pool.wait_ge(shared_in, 16 * 7)
                    pool.wait_ge(zeroed, 1)
                    nc.gpsimd.tensor_copy(x2_all[:, 0, D:D + 1], where[:, NT:NT + 1]).then_inc(marked, 1)

            def put(j):
                pool.wait_ge(ry_ready, j + 1)
                pool.wait_ge(aim_ready, j + 1)
                if j:
                    pool.wait_ge(y_out, 16 * j)
                pool.indirect_dma_start(
                    a["out"], bass.IndirectOffsetOnAxis(ap=aim[:, j:j + 1], axis=0), ry[:, j % 2, :], None,
                    bounds_check=TOKENS + SPARE - 1, compute_op=ALU.add).then_inc(y_out, 16)

            def item(x):
                if x in norms:
                    rows_, cols_ = (pair, 1) if x[0] in ("image", "immul") else (P, TILES)
                    pool.wait_ge(var_ready, norms[x])
                    nc.gpsimd.tensor_tensor(rstd[0:rows_, 0:cols_], var_eps[0:rows_, 0:cols_],
                                            minus_half[0:rows_, 0:cols_], ALU.pow).then_inc(rstd_ready, 1)
                elif x[0] == "gather":
                    b, k = x[1:]
                    if b and k == 0:
                        read_by_pe(pool, ("xtrans", b - 1, TILES - 2), ("xtrans", b - 1, TILES - 1))
                        nc.gpsimd.memset(rows[:, :], 0.0).then_inc(rows_zero, 1)
                        pool.wait_ge(rows_zero, b + 1)
                    if b == 0 and k == 0:
                        pool.wait_ge(local_ready, 1)
                    c0 = 0
                    for t in range(3):
                        pool.indirect_dma_start(
                            erow[:, k, c0:c0 + DIMS[t]], None, a[f"t{t}"],
                            bass.IndirectOffsetOnAxis(ap=local[:, t, b * KT + k:b * KT + k + 1], axis=0),
                            bounds_check=CUTS[t + 1] - CUTS[t] - 1, oob_is_err=False).then_inc(rows_in[k], 16)
                        c0 += DIMS[t]
                elif x[0] in ("part1", "part2") and x[1]:
                    remainder(pool, nc.gpsimd, x)

            places(scan_part, item)
            pool.wait_ge(slots_ready, 1)
            pool.wait_ge(zero_out, 32)
            for k in range(TOPK):
                if k:
                    pool.wait_ge(scattered, 16 * NT)
                    nc.gpsimd.tensor_copy(x2_all[:, :, D + 1], gate[k][:, :]).then_inc(gates_in, 1)
                pool.wait_ge(gates_in, k + 1)
                for t in range(NT):
                    n, _ = tile_rows(t % TILES)
                    pool.indirect_dma_start(
                        sorted_x, bass.IndirectOffsetOnAxis(ap=slot[k][0:n, t:t + 1], axis=0),
                        x2_all[0:n, t, :], None).then_inc(scattered, 16)
            pool.wait_ge(h_out, 16 * 2 * B)
            for j in range(RT):
                pool.wait_ge(xg_in[j % 2], 16 * (j // 2 + 1))
                nc.gpsimd.tensor_copy(share[:, j:j + 1], xg[:, j % 2, D + 1:DR])
                nc.gpsimd.tensor_copy(aim[:, j:j + 1], xg[:, j % 2, D:D + 1]).then_inc(aim_ready, 1)
                if j:
                    put(j - 1)
            put(RT - 1)
            pool.wait_ge(y_out, 16 * RT)

        @block.tensor
        def _(pe):
            def enter(x):
                n = order[x]
                if n >= 2:
                    pe.wait_ge(bank_free[n % 2], n // 2)
                return fill[n % 2]

            def leave(x, ins):
                ins.then_inc(bank_full[bank_of(x)], 1)

            def scan_part(G):
                if G < NG:
                    b, h, i, j = group(G)
                    if G % (GROUPS // DH) == 0:
                        pe.wait_ge(stack_in[h], 16 * RESTACKS * (b + 1))
                    if G == 0:
                        pe.wait_ge(sel_ready, 1)
                    if G:
                        pe.wait_ge(bx_ready, G)
                    for c in range(2):
                        last = nc.tensor.matmul(p_dx[:, c, :], sel[:, i, :], stack[:, 1, 4 * h + j, c * LC:(c + 1) * LC],
                                                start=True, stop=True)
                    last.then_inc(spread_dx, 1)
                    if G:
                        pe.wait_ge(decay_ready, G)
                    for c in range(2):
                        last = nc.tensor.matmul(p_delta[:, c, :], sel[:, i, :], stack[:, 0, 4 * h + j, c * LC:(c + 1) * LC],
                                                start=True, stop=True)
                    last.then_inc(spread_delta, 1)

            def scan_sums(G):
                if 6 <= G < NG + 4 and G % 4 == 2:
                    q = G // 4 - 1
                    b, h, i, _ = group(4 * q)
                    pe.wait_ge(hc_ready, 4 * q + 4)
                    if i == 0 and q:
                        pe.wait_ge(y_ready, q // 4)
                    for c in range(2):
                        for j in range(4):
                            last = nc.tensor.matmul(p_y[32 * j:32 * j + 32, c, :], red[:, i, :],
                                                    ring[:, (4 * q + j) % SLOTS, c * LC:(c + 1) * LC],
                                                    start=(i == 0), stop=(i == 3), tile_position=(0, 32 * j))
                    last.then_inc(summed, 1)

            def item(x):
                kind = x[0]
                if kind == "imtrans":
                    m = x[1]
                    f = enter(x)
                    pe.wait_ge(patch_ready, m + 1)
                    for c in range(PC):
                        last = nc.tensor.transpose(f[:, c * pair:(c + 1) * pair], patches[:, m, c * P:(c + 1) * P],
                                                   ident[0:pair, 0:pair])
                    leave(x, last)
                elif kind == "immul":
                    m = x[1]
                    f = enter(x)
                    pe.wait_ge(pT_ready, m + 1)
                    pe.wait_ge(image_in, 16 * IMAGE_LOADS)
                    pe.wait_ge(const_in, 16 * CONST_LOADS)
                    for c in range(PC):
                        nc.tensor.matmul(f[0:pair, 0:D], pT[:, m, c, :], w_tok[:, c, :], start=(c == 0), stop=False)
                    leave(x, nc.tensor.matmul(f[0:pair, 0:D], ones[0:1, 0:pair], tok_bias[:, :], start=False, stop=True))
                elif kind == "etrans":
                    b, k = x[1:]
                    f = enter(x)
                    pe.wait_ge(rows_in[k], 16 * 3 * (b + 1))
                    nc.tensor.transpose(f[:, 0:P], erow[:, k, 0:P], ident[:, :])
                    nc.tensor.transpose(f[:, P:2 * P], erow[:, k, P:2 * P], ident[:, :])
                    leave(x, nc.tensor.transpose(f[0:ECOLS - D, 2 * P:3 * P], erow[:, k, D:ECOLS], ident[:, :]))
                elif kind == "embed":
                    b, k = x[1:]
                    f = enter(x)
                    taken(pe, ("etrans", b, k))
                    if b == 0 and k == 0:
                        pe.wait_ge(embed_in, 16)
                    nc.tensor.matmul(f[:, 0:D], eT[:, k % 2, 0, :], w_emb[:, 0, :], start=True, stop=False)
                    nc.tensor.matmul(f[:, 0:D], eT[:, k % 2, 1, :], w_emb[:, 1, :], start=False, stop=False)
                    leave(x, nc.tensor.matmul(f[:, 0:D], eT[0:ECOLS - D, k % 2, 2, :], w_emb[0:ECOLS - D, 2, :],
                                              start=False, stop=True))
                elif kind == "place":
                    b = x[1]
                    f = enter(x)
                    pe.wait_ge(himg_ready, b // 2 + 1)
                    nc.tensor.matmul(f[0:NIMG, 0:D], shift[:, b % 2, :], himg[:, b // 2, :], start=True, stop=False)
                    leave(x, nc.tensor.matmul(f[0:NIMG, 0:D], cls_put[:, :], cls[:, :], start=False, stop=True))
                elif kind == "xtrans":
                    b, k = x[1:]
                    n, _ = tile_rows(k)
                    f = enter(x)
                    pe.wait_ge(xn_ready, b + 1)
                    for h in range(DH):
                        last = nc.tensor.transpose(f[:, h * P:h * P + n], xn[0:n, k, h * P:(h + 1) * P], ident[0:n, 0:n])
                    leave(x, last)
                elif kind == "zproj":
                    b, h, c = x[1:]
                    f = enter(x)
                    all_taken(pe, ("xtrans", b, TILES - 2), ("xtrans", b, TILES - 1))
                    for k in range(KD):
                        last = nc.tensor.matmul(f[:, 0:LC], w_delta[:, k, h * P:(h + 1) * P],
                                                xT[:, b % 2, k, c * LC:(c + 1) * LC], start=(k == 0), stop=(k == KD - 1))
                    leave(x, last)
                elif kind == "bcproj":
                    b, w, c = x[1:]
                    f = enter(x)
                    for k in range(KD):
                        last = nc.tensor.matmul(f[:, 0:LC], w_bc[:, k, w, :],
                                                xT[:, b % 2, k, c * LC:(c + 1) * LC], start=(k == 0), stop=(k == KD - 1))
                    leave(x, last)
                elif kind == "ytrans":
                    b, k = x[1:]
                    n, c0 = tile_rows(k)
                    f = enter(x)
                    pe.wait_ge(y_ready, DH * (b + 1))
                    for h in range(DH):
                        last = nc.tensor.transpose(f[0:n, h * P:(h + 1) * P], yT[:, h, c0:c0 + n], ident[:, :])
                    leave(x, last)
                elif kind == "x2trans":
                    b, k = x[1:]
                    n, _ = tile_rows(k)
                    f = enter(x)
                    pe.wait_ge(x2_ready, b + 1)
                    for h in range(DH):
                        last = nc.tensor.transpose(f[:, h * P:h * P + n], x2_all[0:n, b * TILES + k, h * P:(h + 1) * P],
                                                   ident[0:n, 0:n])
                    leave(x, last)
                elif kind == "scores":
                    b, c = x[1:]
                    w = (LC, L - LC)[c]
                    f = enter(x)
                    all_taken(pe, ("x2trans", b, TILES - 2), ("x2trans", b, TILES - 1))
                    for h in range(KD):
                        last = nc.tensor.matmul(f[0:E, 0:w], router[:, h, :], x2T[:, h, c * LC:c * LC + w],
                                                start=(h == 0), stop=(h == KD - 1))
                    leave(x, last)
                elif kind == "logits":
                    b = x[1]
                    f = enter(x)
                    all_taken(pe, ("scores", b, 0), ("scores", b, 1))
                    for k in range(TILES):
                        n, c0 = tile_rows(k)
                        last = nc.tensor.transpose(f[0:n, k * E:(k + 1) * E], scoreT[:, c0:c0 + n], ident[0:E, 0:E])
                    leave(x, last)
                elif kind == "hidden":
                    b, j, c = x[1:]
                    e, m = divmod(j, KH)
                    f = enter(x)
                    if b == 0 and j == 0 and c == 0:
                        pe.wait_ge(shared_in, 16 * 7)
                    for w, o in ((w1s, 0), (w3s, WC)):
                        for k in range(KD):
                            last = nc.tensor.matmul(f[:, o:o + WC], w[:, k, e, m * P:(m + 1) * P],
                                                    x2T[:, k, c * WC:(c + 1) * WC], start=(k == 0), stop=(k == KD - 1))
                    leave(x, last)
                elif kind == "down":
                    b, k = x[1:]
                    n, c0 = tile_rows(k)
                    f = enter(x)
                    pe.wait_ge(gated_ready, NSH * KH * NWC * (b + 1))
                    for j in range(NSH * KH):
                        e, m = divmod(j, KH)
                        last = nc.tensor.matmul(f[0:n, 0:D], gated[:, j, c0:c0 + n], w2s[:, m, e, :],
                                                start=(j == 0), stop=(j == NSH * KH - 1))
                    leave(x, last)
                elif kind == "route":
                    pe.wait_ge(both_ready, 1)
                    m = both[:, :, :].rearrange("p t e -> p (t e)")
                    nc.tensor.matmul(psum[:, 0, 0:NT * E], before_me[:, :], m, start=True, stop=True)
                    nc.tensor.matmul(psum[:, 1, 0:NT * E], ones[:, :], m, start=True, stop=True).then_inc(rank_ready, 1)

            pe.wait_ge(ident_in, 16)
            places(scan_part, item, scan_sums)

            def xtrans(j):
                pe.wait_ge(xg_in[j % 2], 16 * (j // 2 + 1))
                if j:
                    pe.wait_ge(xgT_ready, j)
                for h in range(KD):
                    last = nc.tensor.transpose(psum[:, 0, h * P:(h + 1) * P], xg[:, j % 2, h * P:(h + 1) * P], ident[:, :])
                last.then_inc(xgt_full, 1)

            def up(j):
                pe.wait_ge(xgT_ready, j + 1)
                if j >= 2:
                    pe.wait_ge(rgate_ready, j - 1)
                ex = pe.value_load(tile_expert[0:1, j:j + 1], min_val=0, max_val=E - 1)
                for w, bank in ((w1r, 1 + j % 2), (w3r, 3 + j % 2)):
                    for k in range(KD):
                        last = nc.tensor.matmul(psum[:, bank, :], xgT[:, j % 2, k, :],
                                                w[:, k, bass.ds(ex, 1), :], start=(k == 0), stop=(k == KD - 1))
                    last.then_inc(up_done, 1)

            def gtrans(j):
                pe.wait_ge(rgate_ready, j + 1)
                if j >= 2:
                    pe.wait_ge(rgT_ready, j - 1)
                for m in range(KH):
                    last = nc.tensor.transpose(psum[:, 5 + j % 2, m * P:(m + 1) * P], rgate[:, j % 2, m * P:(m + 1) * P],
                                               ident[:, :])
                last.then_inc(rgt_full, 1)

            def down(j):
                pe.wait_ge(rgT_ready, j + 1)
                if j:
                    pe.wait_ge(ry_ready, j)
                ex = pe.value_load(tile_expert[0:1, j:j + 1], min_val=0, max_val=E - 1)
                for m in range(KH):
                    last = nc.tensor.matmul(psum[:, 7, 0:D], rgT[:, j % 2, m, :], w2r[:, m, bass.ds(ex, 1), :],
                                            start=(m == 0), stop=(m == KH - 1))
                last.then_inc(down_done, 1)

            pe.wait_ge(routed_in, 16 * 3 * E)
            pe.wait_ge(slots_ready, 1)
            xtrans(0)
            for j in range(RT):
                up(j)
                if j + 1 < RT:
                    xtrans(j + 1)
                if j:
                    down(j - 1)
                gtrans(j)
            down(RT - 1)

        @block.scalar
        def _(act):
            steps = [0]

            def link(ins):
                steps[0] += 1
                ins.then_inc(act_done, 1)
                act.wait_ge(act_done, steps[0])

            def full(x):
                act.wait_ge(bank_full[bank_of(x)], turn_of(x))
                return fill[bank_of(x)]

            def scan_part(G):
                if G < NG:
                    b, h, i, j = group(G)
                    act.wait_ge(spread_delta, G + 1)
                    if G >= 2:
                        act.wait_ge(state_ready, G - 1)
                    nc.scalar.activation(decay[:, G % 2, :].rearrange("p (c t) -> p c t", c=2), p_delta, ACT.Exp,
                                         scale=a_neg[:, G % GROUPS:G % GROUPS + 1]).then_inc(decay_ready, 1)

            def item(x):
                kind = x[0]
                if kind == "etrans":
                    b, k = x[1:]
                    f = full(x)
                    if k >= 2:
                        read_by_pe(act, ("embed", b, k - 2))
                    nc.scalar.copy(eT[:, k % 2, 0:2, :].rearrange("p c t -> p (c t)"), f[:, 0:2 * P])
                    nc.scalar.copy(eT[0:ECOLS - D, k % 2, 2, :], f[0:ECOLS - D, 2 * P:3 * P]).then_inc(bank_free[bank_of(x)], 1)
                elif kind in ("embed", "place"):
                    b = x[1]
                    k = 1 + x[2] if kind == "embed" else 0
                    n, _ = tile_rows(k)
                    f = full(x)
                    act.wait_ge(zeroed, 1)
                    nc.scalar.copy(h_all[0:n, b * TILES + k, :], f[0:n, 0:D]).then_inc(bank_free[bank_of(x)], 1)
                elif kind == "xtrans":
                    b, k = x[1:]
                    n, c0 = tile_rows(k)
                    f = full(x)
                    if b >= 2 and k == 0:
                        act.wait_ge(y_ready, DH * (b - 1))
                        act.wait_ge(dx_ready, DH * (b - 1))
                    nc.scalar.copy(xT[:, b % 2, :, c0:c0 + n],
                                   f[:, 0:2 * P].rearrange("p (h t) -> p h t", h=2)[:, :, 0:n]).then_inc(bank_free[bank_of(x)], 1)
                elif kind == "zproj":
                    b, h, c = x[1:]
                    if b == 0 and h == 0 and c == 0:
                        act.wait_ge(const_in, 16 * CONST_LOADS)
                        nc.scalar.activation(sel[:, :, :], sel_f, ACT.Copy).then_inc(sel_ready, 1)
                        link(nc.scalar.activation(a_neg[:, :], a_neg[:, :], ACT.Exp))
                        link(nc.scalar.mul(a_neg[:, :], a_neg[:, :], -1.0))
                    f = full(x)
                    if b and c == 0:
                        act.wait_ge(part3, 2 * ((b - 1) * DH + h + 1))
                    nc.scalar.activation(zed[:, h, c * LC:(c + 1) * LC], f[:, 0:LC], ACT.Identity,
                                         bias=b_delta[:, h:h + 1]).then_inc(bank_free[bank_of(x)], 1)
                elif kind == "abs":
                    b, h = x[1:]
                    all_taken(act, ("zproj", b, h, 0), ("zproj", b, h, 1))
                    nc.scalar.activation(aux[:, h, :], zed[:, h, :], ACT.Abs).then_inc(abs_ready, 1)
                elif kind == "exp":
                    b, h = x[1:]
                    act.wait_ge(abs_ready, b * DH + h + 1)
                    nc.scalar.activation(aux[:, h, :], aux[:, h, :], ACT.Exp, scale=-1.0).then_inc(exp_ready, 1)
                elif kind == "log":
                    b, h = x[1:]
                    act.wait_ge(exp_ready, b * DH + h + 1)
                    nc.scalar.activation(aux[:, h, :], aux[:, h, :], ACT.Ln, bias=1.0).then_inc(log_ready, 1)
                elif kind == "bcproj":
                    b, w, c = x[1:]
                    f = full(x)
                    if b >= 2:
                        act.wait_ge(hc_ready, (b - 1) * GROUPS)
                    nc.scalar.copy((Bn, Cn)[w][:, b % 2, c * LC:(c + 1) * LC], f[:, 0:LC]).then_inc(bank_free[bank_of(x)], 1)
                elif kind == "part1":
                    b, h, v = x[1:]
                    act.wait_ge((delta_ready, dx_ready)[v], b * DH + h + 1)
                    if b and v == 0:
                        act.wait_ge(stack_in[h], 16 * RESTACKS * b)
                    nc.scalar.copy(parts[:, v, 0, h, :], zed[:, h, :]).then_inc(part1, 1)
                elif kind == "part2":
                    b, h, v = x[1:]
                    act.wait_ge(rest1, part_no(x) + 1)
                    nc.scalar.copy(parts[:, v, 1, h, :], aux[:, h, :]).then_inc(part2, 1)
                elif kind == "x2trans":
                    b, k = x[1:]
                    n, c0 = tile_rows(k)
                    f = full(x)
                    if b and k == 0:
                        read_by_pe(act, ("hidden", b - 1, NSH * KH - 1, NWC - 2), ("hidden", b - 1, NSH * KH - 1, NWC - 1))
                    nc.scalar.copy(x2T[:, :, c0:c0 + n],
                                   f[:, 0:2 * P].rearrange("p (h t) -> p h t", h=2)[:, :, 0:n]).then_inc(bank_free[bank_of(x)], 1)
                elif kind == "scores":
                    b, c = x[1:]
                    w = (LC, L - LC)[c]
                    f = full(x)
                    if c == 0:
                        all_taken(act, ("ytrans", b, TILES - 2), ("ytrans", b, TILES - 1))
                    nc.scalar.activation(scoreT[:, c * LC:c * LC + w], f[0:E, 0:w], ACT.Identity,
                                         bias=ebias[:, :]).then_inc(bank_free[bank_of(x)], 1)
                elif kind == "logits":
                    b = x[1]
                    f = full(x)
                    act.wait_ge(zeroed, 1)
                    nc.scalar.copy(logit[0:NIMG, b * TILES, :], f[0:NIMG, 0:E])
                    nc.scalar.copy(logit[:, b * TILES + 1:(b + 1) * TILES, :],
                                   f[:, E:TILES * E].rearrange("p (k e) -> p k e", e=E)).then_inc(bank_free[bank_of(x)], 1)
                elif kind == "hidden":
                    b, j, c = x[1:]
                    f = full(x)
                    n = (b * NSH * KH + j) * NWC + c
                    if n >= UPS:
                        act.wait_ge(gated_ready, n - UPS + 1)
                    nc.scalar.activation(tanh_h[:, n % UPS, :], f[:, 0:WC], ACT.Tanh, scale=0.5)
                    nc.scalar.copy(up_h[:, n % UPS, :, :].rearrange("p a c -> p (a c)"), f[:, 0:2 * WC]).then_inc(bank_free[bank_of(x)], 1)
                elif kind == "route":
                    act.wait_ge(gap_ready, 1)
                    nc.scalar.activation(gate[1][:, :], gate[1][:, :], ACT.Exp).then_inc(gap_exp, 1)

            places(scan_part, item)

            def gated_out(y):
                act.wait_ge(aim_ready, y + 1)
                if y >= 2:
                    act.wait_ge(y_out, 16 * (y - 1))
                nc.scalar.activation(ry[:, y % 2, :], psum[:, 7, 0:D], ACT.Identity,
                                     scale=share[:, y:y + 1]).then_inc(ry_ready, 1)

            for j in range(RT + 1):
                if j < RT:
                    act.wait_ge(xgt_full, j + 1)
                    if j >= 2:
                        act.wait_ge(up_done, 2 * (j - 1))
                    nc.scalar.copy(xgT[:, j % 2, :, :].rearrange("p c t -> p (c t)"), psum[:, 0, 0:D]).then_inc(xgT_ready, 1)
                if j >= 1:
                    if j >= 2:
                        y = j - 2
                        act.wait_ge(down_done, y + 1)
                        gated_out(y)
                if j < RT:
                    act.wait_ge(up_done, 2 * j + 1)
                    if j >= 2:
                        act.wait_ge(rgate_ready, j - 1)
                    nc.scalar.activation(rsilu[:, j % 2, :], psum[:, 1 + j % 2, :], ACT.Silu).then_inc(rsilu_ready, 1)
            y = RT - 1
            act.wait_ge(down_done, y + 1)
            gated_out(y)

        @block.vector
        def _(dve):
            steps = [0]

            def link(ins):
                steps[0] += 1
                ins.then_inc(dve_done, 1)
                dve.wait_ge(dve_done, steps[0])

            def full(x):
                dve.wait_ge(bank_full[bank_of(x)], turn_of(x))
                return fill[bank_of(x)]

            v = nc.vector
            dve.wait_ge(ids_in, 16)
            link(v.tensor_copy(ids_f[:, :], ids[:, :]))
            for t in range(3):
                lo, hi = CUTS[t], CUTS[t + 1]
                link(v.tensor_scalar(inside[:, t, :], ids_f[:, :], float(lo), None, ALU.is_ge))
                link(v.scalar_tensor_tensor(inside[:, t, :], ids_f[:, :], float(hi), inside[:, t, :], ALU.is_lt, ALU.mult))
                link(v.scalar_tensor_tensor(local_f[:, t, :], ids_f[:, :], float(lo) + NOWHERE, inside[:, t, :],
                                            ALU.subtract, ALU.mult))
                link(v.tensor_scalar(local_f[:, t, :], local_f[:, t, :], NOWHERE, None, ALU.add))
            v.tensor_copy(local[:, :, :], local_f[:, :, :]).then_inc(local_ready, 1)
            for b in range(B):
                v.memset(h_all[:, b * TILES, :], 0.0)
            v.memset(x2_all[:, 0, :], 0.0)
            v.memset(logit[:, :, :], 0.0)
            v.memset(ones[:, :], 1.0)
            v.memset(xT[:, :, :, L:LP], 0.0).then_inc(zeroed, 1)

            def scan_part(G):
                if G < NG:
                    b, h, i, j = group(G)
                    if G % GROUPS == 0:
                        all_taken(dve, ("bcproj", b, 1, 0), ("bcproj", b, 1, 1))
                    dve.wait_ge(spread_dx, G + 1)
                    if G >= SLOTS:
                        dve.wait_ge(summed, (G - SLOTS) // 4 + 1)
                    v.tensor_tensor(ring[:, G % SLOTS, :].rearrange("p (c t) -> p c t", c=2), p_dx,
                                    Bn[:, b % 2, :].rearrange("p (c t) -> p c t", c=2), ALU.mult).then_inc(bx_ready, 1)
                if 1 <= G <= NG:
                    s = G - 1
                    dve.wait_ge(decay_ready, s + 1)
                    dve.wait_ge(bx_ready, s + 1)
                    r = ring[:, s % SLOTS, :]
                    v.tensor_tensor_scan(r, decay[:, s % 2, :], r, 0.0, ALU.mult, ALU.add).then_inc(state_ready, 1)
                if 2 <= G <= NG + 1:
                    s = G - 2
                    dve.wait_ge(state_ready, s + 1)
                    r = ring[:, s % SLOTS, :]
                    v.tensor_tensor(r, r, Cn[:, (s // GROUPS) % 2, :], ALU.mult).then_inc(hc_ready, 1)
                if G >= 19 and (G - 19) % 16 == 0:
                    n = (G - 19) // 16
                    b, h = divmod(n, DH)
                    dve.wait_ge(summed, 4 * (n + 1))
                    if b:
                        read_by_pe(dve, ("ytrans", b - 1, TILES - 2), ("ytrans", b - 1, TILES - 1), ("logits", b - 1))
                    v.scalar_tensor_tensor(yT[:, h, :].rearrange("p (c t) -> p c t", c=2),
                                           xT[:, b % 2, h, :].rearrange("p (c t) -> p c t", c=2), d_par[:, h:h + 1], p_y,
                                           ALU.mult, ALU.add).then_inc(y_ready, 1)

            def stats(src):
                for k in range(TILES):
                    last = v.bn_stats(stat[:, k, :], src[:, k, :])
                link(last)
                for k in range(TILES):
                    last = v.bn_aggr(mv[:, k, :], stat[:, k, :])
                link(last)
                v.tensor_scalar(var_eps[:, :], mv[:, :, 1], EPS, None, ALU.add).then_inc(var_ready, 1)

            def norm(dst, src, turn):
                dve.wait_ge(rstd_ready, turn)
                for k in range(TILES):
                    last = v.tensor_scalar(dst[:, k, :], src[:, k, :], mv[:, k, 0:1], rstd[:, k:k + 1],
                                           ALU.subtract, ALU.mult)
                return last

            def item(x):
                kind = x[0]
                if kind == "image":
                    m = x[1]
                    if m == 0:
                        dve.wait_ge(image_in, 16 * IMAGE_LOADS)
                    half = PDIM // 2
                    v.bn_stats(istat[:, 0, :], patches[:, m, 0:half])
                    link(v.bn_stats(istat[:, 1, :], patches[:, m, half:PDIM]))
                    link(v.bn_aggr(imv[:, :], istat[:, :, :].rearrange("p a b -> p (a b)")))
                    v.tensor_scalar(var_eps[0:pair, 0:1], imv[:, 1:2], EPS, None, ALU.add).then_inc(var_ready, 1)
                    dve.wait_ge(rstd_ready, norms[x])
                    v.tensor_scalar(patches[:, m, :], patches[:, m, :], imv[:, 0:1], rstd[0:pair, 0:1],
                                    ALU.subtract, ALU.mult).then_inc(patch_ready, 1)
                elif kind == "imtrans":
                    m = x[1]
                    f = full(x)
                    src = f[:, 0:PC * pair].rearrange("p (c t) -> p c t", c=PC)
                    v.tensor_tensor(pT[:, m, :, :], src, g1[:, :].unsqueeze(2).to_broadcast([P, PC, pair]),
                                    ALU.mult).then_inc(bank_free[bank_of(x)], 1)
                    taken(dve, x)
                    v.tensor_tensor(pT[:, m, :, :], pT[:, m, :, :], b1[:, :].unsqueeze(2).to_broadcast([P, PC, pair]),
                                    ALU.add).then_inc(pT_ready, 1)
                elif kind == "immul":
                    m = x[1]
                    f = full(x)
                    link(v.bn_stats(istat[:, 0, :], f[0:pair, 0:D]))
                    link(v.bn_aggr(imv[:, :], istat[:, 0, :]))
                    v.tensor_scalar(var_eps[0:pair, 0:1], imv[:, 1:2], EPS, None, ALU.add).then_inc(var_ready, 1)
                    dve.wait_ge(rstd_ready, norms[x])
                    v.tensor_scalar(himg[:, m, :], f[0:pair, 0:D], imv[:, 0:1], rstd[0:pair, 0:1],
                                    ALU.subtract, ALU.mult).then_inc(bank_free[bank_of(x)], 1)
                elif kind == "image2":
                    m = x[1]
                    taken(dve, ("immul", m))
                    dve.wait_ge(const_in, 16 * CONST_LOADS)
                    link(v.tensor_tensor(himg[:, m, :], himg[:, m, :], g2, ALU.mult))
                    link(v.tensor_tensor(himg[:, m, :], himg[:, m, :], b2, ALU.add))
                    v.tensor_tensor(himg[:, m, :], himg[:, m, :], pos, ALU.add).then_inc(himg_ready, 1)
                elif kind == "stats1":
                    b = x[1]
                    all_taken(dve, ("embed", b, KT - 1), ("place", b))
                    stats(h_all[:, b * TILES:(b + 1) * TILES, :])
                elif kind == "norm1":
                    b = x[1]
                    norm(xn, h_all[:, b * TILES:(b + 1) * TILES, :], norms[("stats1", b)]).then_inc(xn_ready, 1)
                elif kind == "delta":
                    b, h = x[1:]
                    dve.wait_ge(log_ready, b * DH + h + 1)
                    v.scalar_tensor_tensor(zed[:, h, :], zed[:, h, :], 0.0, aux[:, h, :], ALU.max, ALU.add).then_inc(delta_ready, 1)
                elif kind == "dx":
                    b, h = x[1:]
                    dve.wait_ge(part3, 2 * (b * DH + h) + 1)
                    v.tensor_tensor(zed[:, h, :], zed[:, h, :], xT[:, b % 2, h, :], ALU.mult).then_inc(dx_ready, 1)
                elif kind in ("part1", "part2") and x[1] == 0:
                    remainder(dve, v, x)
                elif kind == "ytrans":
                    b, k = x[1:]
                    n, _ = tile_rows(k)
                    f = full(x)
                    t = b * TILES + k
                    v.tensor_tensor(h_all[0:n, t, :], h_all[0:n, t, :], f[0:n, 0:D], ALU.add).then_inc(bank_free[bank_of(x)], 1)
                elif kind == "stats2":
                    b = x[1]
                    all_taken(dve, ("ytrans", b, TILES - 2), ("ytrans", b, TILES - 1))
                    stats(h_all[:, b * TILES:(b + 1) * TILES, :])
                elif kind == "norm2":
                    b = x[1]
                    if b == 0:
                        dve.wait_ge(zero_out, 32)
                    norm(x2_all[:, b * TILES:(b + 1) * TILES, 0:D],
                         h_all[:, b * TILES:(b + 1) * TILES, :], norms[("stats2", b)]).then_inc(x2_ready, 1)
                elif kind == "hidden":
                    b, j, c = x[1:]
                    taken(dve, x)
                    n = (b * NSH * KH + j) * NWC + c
                    if b and j == 0 and c == 0:
                        read_by_pe(dve, ("down", b - 1, TILES - 2), ("down", b - 1, TILES - 1))
                    v.scalar_tensor_tensor(silu_h[:, n % 2, :], tanh_h[:, n % UPS, :], 1.0, up_h[:, n % UPS, 0, :],
                                           ALU.add, ALU.mult).then_inc(silu_ready, 1)
                    dve.wait_ge(silu_ready, n + 1)
                    v.scalar_tensor_tensor(gated[:, j, c * WC:(c + 1) * WC], up_h[:, n % UPS, 1, :], 0.5, silu_h[:, n % 2, :],
                                           ALU.mult, ALU.mult).then_inc(gated_ready, 1)
                elif kind == "down":
                    b, k = x[1:]
                    n, _ = tile_rows(k)
                    f = full(x)
                    t = b * TILES + k
                    v.tensor_tensor(h_all[0:n, t, :], h_all[0:n, t, :], f[0:n, 0:D], ALU.add).then_inc(bank_free[bank_of(x)], 1)
                elif kind == "route":
                    route()

            def route():
                taken(dve, ("logits", B - 1))
                dve.wait_ge(shared_in, 16 * 7)
                v.tensor_copy(x2_all[:, :, D], where[:, 0:NT])
                src = logit
                for k in range(TOPK):
                    link(v.tensor_reduce(top[k][:, :], src[:, :, :], AX.X, ALU.max))
                    link(v.tensor_tensor(pick[k][:, :, :], src[:, :, :], top[k][:, :].unsqueeze(2).to_broadcast([P, NT, E]),
                                         ALU.is_equal))
                    link(v.tensor_tensor(pick[k][:, :, :], pick[k][:, :, :], desc[:, :, :], ALU.mult))
                    link(v.tensor_reduce(first_of[:, :], pick[k][:, :, :], AX.X, ALU.max))
                    link(v.tensor_tensor(pick[k][:, :, :], desc[:, :, :], first_of[:, :].unsqueeze(2).to_broadcast([P, NT, E]),
                                         ALU.is_equal))
                    if k == 0:
                        link(v.scalar_tensor_tensor(work[:, :, :], pick[0][:, :, :], -3e38, logit[:, :, :], ALU.mult, ALU.add))
                        src = work
                v.tensor_tensor(gate[1][:, :], top[1][:, :], top[0][:, :], ALU.subtract).then_inc(gap_ready, 1)
                link(v.tensor_tensor(both[:, :, :], pick[0][:, :, :], pick[1][:, :, :], ALU.add))
                v.tensor_tensor(both[:, :, :], both[:, :, :], valid[:, :].unsqueeze(2).to_broadcast([P, NT, E]),
                                ALU.mult).then_inc(both_ready, 1)
                dve.wait_ge(gap_exp, 1)
                link(v.tensor_scalar(gate[0][:, :], gate[1][:, :], 1.0, None, ALU.add))
                link(v.reciprocal(gate[0][:, :], gate[0][:, :]))
                link(v.tensor_tensor(gate[1][:, :], gate[1][:, :], gate[0][:, :], ALU.mult))
                v.tensor_copy(x2_all[:, :, D + 1], gate[0][:, :]).then_inc(gates_in, 1)
                dve.wait_ge(rank_ready, 1)
                link(v.tensor_copy(counts[:, :, :], psum[:, 1, 0:NT * E].rearrange("p (t e) -> p e t", e=E)))
                link(v.tensor_tensor_scan(upto[:, :, :].rearrange("p e t -> p (e t)"), keep[:, :, :].rearrange("p e t -> p (e t)"),
                                          counts[:, :, :].rearrange("p e t -> p (e t)"), 0.0, ALU.mult, ALU.add))
                link(v.tensor_tensor(counts[:, :, :], upto[:, :, :], counts[:, :, :], ALU.subtract))
                link(v.tensor_tensor(over[:, :, :], upto[:, :, NT - 1:NT].to_broadcast([P, E, CT]), tile_marks[:, :, :], ALU.is_gt))
                link(v.tensor_reduce(etiles[:, :], over[:, :, :], AX.X, ALU.add))
                link(v.tensor_tensor_scan(eend[:, :], ones[:, 0:E], etiles[:, :], 0.0, ALU.mult, ALU.add))
                link(v.tensor_tensor(past[:, :, :], tile_ids[:, :, :], eend[0:1, :].unsqueeze(1).to_broadcast([1, RT, E]), ALU.is_ge))
                link(v.tensor_reduce(tile_expert_f[:, :], past[:, :, :], AX.X, ALU.add))
                link(v.tensor_scalar(tile_expert_f[:, :], tile_expert_f[:, :], float(E - 1), None, ALU.min))
                link(v.tensor_copy(tile_expert[:, :], tile_expert_f[:, :]))
                link(v.tensor_tensor(eend[:, :], eend[:, :], etiles[:, :], ALU.subtract))
                link(v.scalar_tensor_tensor(counts[:, :, :], eend[:, :].unsqueeze(2).to_broadcast([P, E, NT]), float(P),
                                            counts[:, :, :], ALU.mult, ALU.add))
                link(v.tensor_tensor(work[:, :, :], psum[:, 0, 0:NT * E].rearrange("p (t e) -> p t e", e=E),
                                     counts[:, :, :].rearrange("p e t -> p t e"), ALU.add))
                for k in range(TOPK):
                    link(v.tensor_tensor(pick[k][:, :, :], pick[k][:, :, :], work[:, :, :], ALU.mult))
                    link(v.tensor_reduce(slot_f[k][:, :], pick[k][:, :, :], AX.X, ALU.add))
                    last = v.tensor_copy(slot[k][:, :], slot_f[k][:, :])
                last.then_inc(slots_ready, 1)

            places(scan_part, item)

            for j in range(RT + 1):
                if j < RT:
                    dve.wait_ge(rsilu_ready, j + 1)
                    dve.wait_ge(up_done, 2 * j + 2)
                    if j >= 2:
                        dve.wait_ge(rgt_full, j - 1)
                    v.tensor_tensor(rgate[:, j % 2, :], rsilu[:, j % 2, :], psum[:, 3 + j % 2, :], ALU.mult).then_inc(rgate_ready, 1)
                    dve.wait_ge(rgt_full, j + 1)
                    if j >= 2:
                        dve.wait_ge(down_done, j - 1)
                    v.tensor_copy(rgT[:, j % 2, :, :].rearrange("p c t -> p (c t)"), psum[:, 5 + j % 2, :]).then_inc(rgT_ready, 1)


def position_table():
    f = np.float32
    y, x = np.meshgrid(np.arange(HP), np.arange(HP), indexing="ij")
    omega = np.arange(D // 4, dtype=f) / f(D // 4 - 1)
    omega = f(1.0) / np.power(f(10000.0), omega)
    y = y.reshape(-1)[:, None].astype(f) * omega[None, :]
    x = x.reshape(-1)[:, None].astype(f) * omega[None, :]
    return np.concatenate((np.sin(x), np.cos(x), np.sin(y), np.cos(y)), axis=1).astype(f)


def constants():
    f = np.float32
    c = {"ident": np.eye(P, dtype=f)}
    c["before_me"] = np.triu(np.ones((P, P), f), 1)
    c["pos"] = np.concatenate([position_table()] * 2)
    shift = np.zeros((2 * NPATCH, 2, NIMG), f)
    for m in range(2):
        for r in range(NPATCH):
            shift[m * NPATCH + r, m, r + 1] = 1
    c["shift"] = shift
    put = np.zeros((2, NIMG), f)
    put[:, 0] = 1
    c["cls_put"] = put
    sel = np.zeros((96, 4, P), f)
    red = np.zeros((P, 4, 32), f)
    for i in range(4):
        for m in range(P):
            r = m % R
            for q in range(3):
                sel[32 * q + R * i + r, i, m] = 1
            red[m, i, R * i + r] = 1
    c["sel"], c["red"] = sel, red
    valid = np.ones((P, NT), f)
    valid[NIMG:, ::TILES] = 0
    c["valid"] = valid
    c["desc"] = np.ascontiguousarray(np.broadcast_to(np.arange(E, 0, -1, dtype=f), (P, NT, E)))
    c["tile_marks"] = np.ascontiguousarray(np.broadcast_to(P * np.arange(CT, dtype=f), (P, E, CT)))
    c["tile_ids"] = np.ascontiguousarray(np.broadcast_to(np.arange(RT, dtype=f)[None, :, None], (1, RT, E)))
    keep = np.ones((P, E, NT), f)
    keep[:, :, 0] = 0
    c["keep"] = keep
    first = [b * L + tile_rows(k)[1] for b in range(B) for k in range(TILES)] + [TOKENS]
    c["where"] = (np.array(first, f)[None, :] + np.arange(P, dtype=f)[:, None]).astype(f)
    return c


def layout(x, x_txt, **w):
    t = {k.split("_", 2)[2] if k.startswith("L0_") else k: np.asarray(v) for k, v in w.items()}
    x = np.asarray(x)
    a = {}
    a["patches"] = x.reshape(B, CH, HP, PATCH, HP, PATCH).transpose(0, 2, 4, 3, 5, 1).reshape(B * NPATCH, PDIM)
    a["ids"] = np.asarray(x_txt).reshape(B * KT, P).T
    a["cls"] = np.concatenate([t["cls_token"].reshape(1, D), t["cls_pos_embedding"].reshape(1, D)])
    for n in ("ln1_g", "ln1_b"):
        a[n] = t[n].reshape(PC, P).T
    a["W"] = t["W"]
    a["tok_bias"] = t["bias"].reshape(1, D)
    a["ln2_g"], a["ln2_b"] = t["ln2_g"].reshape(1, D), t["ln2_b"].reshape(1, D)
    for n in ("t0", "t1", "t2"):
        a[n] = t[n]
    rest = np.concatenate([t["w1_txt"], t["w2_txt"], np.zeros((P - DIMS[1] - DIMS[2], D), np.float32)])
    a["w_emb"] = np.stack([t["w0_txt"][:P], t["w0_txt"][P:], rest], axis=1)
    al = t["A_log"].reshape(DH, 4, 4, R, N)
    a["a_log"] = al.transpose(4, 3, 0, 2, 1).reshape(P, GROUPS)
    a["w_delta"] = t["W_delta"].T.reshape(KD, P, D).transpose(1, 0, 2)
    bc = np.stack([t["W_B"], t["W_C"]]).transpose(2, 0, 1).reshape(KD, P, 2, N)
    a["w_bc"] = np.repeat(bc.transpose(1, 0, 2, 3), R, axis=3)
    a["b_delta"] = t["b_delta"].reshape(DH, P).T
    a["d_par"] = t["D_param"].reshape(DH, P).T
    a["router"] = t["router_w"].T.reshape(KD, P, E).transpose(1, 0, 2)
    a["ebias"] = t["expert_bias"].reshape(E, 1)
    for n in ("w1", "w3", "sw1", "sw3"):
        v = t[n]
        a[n] = v.transpose(2, 0, 1).reshape(KD, P, v.shape[0], HID).transpose(1, 0, 2, 3)
    for n in ("w2", "sw2"):
        v = t[n]
        a[n] = v.transpose(2, 0, 1).reshape(KH, P, v.shape[0], D).transpose(1, 0, 2, 3)
    return a


def kernel(**inputs):
    import numpy as _np
    import concourse.bacc as _bacc
    from concourse import mybir as _mybir
    from concourse.bass_utils import run_bass_kernel_spmd as _run

    named = {}
    for k, v in inputs.items():
        if k in ("L0_txt_w0", "L0_txt_w1", "L0_txt_w2"):
            k += "_txt"
        named[k] = v
    arrays = {k: _np.ascontiguousarray(v) for k, v in {**layout(**named), **constants()}.items()}
    nc = _bacc.Bacc("TRN2", target_bir_lowering=False, num_devices=1)
    feed, a = {}, {}
    for name, v in arrays.items():
        feed[f"in_{name}"] = v
        a[name] = nc.dram_tensor(f"in_{name}", v.shape, _mybir.dt.from_np(v.dtype), kind="ExternalInput").ap()
    a["out"] = nc.dram_tensor("out", (TOKENS + SPARE, D), FP32, kind="ExternalOutput").ap()
    embed_scan_moe(nc, a)
    r = _run(nc, [feed], core_ids=[0])
    return r.results[0]["out"][:TOKENS].reshape(B, L, D)
```

```python
from contextlib import ExitStack

import numpy as np

import concourse.bass as bass
from concourse import mybir

FP32 = mybir.dt.float32
BF16 = mybir.dt.bfloat16
I32 = mybir.dt.int32
ALU = mybir.AluOpType
ACT = mybir.ActivationFunctionType
AX = mybir.AxisListType

P = 128
B = 4
IMG, CH, PATCH = 96, 3, 16
HP = IMG // PATCH
NPATCH = HP * HP
PDIM = CH * PATCH * PATCH
PC = PDIM // P
D = 256
DH = D // P
TXT = 512
KT = TXT // P
NIMG = NPATCH + 1
L = NIMG + TXT
TILES = KT + 1
NT = B * TILES
N = 16
R = P // N
GROUPS = D // R
LC = (L + 1) // 2
LP = 2 * LC
HID = 512
E = 8
NSH = 2
TOPK = 2
KD = D // P
KH = HID // P
CUTS = (0, 5000, 15000, 25000)
DIMS = (256, 64, 16)
DR = D + 2
SPARE = P
ECOLS = sum(DIMS)
NOWHERE = 100000.0
EPS = 1e-5
WC = L // 3
NWC = 3
UPS = 2
NG = B * GROUPS
TOKENS = B * L
RT = (TOPK * TOKENS + E * (P - 1)) // P
RMIN = (TOPK * TOKENS + P - 1) // P
CT = (TOKENS + P - 1) // P
SLOTS = 8

BEFORE = [("gather", 2), ("image", 1), ("gather", 2), ("embed", 2), ("image", 1), ("embed", 3), ("image", 1),
          ("embed", 3), ("image", 1), ("embed", 1), ("norm1", 2), ("xtrans", 5), ("zproj", 1), ("bcproj", 1),
          ("zproj", 1), ("softplus", 1), ("half0", 1), ("softplus", 2), ("zproj", 2), ("half0", 2),
          ("bcproj", 1), ("half0", 1), ("bcproj", 1), ("half0", 1), ("bcproj", 1), ("half0", 1),
          ("gather_second", 4)]
AFTER = [("ytrans", 5), ("norm2", 1), ("down", 1), ("norm2", 1), ("down", 1), ("second", 8), ("route", 1),
         ("down", 2), ("route", 1), ("down", 1), ("hidden", 24), ("down_last", 5)]
PLANS = [
    {"first_half1": (0, 10), "norm1": (11, 13), "image": (20, 32), "xtrans": (13, 17), "embed": (21, 33),
     "zproj": (16, 20), "softplus": (18, 22), "bcproj": (20, 27), "half0": (20, 26), "embed_second": (2, 10),
     "half1": (26, 31), "gather": (17, 26)},
    {"ytrans": (5, 6), "second": (9, 13), "half1": (20, 29), "xtrans": (6, 9), "embed": (19, 33),
     "bcproj": (14, 19), "gather": (9, 18), "zproj": (8, 14), "softplus": (13, 15), "norm1": (4, 5),
     "half0": (15, 21), "norm2": (6, 11), "hidden": (13, 31)},
    {"down": (0, 11), "ytrans": (4, 6), "half1": (21, 31), "norm1": (4, 6), "xtrans": (6, 7), "zproj": (8, 14),
     "softplus": (12, 15), "bcproj": (14, 18), "half0": (16, 21), "norm2": (5, 9), "second": (9, 14),
     "hidden": (15, 31)},
    {"down": (0, 11), "ytrans": (4, 6), "second": (9, 14), "norm2": (5, 9), "hidden": (14, 35)},
]


def tile_rows(k):
    return (NIMG, 0) if k == 0 else (P, NIMG + (k - 1) * P)


def schedule():
    def gather(b):
        return [("gather", b, k) for k in range(KT)]

    def embed(b):
        out = [("etrans", b, 0)]
        for k in range(KT):
            out += [("etrans", b, k + 1)] * (k + 1 < KT) + [("embed", b, k)]
        return out + [("place", b)]

    def xtrans(b):
        return [("xtrans", b, k) for k in range(TILES)]

    def zproj(b):
        return [("zproj", b, h, c) for h in range(DH) for c in range(2)]

    def bcproj(b):
        return [("bcproj", b, w, c) for w in range(2) for c in range(2)]

    def ytrans(b):
        return [("ytrans", b, k) for k in range(TILES)]

    def second(b):
        return [("x2trans", b, k) for k in range(TILES)] + [("scores", b, 0), ("scores", b, 1), ("logits", b)]

    def hidden(b):
        return [("hidden", b, j, c) for j in range(NSH * KH) for c in range(NWC)]

    def down(b):
        return [("down", b, k) for k in range(TILES)]

    def image(m):
        return [(x, m) for x in ("image", "imtrans", "immul", "image2")]

    def half(b, h):
        return [("delta", b, h), ("part1", b, h, 0), ("part2", b, h, 0), ("dx", b, h), ("part1", b, h, 1), ("part2", b, h, 1)]

    def softplus(b, h):
        return [("abs", b, h), ("exp", b, h)], [("log", b, h)]

    def take(order, queues):
        out = [queues[name].pop(0) for name, count in order for _ in range(count)]
        assert not any(queues.values())
        return out

    before = take(BEFORE, {
        "gather": gather(0), "image": image(0), "embed": embed(0), "norm1": [("stats1", 0), ("norm1", 0)],
        "xtrans": xtrans(0), "zproj": zproj(0), "softplus": sum(softplus(0, 0), []), "half0": half(0, 0),
        "bcproj": bcproj(0), "gather_second": gather(1)})
    beside = [[] for _ in range(NG + 8)]

    def spread(items, first, last):
        for n, x in enumerate(items):
            beside[first + n * (last - first) // len(items)].append(x)

    def jobs(b):
        out = {}
        if b > 1:
            out["down"] = down(b - 2)
        if b:
            out["ytrans"] = ytrans(b - 1)
            out["norm2"] = [("stats2", b - 1), ("norm2", b - 1)]
            out["second"] = second(b - 1)
            out["hidden"] = hidden(b - 1)
        if b + 1 < B:
            n = b + 1
            out["norm1"] = [("stats1", n), ("norm1", n)]
            out["xtrans"] = xtrans(n)
            out["zproj"] = zproj(n)
            (e0, l0), (e1, l1) = softplus(n, 0), softplus(n, 1)
            out["softplus"] = e0 + e1 + l0 + l1
            out["bcproj"] = bcproj(n)
            out["half0"] = half(n, 0)
            out["half1"] = half(n, 1)
        if b + 2 < B:
            out["gather"] = gather(b + 2)
            out["embed"] = embed(b + 2)
        if b == 0:
            out["first_half1"] = sum(softplus(0, 1), []) + half(0, 1)
            out["image"] = image(1)
            out["embed_second"] = embed(1)
        return out

    for b in range(B):
        todo = jobs(b)
        for name, (first, last) in PLANS[b].items():
            spread(todo.pop(name), b * GROUPS + first, b * GROUPS + last)
        assert not todo
    after = take(AFTER, {
        "ytrans": ytrans(B - 1), "norm2": [("stats2", B - 1), ("norm2", B - 1)], "down": down(B - 2),
        "second": second(B - 1), "route": [("choose",), ("route",)], "hidden": hidden(B - 1), "down_last": down(B - 1)})
    norms = [x for x in before + sum(beside, []) + after if x[0] in ("image", "immul", "stats1", "norm1", "stats2", "norm2")]
    for x, y in zip(norms, norms[1:]):
        assert x[0] not in ("stats1", "stats2") or y == ("norm" + x[0][-1], x[1])
    return before, beside, after


USES_BANK = ("imtrans", "immul", "etrans", "embed", "place", "xtrans", "zproj", "bcproj", "ytrans",
             "x2trans", "scores", "logits", "hidden", "down")


def embed_scan_moe(nc, a):
    before, beside, after = schedule()
    order = {}
    for x in before + [y for p in beside for y in p] + after:
        if x[0] in USES_BANK:
            order[x] = len(order)
    norms = {}
    for x in before + [y for p in beside for y in p] + after:
        if x[0] in ("image", "immul", "stats1", "stats2"):
            norms[x] = len(norms) + 1

    def bank_of(x):
        return order[x] % 2

    def turn_of(x):
        return order[x] // 2 + 1

    ctx = ExitStack()
    with ctx:
        def sem(name):
            return ctx.enter_context(nc.semaphore(name))

        def sb(name, shape, dt=FP32, where=ctx):
            return where.enter_context(nc.sbuf_tensor(name, shape, dt))

        h_all = sb("h_all", [P, NT, D])
        x2_all = sb("x2_all", [P, NT, DR])
        where = sb("where", [P, NT + 1])
        ident = sb("ident", [P, P])
        ones = sb("ones", [P, P])
        before_me = sb("before_me", [P, P])
        router = sb("router", [P, KD, E])
        ebias = sb("ebias", [E, 1])
        logit = sb("logit", [P, NT, E])
        valid = sb("valid", [P, NT])
        desc = sb("desc", [P, NT, E])
        tile_marks = sb("tile_marks", [P, E, CT])
        tile_ids = sb("tile_ids", [1, RT, E])
        keep = sb("keep", [P, E, NT])
        pick = [sb(f"pick{k}", [P, NT, E]) for k in range(TOPK)]
        work = sb("work", [P, NT, E])
        both = sb("both", [P, NT, E])
        counts = sb("counts", [P, E, NT])
        upto = sb("upto", [P, E, NT])
        over = sb("over", [P, E, CT])
        etiles = sb("etiles", [P, E])
        eend = sb("eend", [P, E])
        past = sb("past", [1, RT, E])
        tile_expert_f = sb("tile_expert_f", [1, RT])
        tile_expert = sb("tile_expert", [1, RT], I32)
        tile_count = sb("tile_count", [1, 1], I32)
        top = [sb(f"top{k}", [P, NT]) for k in range(TOPK)]
        first_of = sb("first_of", [P, NT])
        slot_f = [sb(f"slot_f{k}", [P, NT]) for k in range(TOPK)]
        slot = [sb(f"slot{k}", [P, NT], I32) for k in range(TOPK)]
        gate = [sb(f"gate{k}", [P, NT]) for k in range(TOPK)]
        stat = sb("stat", [P, 6, 6])
        mv = sb("mv", [P, TILES, 2])
        var_eps = sb("var_eps", [P, TILES])
        rstd = sb("rstd", [P, TILES])
        minus_half = sb("minus_half", [P, TILES])

        shared_mem = ExitStack()
        w1s = sb("w1s", [P, KD, NSH, HID], where=shared_mem)
        w3s = sb("w3s", [P, KD, NSH, HID], where=shared_mem)
        w2s = sb("w2s", [P, KH, NSH, D], where=shared_mem)
        gated = sb("gated", [P, NSH * KH, L], where=shared_mem)
        x2T = sb("x2T", [P, KD, L], where=shared_mem)
        up_h = sb("up_h", [P, UPS, 2, WC], where=shared_mem)
        tanh_h = sb("tanh_h", [P, UPS, WC], where=shared_mem)
        silu_h = sb("silu_h", [P, 2, WC], where=shared_mem)
        flat = gated[:, :, :].rearrange("p a b -> p (a b)")
        pair = 2 * NPATCH
        patches = flat[0:pair, 0:2 * PDIM].rearrange("p (m c) -> p m c", m=2)
        w_tok = flat[:, 2 * PDIM:2 * PDIM + PC * D].rearrange("p (c d) -> p c d", c=PC)
        pT = flat[:, 2 * PDIM + PC * D:2 * PDIM + PC * D + 2 * PC * pair].rearrange("p (m c t) -> p m c t", m=2, c=PC)

        scan_mem = ExitStack()
        parts = sb("parts", [P, 2, 3, DH, LP], BF16, scan_mem)
        stack = sb("stack", [96, 2, 2 * 4, LP], BF16, scan_mem)
        xT = sb("xT", [P, 2, DH, LP], where=scan_mem)
        zed = sb("zed", [P, DH, LP], where=scan_mem)
        aux = sb("aux", [P, DH, LP], where=scan_mem)
        Bn = sb("Bn", [P, 2, LP], where=scan_mem)
        Cn = sb("Cn", [P, 2, LP], where=scan_mem)
        decay = sb("decay", [P, 2, LP], where=scan_mem)
        ring = sb("ring", [P, SLOTS, LP], where=scan_mem)
        rows = sb("rows", [P, KT * ECOLS], where=scan_mem)
        erow = rows[:, :].rearrange("p (k c) -> p k c", k=KT)
        xn = rows[:, 0:TILES * D].rearrange("p (k c) -> p k c", k=TILES)
        eT = sb("eT", [P, 2, 3, P], where=scan_mem)
        yT = sb("yT", [P, DH, LP], where=scan_mem)
        scoreT = yT[0:E, 0, :]
        w_emb = sb("w_emb", [P, 3, D], where=scan_mem)
        w_delta = sb("w_delta", [P, KD, D], where=scan_mem)
        w_bc = sb("w_bc", [P, KD, 2, P], where=scan_mem)
        b_delta = sb("b_delta", [P, DH], where=scan_mem)
        d_par = sb("d_par", [P, DH], where=scan_mem)
        a_neg = sb("a_neg", [P, GROUPS], where=scan_mem)
        sel_f = ring[0:96, 0, 0:4 * P].rearrange("p (i m) -> p i m", i=4)
        sel = sb("sel", [96, 4, P], BF16, scan_mem)
        red = sb("red", [P, 4, 32], where=scan_mem)
        ids = sb("ids", [P, B * KT], I32, scan_mem)
        ids_f = sb("ids_f", [P, B * KT], where=scan_mem)
        inside = sb("inside", [P, 3, B * KT], where=scan_mem)
        local_f = sb("local_f", [P, 3, B * KT], where=scan_mem)
        local = sb("local", [P, 3, B * KT], I32, scan_mem)
        g1 = sb("g1", [P, PC], where=scan_mem)
        b1 = sb("b1", [P, PC], where=scan_mem)
        tok_bias = sb("tok_bias", [1, D], where=scan_mem)
        g2, b2, pos = (x2_all[0:pair, NT - 1 - i, 0:D] for i in range(3))
        shift = sb("shift", [pair, 2, NIMG], where=scan_mem)
        cls = sb("cls", [2, D], where=scan_mem)
        cls_put = sb("cls_put", [2, NIMG], where=scan_mem)
        himg = x2_all[0:pair, NT - 5:NT - 3, 0:D]
        istat = sb("istat", [pair, 2, 6], where=scan_mem)
        imv = sb("imv", [pair, 2], where=scan_mem)
        scan_mem.close()
        shared_mem.close()

        route_mem = ExitStack()
        ctx.enter_context(route_mem)
        xg = sb("xg", [P, 2, DR], where=route_mem)
        xgT = sb("xgT", [P, 2, KD, P], where=route_mem)
        rsilu = sb("rsilu", [P, 2, HID], where=route_mem)
        rgate = sb("rgate", [P, 2, HID], where=route_mem)
        rgT = sb("rgT", [P, 2, KH, P], where=route_mem)
        ry = sb("ry", [P, 2, D], where=route_mem)
        aim = sb("aim", [P, RT], I32, route_mem)
        share = sb("share", [P, RT], where=route_mem)
        used = (2 * DR + 2 * KD * P + 6 * HID + 2 * D + 2 * RT)
        shared_size = KD * NSH * HID * 2 + KH * NSH * D + NSH * KH * L + KD * L + (2 + 3 * UPS) * WC
        sb("filler", [P, shared_size - used + 64], where=route_mem)
        w1r = sb("w1r", [P, KD, E, HID], where=route_mem)
        w3r = sb("w3r", [P, KD, E, HID], where=route_mem)
        w2r = sb("w2r", [P, KH, E, D], where=route_mem)

        sorted_x = nc.dram_tensor("sorted_x", (RT * P, DR), FP32).ap()

        psum = ctx.enter_context(nc.psum_tensor("psum", [P, 8, 512], FP32))
        p_delta = psum[:, 0:2, 0:LC]
        p_dx = psum[:, 2:4, 0:LC]
        p_y = psum[:, 4:6, 0:LC]
        fill = [psum[:, 6, :], psum[:, 7, :]]

        ids_in = sem("ids_in")
        image_in = sem("image_in")
        ident_in = sem("ident_in")
        embed_in = sem("embed_in")
        const_in = sem("const_in")
        shared_in = sem("shared_in")
        routed_in = sem("routed_in")
        rows_in = [sem(f"rows_in{k}") for k in range(KT)]
        stack_in = [sem(f"stack_in{j}") for j in range(DH * 4)]
        zero_out = sem("zero_out")
        bank_full = [sem("bank_full0"), sem("bank_full1")]
        bank_free = [sem("bank_free0"), sem("bank_free1")]
        zeroed = sem("zeroed")
        local_ready = sem("local_ready")
        rows_zero = sem("rows_zero")
        marked = sem("marked")
        patch_ready = sem("patch_ready")
        pT_ready = sem("pT_ready")
        himg_ready = sem("himg_ready")
        xn_ready = sem("xn_ready")
        log_ready = sem("log_ready")
        delta_ready = sem("delta_ready")
        dx_ready = sem("dx_ready")
        part1 = sem("part1")
        rest1 = sem("rest1")
        part2 = sem("part2")
        part3 = sem("part3")
        sel_ready = sem("sel_ready")
        spread_delta = sem("spread_delta")
        spread_dx = sem("spread_dx")
        decay_ready = sem("decay_ready")
        bx_ready = sem("bx_ready")
        state_ready = sem("state_ready")
        abs_ready = sem("abs_ready")
        exp_ready = sem("exp_ready")
        silu_ready = sem("silu_ready")
        hc_ready = sem("hc_ready")
        summed = sem("summed")
        y_ready = sem("y_ready")
        x2_ready = sem("x2_ready")
        gated_ready = sem("gated_ready")
        var_ready = sem("var_ready")
        rstd_ready = sem("rstd_ready")
        dve_done = sem("dve_done")
        act_done = sem("act_done")
        both_ready = sem("both_ready")
        rank_ready = sem("rank_ready")
        gap_ready = sem("gap_ready")
        gap_exp = sem("gap_exp")
        slots_ready = sem("slots_ready")
        experts_ready = sem("experts_ready")
        scattered = [sem("scattered0"), sem("scattered1")]
        xg_in = [sem("xg_in0"), sem("xg_in1")]
        xgt_full = sem("xgt_full")
        xgT_ready = sem("xgT_ready")
        up_done = sem("up_done")
        rsilu_ready = sem("rsilu_ready")
        rgate_ready = sem("rgate_ready")
        rgt_full = sem("rgt_full")
        rgT_ready = sem("rgT_ready")
        down_done = sem("down_done")
        ry_ready = sem("ry_ready")
        y_out = sem("y_out")
        h_out = sem("h_out")
        aim_ready = sem("aim_ready")
        gates_in = sem("gates_in")

        block = ctx.enter_context(nc.Block())

        def taken(eng, x):
            eng.wait_ge(bank_free[bank_of(x)], turn_of(x))

        def all_taken(eng, *last):
            for x in last:
                taken(eng, x)

        def read_by_pe(eng, *last):
            for x in last:
                eng.wait_ge(bank_full[bank_of(x)], turn_of(x))

        def places(visit, visit_scan=None, visit_end=None):
            for x in before:
                visit(x)
            for G, items in enumerate(beside):
                if visit_scan:
                    visit_scan(G)
                for x in items:
                    visit(x)
                if visit_end:
                    visit_end(G)
            for x in after:
                visit(x)

        def part_no(x):
            return (x[1] * DH + x[2]) * 2 + x[3]

        def remainder(eng, unit, x):
            _, b, h, v = x
            n = part_no(x) + 1
            if x[0] == "part1":
                eng.wait_ge(part1, n)
                unit.tensor_tensor(aux[:, h, :], zed[:, h, :], parts[:, v, 0, h, :], ALU.subtract).then_inc(rest1, 1)
            else:
                eng.wait_ge(rest1, n)
                eng.wait_ge(part2, n)
                unit.tensor_tensor(parts[:, v, 2, h, :], aux[:, h, :], parts[:, v, 1, h, :], ALU.subtract).then_inc(part3, 1)

        def routed_tiles(eng, tile, finish=None):
            for j in range(RMIN):
                tile(j)
            eng.wait_ge(experts_ready, 1)
            filled = eng.value_load(tile_count[0:1, 0:1], min_val=RMIN, max_val=RT)
            for j in range(RMIN, RT + 1):
                if j < RT:
                    with eng.If(filled > j):
                        tile(j)
                if finish:
                    with eng.If(filled == j):
                        finish(j)

        def gate_hidden(eng, unit, x):
            _, b, j, c = x
            n = (b * NSH * KH + j) * NWC + c
            if b and j == 0 and c == 0:
                read_by_pe(eng, ("down", b - 1, TILES - 2), ("down", b - 1, TILES - 1))
            eng.wait_ge(silu_ready, n + 1)
            unit.tensor_tensor(gated[:, j, c * WC:(c + 1) * WC], up_h[:, n % UPS, 1, :], silu_h[:, n % 2, :],
                               ALU.mult).then_inc(gated_ready, 1)

        def group(G):
            b, g = divmod(G, GROUPS)
            h, g = divmod(g, GROUPS // DH)
            i, j = divmod(g, 4)
            return b, h, i, j

        IMAGE_LOADS, CONST_LOADS, SHARED_LOADS = 4, 20, 6
        RESTACKS = 3

        @block.sync
        def _(sp):
            def restack(b):
                for h in range(DH):
                    sp.wait_ge(part3, 2 * (b * DH + h + 1))
                    if b:
                        sp.wait_ge(spread_delta, (b - 1) * GROUPS + (h + 1) * GROUPS // DH)
                    for j in range(4):
                        for q in range(3):
                            sp.dma_start(stack[32 * q:32 * q + 32, :, 4 * h + j, :],
                                         parts[32 * j:32 * j + 32, :, q, h, :]).then_inc(stack_in[4 * h + j], 16)

            sp.dma_start(ids[:, :], a["ids"]).then_inc(ids_in, 16)
            sp.dma_start(ident[:, :], a["ident"]).then_inc(ident_in, 16)
            sp.dma_start(patches, a["patches"].rearrange("(m p) c -> p m c", m=2)).then_inc(image_in, 16)
            sp.dma_start(w_emb[:, :, :], a["w_emb"]).then_inc(embed_in, 16)
            sp.dma_start(g1[:, :], a["ln1_g"]).then_inc(image_in, 16)
            sp.dma_start(b1[:, :], a["ln1_b"]).then_inc(image_in, 16)
            sp.dma_start(w_tok, a["W"].rearrange("(c p) d -> p c d", p=P)).then_inc(image_in, 16)
            for dst, src in ((tok_bias[:, :], a["tok_bias"]),
                             (g2, a["ln2_g"].to_broadcast([pair, D])),
                             (b2, a["ln2_b"].to_broadcast([pair, D])),
                             (pos, a["pos"]), (shift[:, :, :], a["shift"]),
                             (cls[:, :], a["cls"]), (cls_put[:, :], a["cls_put"]),
                             (w_delta[:, :, :], a["w_delta"]), (w_bc[:, :, :, :], a["w_bc"]),
                             (b_delta[:, :], a["b_delta"]), (d_par[:, :], a["d_par"]),
                             (a_neg[:, :], a["a_log"]), (sel_f, a["sel"]), (red[:, :, :], a["red"]),
                             (router[:, :, :], a["router"]), (ebias[:, :], a["ebias"]),
                             (before_me[:, :], a["before_me"]), (valid[:, :], a["valid"]),
                             (desc[:, :, :], a["desc"]), (where[:, :], a["where"])):
                sp.dma_start(dst, src).then_inc(const_in, 16)
            sp.wait_ge(marked, 1)
            sp.dma_start(sorted_x.rearrange("(j p) d -> p j d", p=P),
                         x2_all[:, 0, :].unsqueeze(1).to_broadcast([P, RT, DR])).then_inc(zero_out, 16)
            sp.dma_start(a["out"][TOKENS:TOKENS + SPARE, :], x2_all[:, 0, 0:D]).then_inc(zero_out, 16)
            restack(0)
            for dst, src in ((w1s, a["sw1"]), (w3s, a["sw3"]), (w2s, a["sw2"]),
                             (tile_marks, a["tile_marks"]), (tile_ids, a["tile_ids"]), (keep, a["keep"])):
                sp.dma_start(dst[tuple([slice(None)] * len(dst.shape))], src).then_inc(shared_in, 16)
            def store(b):
                all_taken(sp, ("down", b, TILES - 2), ("down", b, TILES - 1))
                o = b * L
                sp.dma_start(a["out"][o:o + NIMG, :], h_all[0:NIMG, b * TILES, :]).then_inc(h_out, 16)
                sp.dma_start(a["out"][o + NIMG:o + L, :].rearrange("(k p) d -> p k d", p=P),
                             h_all[:, b * TILES + 1:(b + 1) * TILES, :]).then_inc(h_out, 16)

            for b in range(1, B):
                restack(b)
                if b >= 2:
                    store(b - 2)
            sp.wait_ge(x2_ready, B)
            all_taken(sp, ("ytrans", B - 1, TILES - 2), ("ytrans", B - 1, TILES - 1))
            sp.wait_ge(summed, NG // 4)
            for w, src in ((w1r, a["w1"]), (w3r, a["w3"]), (w2r, a["w2"])):
                if w is w2r:
                    taken(sp, ("logits", B - 1))
                for e in range(E):
                    sp.dma_start(w[:, :, e, :], src[:, :, e, :]).then_inc(routed_in, 16)
            store(B - 2)
            read_by_pe(sp, ("hidden", B - 1, NSH * KH - 1, NWC - 2), ("hidden", B - 1, NSH * KH - 1, NWC - 1))
            sp.wait_ge(scattered[0], 16 * TOPK * (NT - TILES))
            sp.wait_ge(scattered[1], 16 * TOPK * TILES)

            def load(j):
                if j >= 2:
                    sp.wait_ge(xgt_full, j - 1)
                    sp.wait_ge(aim_ready, j - 1)
                sp.dma_start(xg[:, j % 2, :], sorted_x[j * P:(j + 1) * P, :]).then_inc(xg_in[j % 2], 16)

            def load_next(j):
                if 0 < j < RT - 1:
                    load(j + 1)

            load(0)
            load(1)
            store(B - 1)

            routed_tiles(sp, load_next)

        @block.gpsimd
        def _(pool):
            nc.gpsimd.memset(minus_half[:, :], -0.5)
            nc.gpsimd.memset(rows[:, :], 0.0).then_inc(rows_zero, 1)
            pool.wait_ge(rows_zero, 1)

            def put(j):
                pool.wait_ge(ry_ready, j + 1)
                pool.wait_ge(aim_ready, j + 1)
                if j:
                    pool.wait_ge(y_out, 16 * j)
                pool.indirect_dma_start(
                    a["out"], bass.IndirectOffsetOnAxis(ap=aim[:, j:j + 1], axis=0), ry[:, j % 2, :], None,
                    bounds_check=TOKENS + SPARE - 1, compute_op=ALU.add).then_inc(y_out, 16)

            def item(x):
                if x in norms:
                    rows_, cols_ = (pair, 1) if x[0] in ("image", "immul") else (P, TILES)
                    pool.wait_ge(var_ready, norms[x])
                    nc.gpsimd.tensor_tensor(rstd[0:rows_, 0:cols_], var_eps[0:rows_, 0:cols_],
                                            minus_half[0:rows_, 0:cols_], ALU.pow).then_inc(rstd_ready, 1)
                elif x[0] == "gather":
                    b, k = x[1:]
                    if b and k == 0:
                        read_by_pe(pool, ("xtrans", b - 1, TILES - 2), ("xtrans", b - 1, TILES - 1))
                        nc.gpsimd.memset(rows[:, :], 0.0).then_inc(rows_zero, 1)
                        pool.wait_ge(rows_zero, b + 1)
                    if b == 0 and k == 0:
                        pool.wait_ge(local_ready, 1)
                    c0 = 0
                    for t in range(3):
                        pool.indirect_dma_start(
                            erow[:, k, c0:c0 + DIMS[t]], None, a[f"t{t}"],
                            bass.IndirectOffsetOnAxis(ap=local[:, t, b * KT + k:b * KT + k + 1], axis=0),
                            bounds_check=CUTS[t + 1] - CUTS[t] - 1, oob_is_err=False).then_inc(rows_in[k], 16)
                        c0 += DIMS[t]
                elif x[0] in ("part1", "part2") and x[1]:
                    remainder(pool, nc.gpsimd, x)
                elif x[0] == "hidden" and x[1] < B - 1:
                    gate_hidden(pool, nc.gpsimd, x)

            places(item)
            pool.wait_ge(slots_ready, 1)
            pool.wait_ge(zero_out, 32)
            pool.wait_ge(gates_in, 1)
            for k in range(TOPK):
                for part, (t0, t1) in enumerate(((0, NT - TILES), (NT - TILES, NT))):
                    if k:
                        pool.wait_ge(scattered[part], 16 * (t1 - t0))
                        nc.gpsimd.tensor_copy(x2_all[:, t0:t1, D + 1], gate[k][:, t0:t1]).then_inc(gates_in, 1)
                        pool.wait_ge(gates_in, part + 2)
                    for t in range(t0, t1):
                        n, _ = tile_rows(t % TILES)
                        pool.indirect_dma_start(
                            sorted_x, bass.IndirectOffsetOnAxis(ap=slot[k][0:n, t:t + 1], axis=0),
                            x2_all[0:n, t, :], None).then_inc(scattered[part], 16)
            pool.wait_ge(h_out, 16 * 2 * B)
            def tile(j):
                pool.wait_ge(xg_in[j % 2], 16 * (j // 2 + 1))
                nc.gpsimd.tensor_copy(share[:, j:j + 1], xg[:, j % 2, D + 1:DR])
                nc.gpsimd.tensor_copy(aim[:, j:j + 1], xg[:, j % 2, D:D + 1]).then_inc(aim_ready, 1)
                if j:
                    put(j - 1)

            def finish(j):
                put(j - 1)
                pool.wait_ge(y_out, 16 * j)

            routed_tiles(pool, tile, finish)

        @block.tensor
        def _(pe):
            def enter(x):
                n = order[x]
                if n >= 2:
                    pe.wait_ge(bank_free[n % 2], n // 2)
                return fill[n % 2]

            def leave(x, ins):
                ins.then_inc(bank_full[bank_of(x)], 1)

            def scan_part(G):
                if G < NG:
                    b, h, i, j = group(G)
                    if i == 0:
                        pe.wait_ge(stack_in[4 * h + j], 16 * RESTACKS * (b + 1))
                    if G == 0:
                        pe.wait_ge(sel_ready, 1)
                    if G:
                        pe.wait_ge(bx_ready, G)
                    for c in range(2):
                        last = nc.tensor.matmul(p_dx[:, c, :], sel[:, i, :], stack[:, 1, 4 * h + j, c * LC:(c + 1) * LC],
                                                start=True, stop=True)
                    last.then_inc(spread_dx, 1)
                    if G:
                        pe.wait_ge(decay_ready, G)
                    for c in range(2):
                        last = nc.tensor.matmul(p_delta[:, c, :], sel[:, i, :], stack[:, 0, 4 * h + j, c * LC:(c + 1) * LC],
                                                start=True, stop=True)
                    last.then_inc(spread_delta, 1)

            def scan_sums(G):
                if 6 <= G < NG + 4 and G % 4 == 2:
                    q = G // 4 - 1
                    b, h, i, _ = group(4 * q)
                    pe.wait_ge(hc_ready, 4 * q + 4)
                    if i == 0 and q:
                        pe.wait_ge(y_ready, q // 4)
                    for c in range(2):
                        for j in range(4):
                            last = nc.tensor.matmul(p_y[32 * j:32 * j + 32, c, :], red[:, i, :],
                                                    ring[:, (4 * q + j) % SLOTS, c * LC:(c + 1) * LC],
                                                    start=(i == 0), stop=(i == 3), tile_position=(0, 32 * j))
                    last.then_inc(summed, 1)

            def item(x):
                kind = x[0]
                if kind == "imtrans":
                    m = x[1]
                    f = enter(x)
                    pe.wait_ge(patch_ready, m + 1)
                    for c in range(PC):
                        last = nc.tensor.transpose(f[:, c * pair:(c + 1) * pair], patches[:, m, c * P:(c + 1) * P],
                                                   ident[0:pair, 0:pair])
                    leave(x, last)
                elif kind == "immul":
                    m = x[1]
                    f = enter(x)
                    pe.wait_ge(pT_ready, m + 1)
                    pe.wait_ge(image_in, 16 * IMAGE_LOADS)
                    pe.wait_ge(const_in, 16 * CONST_LOADS)
                    for c in range(PC):
                        nc.tensor.matmul(f[0:pair, 0:D], pT[:, m, c, :], w_tok[:, c, :], start=(c == 0), stop=False)
                    leave(x, nc.tensor.matmul(f[0:pair, 0:D], ones[0:1, 0:pair], tok_bias[:, :], start=False, stop=True))
                elif kind == "etrans":
                    b, k = x[1:]
                    f = enter(x)
                    pe.wait_ge(rows_in[k], 16 * 3 * (b + 1))
                    nc.tensor.transpose(f[:, 0:P], erow[:, k, 0:P], ident[:, :])
                    nc.tensor.transpose(f[:, P:2 * P], erow[:, k, P:2 * P], ident[:, :])
                    leave(x, nc.tensor.transpose(f[0:ECOLS - D, 2 * P:3 * P], erow[:, k, D:ECOLS], ident[:, :]))
                elif kind == "embed":
                    b, k = x[1:]
                    f = enter(x)
                    taken(pe, ("etrans", b, k))
                    if b == 0 and k == 0:
                        pe.wait_ge(embed_in, 16)
                    nc.tensor.matmul(f[:, 0:D], eT[:, k % 2, 0, :], w_emb[:, 0, :], start=True, stop=False)
                    nc.tensor.matmul(f[:, 0:D], eT[:, k % 2, 1, :], w_emb[:, 1, :], start=False, stop=False)
                    leave(x, nc.tensor.matmul(f[:, 0:D], eT[0:ECOLS - D, k % 2, 2, :], w_emb[0:ECOLS - D, 2, :],
                                              start=False, stop=True))
                elif kind == "place":
                    b = x[1]
                    f = enter(x)
                    pe.wait_ge(himg_ready, b // 2 + 1)
                    nc.tensor.matmul(f[0:NIMG, 0:D], shift[:, b % 2, :], himg[:, b // 2, :], start=True, stop=False)
                    leave(x, nc.tensor.matmul(f[0:NIMG, 0:D], cls_put[:, :], cls[:, :], start=False, stop=True))
                elif kind == "xtrans":
                    b, k = x[1:]
                    n, _ = tile_rows(k)
                    f = enter(x)
                    pe.wait_ge(xn_ready, b + 1)
                    for h in range(DH):
                        last = nc.tensor.transpose(f[:, h * P:h * P + n], xn[0:n, k, h * P:(h + 1) * P], ident[0:n, 0:n])
                    leave(x, last)
                elif kind == "zproj":
                    b, h, c = x[1:]
                    f = enter(x)
                    all_taken(pe, ("xtrans", b, TILES - 2), ("xtrans", b, TILES - 1))
                    for k in range(KD):
                        last = nc.tensor.matmul(f[:, 0:LC], w_delta[:, k, h * P:(h + 1) * P],
                                                xT[:, b % 2, k, c * LC:(c + 1) * LC], start=(k == 0), stop=(k == KD - 1))
                    leave(x, last)
                elif kind == "bcproj":
                    b, w, c = x[1:]
                    f = enter(x)
                    all_taken(pe, ("xtrans", b, TILES - 2), ("xtrans", b, TILES - 1))
                    for k in range(KD):
                        last = nc.tensor.matmul(f[:, 0:LC], w_bc[:, k, w, :],
                                                xT[:, b % 2, k, c * LC:(c + 1) * LC], start=(k == 0), stop=(k == KD - 1))
                    leave(x, last)
                elif kind == "ytrans":
                    b, k = x[1:]
                    n, c0 = tile_rows(k)
                    f = enter(x)
                    pe.wait_ge(y_ready, DH * (b + 1))
                    for h in range(DH):
                        last = nc.tensor.transpose(f[0:n, h * P:(h + 1) * P], yT[:, h, c0:c0 + n], ident[:, :])
                    leave(x, last)
                elif kind == "x2trans":
                    b, k = x[1:]
                    n, _ = tile_rows(k)
                    f = enter(x)
                    pe.wait_ge(x2_ready, b + 1)
                    for h in range(DH):
                        last = nc.tensor.transpose(f[:, h * P:h * P + n], x2_all[0:n, b * TILES + k, h * P:(h + 1) * P],
                                                   ident[0:n, 0:n])
                    leave(x, last)
                elif kind == "scores":
                    b, c = x[1:]
                    w = (LC, L - LC)[c]
                    f = enter(x)
                    all_taken(pe, ("x2trans", b, TILES - 2), ("x2trans", b, TILES - 1))
                    for h in range(KD):
                        last = nc.tensor.matmul(f[0:E, 0:w], router[:, h, :], x2T[:, h, c * LC:c * LC + w],
                                                start=(h == 0), stop=(h == KD - 1))
                    leave(x, last)
                elif kind == "logits":
                    b = x[1]
                    f = enter(x)
                    all_taken(pe, ("scores", b, 0), ("scores", b, 1))
                    for k in range(TILES):
                        n, c0 = tile_rows(k)
                        last = nc.tensor.transpose(f[0:n, k * E:(k + 1) * E], scoreT[:, c0:c0 + n], ident[0:E, 0:E])
                    leave(x, last)
                elif kind == "hidden":
                    b, j, c = x[1:]
                    e, m = divmod(j, KH)
                    f = enter(x)
                    if b == 0 and j == 0 and c == 0:
                        pe.wait_ge(shared_in, 16 * SHARED_LOADS)
                    if j == 0 and c == 0:
                        all_taken(pe, ("x2trans", b, TILES - 2), ("x2trans", b, TILES - 1))
                    for w, o in ((w1s, 0), (w3s, WC)):
                        for k in range(KD):
                            last = nc.tensor.matmul(f[:, o:o + WC], w[:, k, e, m * P:(m + 1) * P],
                                                    x2T[:, k, c * WC:(c + 1) * WC], start=(k == 0), stop=(k == KD - 1))
                    leave(x, last)
                elif kind == "down":
                    b, k = x[1:]
                    n, c0 = tile_rows(k)
                    f = enter(x)
                    pe.wait_ge(gated_ready, NSH * KH * NWC * (b + 1))
                    for j in range(NSH * KH):
                        e, m = divmod(j, KH)
                        last = nc.tensor.matmul(f[0:n, 0:D], gated[:, j, c0:c0 + n], w2s[:, m, e, :],
                                                start=(j == 0), stop=(j == NSH * KH - 1))
                    leave(x, last)
                elif kind == "route":
                    pe.wait_ge(both_ready, 1)
                    m = both[:, :, :].rearrange("p t e -> p (t e)")
                    nc.tensor.matmul(psum[:, 0, 0:NT * E], before_me[:, :], m, start=True, stop=True)
                    nc.tensor.matmul(psum[:, 1, 0:NT * E], ones[:, :], m, start=True, stop=True).then_inc(rank_ready, 1)

            pe.wait_ge(ident_in, 16)
            places(item, scan_part, scan_sums)

            def xtrans(j):
                pe.wait_ge(xg_in[j % 2], 16 * (j // 2 + 1))
                if j:
                    pe.wait_ge(xgT_ready, j)
                for h in range(KD):
                    last = nc.tensor.transpose(psum[:, 0, h * P:(h + 1) * P], xg[:, j % 2, h * P:(h + 1) * P], ident[:, :])
                last.then_inc(xgt_full, 1)

            def up(j):
                pe.wait_ge(xgT_ready, j + 1)
                if j >= 2:
                    pe.wait_ge(rgate_ready, j - 1)
                ex = pe.value_load(tile_expert[0:1, j:j + 1], min_val=0, max_val=E - 1)
                for w, bank in ((w1r, 1 + j % 2), (w3r, 3 + j % 2)):
                    for k in range(KD):
                        last = nc.tensor.matmul(psum[:, bank, :], xgT[:, j % 2, k, :],
                                                w[:, k, bass.ds(ex, 1), :], start=(k == 0), stop=(k == KD - 1))
                    last.then_inc(up_done, 1)

            def gtrans(j):
                pe.wait_ge(rgate_ready, j + 1)
                if j >= 2:
                    pe.wait_ge(rgT_ready, j - 1)
                for m in range(KH):
                    last = nc.tensor.transpose(psum[:, 5 + j % 2, m * P:(m + 1) * P], rgate[:, j % 2, m * P:(m + 1) * P],
                                               ident[:, :])
                last.then_inc(rgt_full, 1)

            def down(j):
                pe.wait_ge(rgT_ready, j + 1)
                if j:
                    pe.wait_ge(ry_ready, j)
                ex = pe.value_load(tile_expert[0:1, j:j + 1], min_val=0, max_val=E - 1)
                for m in range(KH):
                    last = nc.tensor.matmul(psum[:, 7, 0:D], rgT[:, j % 2, m, :], w2r[:, m, bass.ds(ex, 1), :],
                                            start=(m == 0), stop=(m == KH - 1))
                last.then_inc(down_done, 1)

            pe.wait_ge(routed_in, 16 * 3 * E)
            pe.wait_ge(experts_ready, 1)
            xtrans(0)

            def tile(j):
                up(j)
                if j + 1 < RT:
                    xtrans(j + 1)
                if j:
                    down(j - 1)
                gtrans(j)

            routed_tiles(pe, tile, lambda j: down(j - 1))

        @block.scalar
        def _(act):
            steps = [0]

            def link(ins):
                steps[0] += 1
                ins.then_inc(act_done, 1)
                act.wait_ge(act_done, steps[0])

            def full(x):
                act.wait_ge(bank_full[bank_of(x)], turn_of(x))
                return fill[bank_of(x)]

            def scan_part(G):
                if G < NG:
                    b, h, i, j = group(G)
                    act.wait_ge(spread_delta, G + 1)
                    if G >= 2:
                        act.wait_ge(state_ready, G - 1)
                    nc.scalar.activation(decay[:, G % 2, :].rearrange("p (c t) -> p c t", c=2), p_delta, ACT.Exp,
                                         scale=a_neg[:, G % GROUPS:G % GROUPS + 1]).then_inc(decay_ready, 1)

            def item(x):
                kind = x[0]
                if kind == "etrans":
                    b, k = x[1:]
                    f = full(x)
                    if k >= 2:
                        read_by_pe(act, ("embed", b, k - 2))
                    nc.scalar.copy(eT[:, k % 2, 0:2, :].rearrange("p c t -> p (c t)"), f[:, 0:2 * P])
                    nc.scalar.copy(eT[0:ECOLS - D, k % 2, 2, :], f[0:ECOLS - D, 2 * P:3 * P]).then_inc(bank_free[bank_of(x)], 1)
                elif kind in ("embed", "place"):
                    b = x[1]
                    k = 1 + x[2] if kind == "embed" else 0
                    n, _ = tile_rows(k)
                    f = full(x)
                    act.wait_ge(zeroed, 1)
                    nc.scalar.copy(h_all[0:n, b * TILES + k, :], f[0:n, 0:D]).then_inc(bank_free[bank_of(x)], 1)
                elif kind == "xtrans":
                    b, k = x[1:]
                    n, c0 = tile_rows(k)
                    f = full(x)
                    if b >= 2 and k == 0:
                        act.wait_ge(y_ready, DH * (b - 1))
                        act.wait_ge(dx_ready, DH * (b - 1))
                    nc.scalar.copy(xT[:, b % 2, :, c0:c0 + n],
                                   f[:, 0:2 * P].rearrange("p (h t) -> p h t", h=2)[:, :, 0:n]).then_inc(bank_free[bank_of(x)], 1)
                elif kind == "zproj":
                    b, h, c = x[1:]
                    if b == 0 and h == 0 and c == 0:
                        act.wait_ge(const_in, 16 * CONST_LOADS)
                        nc.scalar.activation(sel[:, :, :], sel_f, ACT.Copy).then_inc(sel_ready, 1)
                        link(nc.scalar.activation(a_neg[:, :], a_neg[:, :], ACT.Exp))
                        link(nc.scalar.mul(a_neg[:, :], a_neg[:, :], -1.0))
                    f = full(x)
                    if b and c == 0:
                        act.wait_ge(part3, 2 * ((b - 1) * DH + h + 1))
                    nc.scalar.activation(zed[:, h, c * LC:(c + 1) * LC], f[:, 0:LC], ACT.Identity,
                                         bias=b_delta[:, h:h + 1]).then_inc(bank_free[bank_of(x)], 1)
                elif kind == "abs":
                    b, h = x[1:]
                    all_taken(act, ("zproj", b, h, 0), ("zproj", b, h, 1))
                    nc.scalar.activation(aux[:, h, :], zed[:, h, :], ACT.Abs).then_inc(abs_ready, 1)
                elif kind == "exp":
                    b, h = x[1:]
                    act.wait_ge(abs_ready, b * DH + h + 1)
                    nc.scalar.activation(aux[:, h, :], aux[:, h, :], ACT.Exp, scale=-1.0).then_inc(exp_ready, 1)
                elif kind == "log":
                    b, h = x[1:]
                    act.wait_ge(exp_ready, b * DH + h + 1)
                    nc.scalar.activation(aux[:, h, :], aux[:, h, :], ACT.Ln, bias=1.0).then_inc(log_ready, 1)
                elif kind == "bcproj":
                    b, w, c = x[1:]
                    f = full(x)
                    if b >= 2:
                        act.wait_ge(hc_ready, (b - 1) * GROUPS)
                    nc.scalar.copy((Bn, Cn)[w][:, b % 2, c * LC:(c + 1) * LC], f[:, 0:LC]).then_inc(bank_free[bank_of(x)], 1)
                elif kind == "part1":
                    b, h, v = x[1:]
                    act.wait_ge((delta_ready, dx_ready)[v], b * DH + h + 1)
                    if b and v == 0:
                        for j in range(4):
                            act.wait_ge(stack_in[4 * h + j], 16 * RESTACKS * b)
                    nc.scalar.copy(parts[:, v, 0, h, :], zed[:, h, :]).then_inc(part1, 1)
                elif kind == "part2":
                    b, h, v = x[1:]
                    act.wait_ge(rest1, part_no(x) + 1)
                    nc.scalar.copy(parts[:, v, 1, h, :], aux[:, h, :]).then_inc(part2, 1)
                elif kind == "x2trans":
                    b, k = x[1:]
                    n, c0 = tile_rows(k)
                    f = full(x)
                    if b and k == 0:
                        read_by_pe(act, ("hidden", b - 1, NSH * KH - 1, NWC - 2), ("hidden", b - 1, NSH * KH - 1, NWC - 1))
                    nc.scalar.copy(x2T[:, :, c0:c0 + n],
                                   f[:, 0:2 * P].rearrange("p (h t) -> p h t", h=2)[:, :, 0:n]).then_inc(bank_free[bank_of(x)], 1)
                elif kind == "scores":
                    b, c = x[1:]
                    w = (LC, L - LC)[c]
                    f = full(x)
                    if c == 0:
                        all_taken(act, ("ytrans", b, TILES - 2), ("ytrans", b, TILES - 1))
                    nc.scalar.activation(scoreT[:, c * LC:c * LC + w], f[0:E, 0:w], ACT.Identity,
                                         bias=ebias[:, :]).then_inc(bank_free[bank_of(x)], 1)
                elif kind == "logits":
                    b = x[1]
                    f = full(x)
                    act.wait_ge(zeroed, 1)
                    nc.scalar.copy(logit[0:NIMG, b * TILES, :], f[0:NIMG, 0:E])
                    nc.scalar.copy(logit[:, b * TILES + 1:(b + 1) * TILES, :],
                                   f[:, E:TILES * E].rearrange("p (k e) -> p k e", e=E)).then_inc(bank_free[bank_of(x)], 1)
                elif kind == "hidden":
                    b, j, c = x[1:]
                    f = full(x)
                    n = (b * NSH * KH + j) * NWC + c
                    if n >= UPS:
                        act.wait_ge(gated_ready, n - UPS + 1)
                    nc.scalar.activation(tanh_h[:, n % UPS, :], f[:, 0:WC], ACT.Tanh, scale=0.5)
                    nc.scalar.copy(up_h[:, n % UPS, :, :].rearrange("p a c -> p (a c)"), f[:, 0:2 * WC]).then_inc(bank_free[bank_of(x)], 1)
                elif kind == "route":
                    act.wait_ge(gap_ready, 1)
                    nc.scalar.activation(gate[1][:, :], gate[1][:, :], ACT.Exp).then_inc(gap_exp, 1)

            places(item, scan_part)

            def gated_out(y):
                act.wait_ge(down_done, y + 1)
                act.wait_ge(aim_ready, y + 1)
                if y >= 2:
                    act.wait_ge(y_out, 16 * (y - 1))
                nc.scalar.activation(ry[:, y % 2, :], psum[:, 7, 0:D], ACT.Identity,
                                     scale=share[:, y:y + 1]).then_inc(ry_ready, 1)

            def tile(j):
                act.wait_ge(xgt_full, j + 1)
                if j >= 2:
                    act.wait_ge(up_done, 2 * (j - 1))
                nc.scalar.copy(xgT[:, j % 2, :, :].rearrange("p c t -> p (c t)"), psum[:, 0, 0:D]).then_inc(xgT_ready, 1)
                if j >= 2:
                    gated_out(j - 2)
                act.wait_ge(up_done, 2 * j + 1)
                if j >= 2:
                    act.wait_ge(rgate_ready, j - 1)
                nc.scalar.activation(rsilu[:, j % 2, :], psum[:, 1 + j % 2, :], ACT.Silu).then_inc(rsilu_ready, 1)

            def finish(j):
                gated_out(j - 2)
                gated_out(j - 1)

            routed_tiles(act, tile, finish)

        @block.vector
        def _(dve):
            steps = [0]

            def link(ins):
                steps[0] += 1
                ins.then_inc(dve_done, 1)
                dve.wait_ge(dve_done, steps[0])

            def full(x):
                dve.wait_ge(bank_full[bank_of(x)], turn_of(x))
                return fill[bank_of(x)]

            v = nc.vector
            dve.wait_ge(ids_in, 16)
            link(v.tensor_copy(ids_f[:, :], ids[:, :]))
            for t in range(3):
                lo, hi = CUTS[t], CUTS[t + 1]
                link(v.tensor_scalar(inside[:, t, :], ids_f[:, :], float(lo), None, ALU.is_ge))
                link(v.scalar_tensor_tensor(inside[:, t, :], ids_f[:, :], float(hi), inside[:, t, :], ALU.is_lt, ALU.mult))
                link(v.scalar_tensor_tensor(local_f[:, t, :], ids_f[:, :], float(lo) + NOWHERE, inside[:, t, :],
                                            ALU.subtract, ALU.mult))
                link(v.tensor_scalar(local_f[:, t, :], local_f[:, t, :], NOWHERE, None, ALU.add))
            v.tensor_copy(local[:, :, :], local_f[:, :, :]).then_inc(local_ready, 1)
            for b in range(B):
                v.memset(h_all[:, b * TILES, :], 0.0)
            v.memset(x2_all[:, 0, :], 0.0)
            v.memset(logit[:, :, :], 0.0)
            v.memset(ones[:, :], 1.0)
            v.memset(xT[:, :, :, L:LP], 0.0).then_inc(zeroed, 1)

            def scan_part(G):
                if G < NG:
                    b, h, i, j = group(G)
                    if G % GROUPS == 0:
                        all_taken(dve, ("bcproj", b, 1, 0), ("bcproj", b, 1, 1))
                    dve.wait_ge(spread_dx, G + 1)
                    if G >= SLOTS:
                        dve.wait_ge(summed, (G - SLOTS) // 4 + 1)
                    v.tensor_tensor(ring[:, G % SLOTS, :].rearrange("p (c t) -> p c t", c=2), p_dx,
                                    Bn[:, b % 2, :].rearrange("p (c t) -> p c t", c=2), ALU.mult).then_inc(bx_ready, 1)
                if 1 <= G <= NG:
                    s = G - 1
                    dve.wait_ge(decay_ready, s + 1)
                    dve.wait_ge(bx_ready, s + 1)
                    r = ring[:, s % SLOTS, :]
                    v.tensor_tensor_scan(r, decay[:, s % 2, :], r, 0.0, ALU.mult, ALU.add).then_inc(state_ready, 1)
                if 2 <= G <= NG + 1:
                    s = G - 2
                    dve.wait_ge(state_ready, s + 1)
                    r = ring[:, s % SLOTS, :]
                    v.tensor_tensor(r, r, Cn[:, (s // GROUPS) % 2, :], ALU.mult).then_inc(hc_ready, 1)
                if G >= 19 and (G - 19) % 16 == 0:
                    n = (G - 19) // 16
                    b, h = divmod(n, DH)
                    dve.wait_ge(summed, 4 * (n + 1))
                    if b:
                        read_by_pe(dve, ("ytrans", b - 1, TILES - 2), ("ytrans", b - 1, TILES - 1), ("logits", b - 1))
                    v.scalar_tensor_tensor(yT[:, h, :].rearrange("p (c t) -> p c t", c=2),
                                           xT[:, b % 2, h, :].rearrange("p (c t) -> p c t", c=2), d_par[:, h:h + 1], p_y,
                                           ALU.mult, ALU.add).then_inc(y_ready, 1)

            def stats(src):
                for k in range(TILES):
                    last = v.bn_stats(stat[:, k, :], src[:, k, :])
                link(last)
                for k in range(TILES):
                    last = v.bn_aggr(mv[:, k, :], stat[:, k, :])
                link(last)
                v.tensor_scalar(var_eps[:, :], mv[:, :, 1], EPS, None, ALU.add).then_inc(var_ready, 1)

            def norm(dst, src, turn):
                dve.wait_ge(rstd_ready, turn)
                for k in range(TILES):
                    last = v.tensor_scalar(dst[:, k, :], src[:, k, :], mv[:, k, 0:1], rstd[:, k:k + 1],
                                           ALU.subtract, ALU.mult)
                return last

            def item(x):
                kind = x[0]
                if kind == "image":
                    m = x[1]
                    if m == 0:
                        dve.wait_ge(image_in, 16 * IMAGE_LOADS)
                    half = PDIM // 2
                    v.bn_stats(istat[:, 0, :], patches[:, m, 0:half])
                    link(v.bn_stats(istat[:, 1, :], patches[:, m, half:PDIM]))
                    link(v.bn_aggr(imv[:, :], istat[:, :, :].rearrange("p a b -> p (a b)")))
                    v.tensor_scalar(var_eps[0:pair, 0:1], imv[:, 1:2], EPS, None, ALU.add).then_inc(var_ready, 1)
                    dve.wait_ge(rstd_ready, norms[x])
                    v.tensor_scalar(patches[:, m, :], patches[:, m, :], imv[:, 0:1], rstd[0:pair, 0:1],
                                    ALU.subtract, ALU.mult).then_inc(patch_ready, 1)
                elif kind == "imtrans":
                    m = x[1]
                    f = full(x)
                    src = f[:, 0:PC * pair].rearrange("p (c t) -> p c t", c=PC)
                    v.tensor_tensor(pT[:, m, :, :], src, g1[:, :].unsqueeze(2).to_broadcast([P, PC, pair]),
                                    ALU.mult).then_inc(bank_free[bank_of(x)], 1)
                    taken(dve, x)
                    v.tensor_tensor(pT[:, m, :, :], pT[:, m, :, :], b1[:, :].unsqueeze(2).to_broadcast([P, PC, pair]),
                                    ALU.add).then_inc(pT_ready, 1)
                elif kind == "immul":
                    m = x[1]
                    f = full(x)
                    link(v.bn_stats(istat[:, 0, :], f[0:pair, 0:D]))
                    link(v.bn_aggr(imv[:, :], istat[:, 0, :]))
                    v.tensor_scalar(var_eps[0:pair, 0:1], imv[:, 1:2], EPS, None, ALU.add).then_inc(var_ready, 1)
                    dve.wait_ge(rstd_ready, norms[x])
                    v.tensor_scalar(himg[:, m, :], f[0:pair, 0:D], imv[:, 0:1], rstd[0:pair, 0:1],
                                    ALU.subtract, ALU.mult).then_inc(bank_free[bank_of(x)], 1)
                elif kind == "image2":
                    m = x[1]
                    taken(dve, ("immul", m))
                    dve.wait_ge(const_in, 16 * CONST_LOADS)
                    if m == 0:
                        dve.wait_ge(zeroed, 1)
                        v.tensor_copy(x2_all[:, 0, D:D + 1], where[:, NT:NT + 1]).then_inc(marked, 1)
                    link(v.tensor_tensor(himg[:, m, :], himg[:, m, :], g2, ALU.mult))
                    link(v.tensor_tensor(himg[:, m, :], himg[:, m, :], b2, ALU.add))
                    v.tensor_tensor(himg[:, m, :], himg[:, m, :], pos, ALU.add).then_inc(himg_ready, 1)
                elif kind == "stats1":
                    b = x[1]
                    all_taken(dve, ("embed", b, KT - 1), ("place", b))
                    stats(h_all[:, b * TILES:(b + 1) * TILES, :])
                elif kind == "norm1":
                    b = x[1]
                    norm(xn, h_all[:, b * TILES:(b + 1) * TILES, :], norms[("stats1", b)]).then_inc(xn_ready, 1)
                elif kind == "delta":
                    b, h = x[1:]
                    dve.wait_ge(log_ready, b * DH + h + 1)
                    v.scalar_tensor_tensor(zed[:, h, :], zed[:, h, :], 0.0, aux[:, h, :], ALU.max, ALU.add).then_inc(delta_ready, 1)
                elif kind == "dx":
                    b, h = x[1:]
                    dve.wait_ge(part3, 2 * (b * DH + h) + 1)
                    v.tensor_tensor(zed[:, h, :], zed[:, h, :], xT[:, b % 2, h, :], ALU.mult).then_inc(dx_ready, 1)
                elif kind in ("part1", "part2") and x[1] == 0:
                    remainder(dve, v, x)
                elif kind == "ytrans":
                    b, k = x[1:]
                    n, _ = tile_rows(k)
                    f = full(x)
                    t = b * TILES + k
                    v.tensor_tensor(h_all[0:n, t, :], h_all[0:n, t, :], f[0:n, 0:D], ALU.add).then_inc(bank_free[bank_of(x)], 1)
                elif kind == "stats2":
                    b = x[1]
                    all_taken(dve, ("ytrans", b, TILES - 2), ("ytrans", b, TILES - 1))
                    stats(h_all[:, b * TILES:(b + 1) * TILES, :])
                elif kind == "norm2":
                    b = x[1]
                    if b == 0:
                        dve.wait_ge(zero_out, 32)
                    norm(x2_all[:, b * TILES:(b + 1) * TILES, 0:D],
                         h_all[:, b * TILES:(b + 1) * TILES, :], norms[("stats2", b)]).then_inc(x2_ready, 1)
                elif kind == "hidden":
                    b, j, c = x[1:]
                    taken(dve, x)
                    n = (b * NSH * KH + j) * NWC + c
                    if n >= 2:
                        dve.wait_ge(gated_ready, n - 1)
                    v.scalar_tensor_tensor(silu_h[:, n % 2, :], tanh_h[:, n % UPS, :], 1.0, up_h[:, n % UPS, 0, :],
                                           ALU.add, ALU.mult).then_inc(silu_ready, 1)
                    if b == B - 1:
                        gate_hidden(dve, v, x)
                elif kind == "down":
                    b, k = x[1:]
                    n, _ = tile_rows(k)
                    f = full(x)
                    t = b * TILES + k
                    v.scalar_tensor_tensor(h_all[0:n, t, :], f[0:n, 0:D], 0.5, h_all[0:n, t, :],
                                           ALU.mult, ALU.add).then_inc(bank_free[bank_of(x)], 1)
                elif kind == "choose":
                    choose()
                elif kind == "route":
                    route()

            def choose():
                taken(dve, ("logits", B - 1))
                dve.wait_ge(shared_in, 16 * SHARED_LOADS)
                src = logit
                for k in range(TOPK):
                    link(v.tensor_reduce(top[k][:, :], src[:, :, :], AX.X, ALU.max))
                    link(v.tensor_tensor(pick[k][:, :, :], src[:, :, :], top[k][:, :].unsqueeze(2).to_broadcast([P, NT, E]),
                                         ALU.is_equal))
                    link(v.tensor_tensor(pick[k][:, :, :], pick[k][:, :, :], desc[:, :, :], ALU.mult))
                    link(v.tensor_reduce(first_of[:, :], pick[k][:, :, :], AX.X, ALU.max))
                    link(v.tensor_tensor(pick[k][:, :, :], desc[:, :, :], first_of[:, :].unsqueeze(2).to_broadcast([P, NT, E]),
                                         ALU.is_equal))
                    if k == 0:
                        link(v.scalar_tensor_tensor(work[:, :, :], pick[0][:, :, :], -3e38, logit[:, :, :], ALU.mult, ALU.add))
                        src = work
                v.tensor_tensor(gate[1][:, :], top[1][:, :], top[0][:, :], ALU.subtract).then_inc(gap_ready, 1)
                link(v.tensor_tensor(both[:, :, :], pick[0][:, :, :], pick[1][:, :, :], ALU.add))
                v.tensor_tensor(both[:, :, :], both[:, :, :], valid[:, :].unsqueeze(2).to_broadcast([P, NT, E]),
                                ALU.mult).then_inc(both_ready, 1)

            def route():
                dve.wait_ge(gap_exp, 1)
                link(v.tensor_scalar(gate[0][:, :], gate[1][:, :], 1.0, None, ALU.add))
                link(v.reciprocal(gate[0][:, :], gate[0][:, :]))
                link(v.tensor_tensor(gate[1][:, :], gate[1][:, :], gate[0][:, :], ALU.mult))
                v.tensor_copy(x2_all[:, :, D], where[:, 0:NT])
                v.tensor_copy(x2_all[:, :, D + 1], gate[0][:, :]).then_inc(gates_in, 1)
                dve.wait_ge(rank_ready, 1)
                link(v.tensor_copy(counts[:, :, :], psum[:, 1, 0:NT * E].rearrange("p (t e) -> p e t", e=E)))
                link(v.tensor_tensor_scan(upto[:, :, :].rearrange("p e t -> p (e t)"), keep[:, :, :].rearrange("p e t -> p (e t)"),
                                          counts[:, :, :].rearrange("p e t -> p (e t)"), 0.0, ALU.mult, ALU.add))
                link(v.tensor_tensor(counts[:, :, :], upto[:, :, :], counts[:, :, :], ALU.subtract))
                link(v.tensor_tensor(over[:, :, :], upto[:, :, NT - 1:NT].to_broadcast([P, E, CT]), tile_marks[:, :, :], ALU.is_gt))
                link(v.tensor_reduce(etiles[:, :], over[:, :, :], AX.X, ALU.add))
                link(v.tensor_tensor_scan(eend[:, :], ones[:, 0:E], etiles[:, :], 0.0, ALU.mult, ALU.add))
                link(v.tensor_tensor(etiles[:, :], eend[:, :], etiles[:, :], ALU.subtract))
                link(v.scalar_tensor_tensor(counts[:, :, :], etiles[:, :].unsqueeze(2).to_broadcast([P, E, NT]), float(P),
                                            counts[:, :, :], ALU.mult, ALU.add))
                link(v.tensor_tensor(work[:, :, :], psum[:, 0, 0:NT * E].rearrange("p (t e) -> p t e", e=E),
                                     counts[:, :, :].rearrange("p e t -> p t e"), ALU.add))
                for k in range(TOPK):
                    link(v.tensor_tensor(pick[k][:, :, :], pick[k][:, :, :], work[:, :, :], ALU.mult))
                    link(v.tensor_reduce(slot_f[k][:, :], pick[k][:, :, :], AX.X, ALU.add))
                    last = v.tensor_copy(slot[k][:, :], slot_f[k][:, :])
                last.then_inc(slots_ready, 1)
                link(v.tensor_tensor(past[:, :, :], tile_ids[:, :, :], eend[0:1, :].unsqueeze(1).to_broadcast([1, RT, E]), ALU.is_ge))
                link(v.tensor_reduce(tile_expert_f[:, :], past[:, :, :], AX.X, ALU.add))
                link(v.tensor_scalar(tile_expert_f[:, :], tile_expert_f[:, :], float(E - 1), None, ALU.min))
                v.tensor_copy(tile_expert[:, :], tile_expert_f[:, :])
                v.tensor_copy(tile_count[:, :], eend[0:1, E - 1:E]).then_inc(experts_ready, 1)

            places(item, scan_part)

            def tile(j):
                dve.wait_ge(rsilu_ready, j + 1)
                dve.wait_ge(up_done, 2 * j + 2)
                if j >= 2:
                    dve.wait_ge(rgt_full, j - 1)
                v.tensor_tensor(rgate[:, j % 2, :], rsilu[:, j % 2, :], psum[:, 3 + j % 2, :], ALU.mult).then_inc(rgate_ready, 1)
                dve.wait_ge(rgt_full, j + 1)
                if j >= 2:
                    dve.wait_ge(down_done, j - 1)
                v.tensor_copy(rgT[:, j % 2, :, :].rearrange("p c t -> p (c t)"), psum[:, 5 + j % 2, :]).then_inc(rgT_ready, 1)

            routed_tiles(dve, tile)


def position_table():
    f = np.float32
    y, x = np.meshgrid(np.arange(HP), np.arange(HP), indexing="ij")
    omega = np.arange(D // 4, dtype=f) / f(D // 4 - 1)
    omega = f(1.0) / np.power(f(10000.0), omega)
    y = y.reshape(-1)[:, None].astype(f) * omega[None, :]
    x = x.reshape(-1)[:, None].astype(f) * omega[None, :]
    return np.concatenate((np.sin(x), np.cos(x), np.sin(y), np.cos(y)), axis=1).astype(f)


def constants():
    f = np.float32
    c = {"ident": np.eye(P, dtype=f)}
    c["before_me"] = np.triu(np.ones((P, P), f), 1)
    c["pos"] = np.concatenate([position_table()] * 2)
    shift = np.zeros((2 * NPATCH, 2, NIMG), f)
    for m in range(2):
        for r in range(NPATCH):
            shift[m * NPATCH + r, m, r + 1] = 1
    c["shift"] = shift
    put = np.zeros((2, NIMG), f)
    put[:, 0] = 1
    c["cls_put"] = put
    sel = np.zeros((96, 4, P), f)
    red = np.zeros((P, 4, 32), f)
    for i in range(4):
        for m in range(P):
            r = m % R
            for q in range(3):
                sel[32 * q + R * i + r, i, m] = 1
            red[m, i, R * i + r] = 1
    c["sel"], c["red"] = sel, red
    valid = np.ones((P, NT), f)
    valid[NIMG:, ::TILES] = 0
    c["valid"] = valid
    c["desc"] = np.ascontiguousarray(np.broadcast_to(np.arange(E, 0, -1, dtype=f), (P, NT, E)))
    c["tile_marks"] = np.ascontiguousarray(np.broadcast_to(P * np.arange(CT, dtype=f), (P, E, CT)))
    c["tile_ids"] = np.ascontiguousarray(np.broadcast_to(np.arange(RT, dtype=f)[None, :, None], (1, RT, E)))
    keep = np.ones((P, E, NT), f)
    keep[:, :, 0] = 0
    c["keep"] = keep
    first = [b * L + tile_rows(k)[1] for b in range(B) for k in range(TILES)] + [TOKENS]
    c["where"] = (np.array(first, f)[None, :] + np.arange(P, dtype=f)[:, None]).astype(f)
    return c


def layout(x, x_txt, **w):
    t = {k.split("_", 2)[2] if k.startswith("L0_") else k: np.asarray(v) for k, v in w.items()}
    x = np.asarray(x)
    a = {}
    a["patches"] = x.reshape(B, CH, HP, PATCH, HP, PATCH).transpose(0, 2, 4, 3, 5, 1).reshape(B * NPATCH, PDIM)
    a["ids"] = np.asarray(x_txt).reshape(B * KT, P).T
    a["cls"] = np.concatenate([t["cls_token"].reshape(1, D), t["cls_pos_embedding"].reshape(1, D)])
    for n in ("ln1_g", "ln1_b"):
        a[n] = t[n].reshape(PC, P).T
    a["W"] = t["W"]
    a["tok_bias"] = t["bias"].reshape(1, D)
    a["ln2_g"], a["ln2_b"] = t["ln2_g"].reshape(1, D), t["ln2_b"].reshape(1, D)
    for n in ("t0", "t1", "t2"):
        a[n] = t[n]
    rest = np.concatenate([t["w1_txt"], t["w2_txt"], np.zeros((P - DIMS[1] - DIMS[2], D), np.float32)])
    a["w_emb"] = np.stack([t["w0_txt"][:P], t["w0_txt"][P:], rest], axis=1)
    al = t["A_log"].reshape(DH, 4, 4, R, N)
    a["a_log"] = al.transpose(4, 3, 0, 2, 1).reshape(P, GROUPS)
    a["w_delta"] = t["W_delta"].T.reshape(KD, P, D).transpose(1, 0, 2)
    bc = np.stack([t["W_B"], t["W_C"]]).transpose(2, 0, 1).reshape(KD, P, 2, N)
    a["w_bc"] = np.repeat(bc.transpose(1, 0, 2, 3), R, axis=3)
    a["b_delta"] = t["b_delta"].reshape(DH, P).T
    a["d_par"] = t["D_param"].reshape(DH, P).T
    a["router"] = t["router_w"].T.reshape(KD, P, E).transpose(1, 0, 2)
    a["ebias"] = t["expert_bias"].reshape(E, 1)
    for n in ("w1", "w3", "sw1", "sw3"):
        v = t[n]
        a[n] = v.transpose(2, 0, 1).reshape(KD, P, v.shape[0], HID).transpose(1, 0, 2, 3)
    for n in ("w2", "sw2"):
        v = t[n]
        a[n] = v.transpose(2, 0, 1).reshape(KH, P, v.shape[0], D).transpose(1, 0, 2, 3)
    return a


def kernel(**inputs):
    import numpy as _np
    import concourse.bacc as _bacc
    from concourse import mybir as _mybir
    from concourse.bass_utils import run_bass_kernel_spmd as _run

    named = {}
    for k, v in inputs.items():
        if k in ("L0_txt_w0", "L0_txt_w1", "L0_txt_w2"):
            k += "_txt"
        named[k] = v
    arrays = {k: _np.ascontiguousarray(v) for k, v in {**layout(**named), **constants()}.items()}
    nc = _bacc.Bacc("TRN2", target_bir_lowering=False, num_devices=1)
    feed, a = {}, {}
    for name, v in arrays.items():
        feed[f"in_{name}"] = v
        a[name] = nc.dram_tensor(f"in_{name}", v.shape, _mybir.dt.from_np(v.dtype), kind="ExternalInput").ap()
    a["out"] = nc.dram_tensor("out", (TOKENS + SPARE, D), FP32, kind="ExternalOutput").ap()
    embed_scan_moe(nc, a)
    r = _run(nc, [feed], core_ids=[0])
    return r.results[0]["out"][:TOKENS].reshape(B, L, D)
```
